# Optimizing a Trainium2 kernel written in Bass

```python
import numpy as np
import jax
import jax.numpy as jnp

def _softmax(x, axis=-1):
    return jax.nn.softmax(x, axis=axis)

def _gelu(x):
    return jax.nn.gelu(x, approximate=True)

def _silu(x):
    return jax.nn.silu(x)

def _sigmoid(x):
    return jax.nn.sigmoid(x)

def _layernorm(x, axis=-1, eps=1e-05):
    m = jnp.mean(x, axis=axis, keepdims=True)
    v = jnp.var(x, axis=axis, keepdims=True)
    return (x - m) / jnp.sqrt(v + eps)

def _scatter_add(tgt, idx, src, axis=0):
    return tgt.at[idx].add(src)

def _segment_sum(src, seg, n):
    return jax.ops.segment_sum(src, seg, n)
kernel_name = 'mk_perceiver_d2_seqx_r8_0f4fdb'

def setup_inputs(seed: int=0):
    np.random.seed(seed)
    _w = jnp.asarray

    def _rec_inputs():
        import jax
        import jax.numpy as jnp
        _rk = jax.random.key(seed)
        x = -0.0005146 + 1 * jax.random.normal(jax.random.fold_in(_rk, 1), (1, 64, 128), jnp.float32)
        _lenS = 64 - jax.random.randint(jax.random.fold_in(_rk, 7), (1,), 0, max(1, 64 // 4) + 1, jnp.int32)
        _lenS2 = 6272 - jax.random.randint(jax.random.fold_in(_rk, 8), (1,), 0, max(1, 6272 // 4) + 1, jnp.int32)
        _ctx_1024P = jax.random.normal(jax.random.fold_in(_rk, 11), (1, 16, 128), jnp.float32)
        _ctx_1024c = jax.random.dirichlet(jax.random.fold_in(_rk, 511), 0.3 * jnp.ones((16,), jnp.float32), (1, 6272))
        _ctx_1024t = jnp.einsum('bsk,bkd->bsd', _ctx_1024c, _ctx_1024P)
        _ctx_1024t = _ctx_1024t * jax.lax.rsqrt(jnp.mean(jnp.square(_ctx_1024t)) + 1e-12) * 0.953939
        ctx_1024 = -0.000125008 + 0.999885 * (_ctx_1024t + 0.3 * jax.random.normal(jax.random.fold_in(_rk, 611), (1, 6272, 128), jnp.float32))
        _validS = jnp.arange(64)[None, :] < _lenS[:, None]
        _validS2 = jnp.arange(6272)[None, :] < _lenS2[:, None]
        _causal = jnp.tril(jnp.ones((64, 64), dtype=bool))
        mask_Bx1xSxS2_ik1 = jnp.where(jnp.broadcast_to(_validS2[:, None, None, :], (1, 1, 64, 6272)), 1, 0).astype(jnp.int32)
        return (x, ctx_1024, mask_Bx1xSxS2_ik1)
    x, ctx_1024, mask_Bx1xSxS2_ik1 = _rec_inputs()

    def _L0_xattn_setup():
        import jax, jax.numpy as jnp
        import numpy as np
        DIM = 128
        NUM_HEADS = 16
        HEAD_DIM = DIM // NUM_HEADS
        SCALE = HEAD_DIM ** (-0.5)
        key = jax.random.key(seed)
        k1, k2, k3, k4, k5, k6 = jax.random.split(key, 6)
        B, S, L = (4, 1024, 64)
        x = jax.random.normal(k1, (B, S, DIM), dtype=jnp.float32)
        latents = jax.random.normal(k2, (B, L, DIM), dtype=jnp.float32)
        w_q = jax.random.normal(k3, (DIM, DIM), dtype=jnp.float32) * DIM ** (-0.5)
        w_kv = jax.random.normal(k4, (2 * DIM, DIM), dtype=jnp.float32) * DIM ** (-0.5)
        w_out = jax.random.normal(k5, (DIM, DIM), dtype=jnp.float32) * DIM ** (-0.5)
        b_out = jax.random.normal(k6, (DIM,), dtype=jnp.float32) * 0.01
        return {'x': x, 'latents': latents, 'w_q': w_q, 'w_kv': w_kv, 'w_out': w_out, 'b_out': b_out}
    _L0_xattn_all = _L0_xattn_setup()
    _L0_xattn_in = {k: v for k, v in _L0_xattn_all.items() if k in ('w_q', 'w_kv', 'w_out', 'b_out')}
    del _L0_xattn_all

    def _L0_attn_setup():
        import jax, jax.numpy as jnp
        import numpy as np
        B, S, D, H = (2, 256, 128, 16)
        HD = D // H

        def _rope_cos_sin(seq_len, head_dim, base=10000.0):
            i = jnp.arange(head_dim // 2, dtype=jnp.float32)
            theta = base ** (-2.0 * i / head_dim)
            m = jnp.arange(seq_len, dtype=jnp.float32)
            ang = jnp.outer(m, theta)
            return (jnp.cos(ang), jnp.sin(ang))

        def _apply_rope(x, cos, sin):
            xr = x[..., 0::2]
            xi = x[..., 1::2]
            c = cos[None, :, None, :]
            s = sin[None, :, None, :]
            out_r = xr * c - xi * s
            out_i = xr * s + xi * c
            return jnp.stack([out_r, out_i], axis=-1).reshape(x.shape)
        key = jax.random.key(seed)
        ks = jax.random.split(key, 7)
        sc = 1.0 / np.sqrt(D)
        return {'x': jax.random.normal(ks[0], (B, S, D), dtype=jnp.float32), 'wq_w': jax.random.normal(ks[1], (D, D), dtype=jnp.float32) * sc, 'wq_b': jax.random.normal(ks[2], (D,), dtype=jnp.float32) * 0.01, 'wk_w': jax.random.normal(ks[3], (D, D), dtype=jnp.float32) * sc, 'wk_b': jax.random.normal(ks[4], (D,), dtype=jnp.float32) * 0.01, 'wv_w': jax.random.normal(ks[5], (D, D), dtype=jnp.float32) * sc, 'wv_b': jax.random.normal(ks[6], (D,), dtype=jnp.float32) * 0.01}
    _L0_attn_all = _L0_attn_setup()
    _L0_attn_in = {k: v for k, v in _L0_attn_all.items() if k in ('wq_w', 'wq_b', 'wk_w', 'wk_b', 'wv_w', 'wv_b')}
    del _L0_attn_all

    def _L0_ffn_setup():
        import jax, jax.numpy as jnp
        import numpy as np
        B, S, D, H, E = (4, 256, 128, 512, 8)
        key = jax.random.key(seed)
        ks = jax.random.split(key, 8)
        s_d = 1.0 / np.sqrt(D)
        s_h = 1.0 / np.sqrt(H)
        return {'x': jax.random.normal(ks[0], (B, S, D), dtype=jnp.float32), 'gate_w': jax.random.uniform(ks[1], (E, D), jnp.float32, -s_d, s_d), 'gate_b': jax.random.uniform(ks[2], (E,), jnp.float32, -s_d, s_d), 'w1': jax.random.uniform(ks[3], (E, H, D), jnp.float32, -s_d, s_d), 'b1': jax.random.uniform(ks[4], (E, H), jnp.float32, -s_d, s_d), 'w2': jax.random.uniform(ks[5], (E, D, H), jnp.float32, -s_h, s_h), 'b2': jax.random.uniform(ks[6], (E, D), jnp.float32, -s_h, s_h)}
    _L0_ffn_all = _L0_ffn_setup()
    _L0_ffn_in = {k: v for k, v in _L0_ffn_all.items() if k in ('gate_w', 'gate_b', 'w1', 'b1', 'w2', 'b2')}
    del _L0_ffn_all

    def _L1_xattn_setup():
        import jax, jax.numpy as jnp
        import numpy as np
        D_MODEL = 128
        N_HEAD = 16
        B, S = (4, 256)

        def _split_heads(x):
            b, l, d = x.shape
            return x.reshape(b, l, N_HEAD, d // N_HEAD).transpose(0, 2, 1, 3)
        key = jax.random.key(seed)
        ks = jax.random.split(key, 13)
        s = 1.0 / np.sqrt(D_MODEL)
        inp = {'query': jax.random.normal(ks[0], (B, S, D_MODEL), jnp.float32), 'key_': jax.random.normal(ks[1], (B, S, D_MODEL), jnp.float32), 'value': jax.random.normal(ks[2], (B, S, D_MODEL), jnp.float32), 'mask': jax.random.randint(ks[3], (B, 1, S, S), 0, 2, jnp.int32), 'Wq': jax.random.normal(ks[4], (D_MODEL, D_MODEL), jnp.float32) * s, 'bq': jax.random.normal(ks[5], (D_MODEL,), jnp.float32) * 0.02, 'Wk': jax.random.normal(ks[6], (D_MODEL, D_MODEL), jnp.float32) * s, 'bk': jax.random.normal(ks[7], (D_MODEL,), jnp.float32) * 0.02, 'Wv': jax.random.normal(ks[8], (D_MODEL, D_MODEL), jnp.float32) * s, 'bv': jax.random.normal(ks[9], (D_MODEL,), jnp.float32) * 0.02, 'Wo': jax.random.normal(ks[10], (D_MODEL, D_MODEL), jnp.float32) * s, 'bo': jax.random.normal(ks[11], (D_MODEL,), jnp.float32) * 0.02}
        return inp
    _L1_xattn_all = _L1_xattn_setup()
    _L1_xattn_in = {k: v for k, v in _L1_xattn_all.items() if k in ('Wq', 'bq', 'Wk', 'bk', 'Wv', 'bv', 'Wo', 'bo')}
    del _L1_xattn_all

    def _L1_attn_setup():
        import jax, jax.numpy as jnp
        import numpy as np
        EMBED_DIM = 128
        NUM_HEADS = 16
        HEAD_DIM = EMBED_DIM // NUM_HEADS
        SCALE = 1.0 / np.sqrt(HEAD_DIM)
        key = jax.random.key(seed)
        ks = jax.random.split(key, 5)
        B, S, D = (2, 256, EMBED_DIM)
        s = 0.02
        return {'x': jax.random.normal(ks[0], (B, S, D), jnp.float32), 'Wqkv': jax.random.normal(ks[1], (D, 3 * D), jnp.float32) * s, 'bqkv': jax.random.normal(ks[2], (3 * D,), jnp.float32) * s, 'Wout': jax.random.normal(ks[3], (D, D), jnp.float32) * s, 'bout': jax.random.normal(ks[4], (D,), jnp.float32) * s}
    _L1_attn_all = _L1_attn_setup()
    _L1_attn_in = {k: v for k, v in _L1_attn_all.items() if k in ('Wqkv', 'bqkv', 'Wout', 'bout')}
    del _L1_attn_all

    def _L1_ffn_setup():
        import math
        import jax, jax.numpy as jnp
        import numpy as np
        B, T, D, H, E, K, S = (4, 512, 128, 256, 16, 2, 2)
        ROUTE_SCALE = 1.0

        def _swiglu(x, w1, w3, w2):
            return jax.nn.silu(x @ w1) * (x @ w3) @ w2
        key = jax.random.key(seed)
        ks = jax.random.split(key, 9)
        s = 0.02
        return {'x': jax.random.normal(ks[0], (B, T, D), jnp.float32), 'gate_w': jax.random.normal(ks[1], (D, E), jnp.float32) * s, 'gate_b': jnp.zeros((E,), jnp.float32), 'ew1': jax.random.normal(ks[2], (E, D, H), jnp.float32) * s, 'ew3': jax.random.normal(ks[3], (E, D, H), jnp.float32) * s, 'ew2': jax.random.normal(ks[4], (E, H, D), jnp.float32) * s, 'sw1': jax.random.normal(ks[5], (S, D, H), jnp.float32) * s, 'sw3': jax.random.normal(ks[6], (S, D, H), jnp.float32) * s, 'sw2': jax.random.normal(ks[7], (S, H, D), jnp.float32) * s}
    _L1_ffn_all = _L1_ffn_setup()
    _L1_ffn_in = {k: v for k, v in _L1_ffn_all.items() if k in ('gate_w', 'gate_b', 'ew1', 'ew3', 'ew2', 'sw1', 'sw3', 'sw2')}
    del _L1_ffn_all
    return {'x': x, 'ctx_1024': ctx_1024, 'mask_Bx1xSxS2_ik1': mask_Bx1xSxS2_ik1, 'L0_xattn_w_q': _L0_xattn_in['w_q'], 'L0_xattn_w_kv': _L0_xattn_in['w_kv'], 'L0_xattn_w_out': _L0_xattn_in['w_out'], 'L0_xattn_b_out': _L0_xattn_in['b_out'], 'L0_attn_wq_w': _L0_attn_in['wq_w'], 'L0_attn_wq_b': _L0_attn_in['wq_b'], 'L0_attn_wk_w': _L0_attn_in['wk_w'], 'L0_attn_wk_b': _L0_attn_in['wk_b'], 'L0_attn_wv_w': _L0_attn_in['wv_w'], 'L0_attn_wv_b': _L0_attn_in['wv_b'], 'L0_ffn_gate_w': _L0_ffn_in['gate_w'], 'L0_ffn_gate_b': _L0_ffn_in['gate_b'], 'L0_ffn_w1': _L0_ffn_in['w1'], 'L0_ffn_b1': _L0_ffn_in['b1'], 'L0_ffn_w2': _L0_ffn_in['w2'], 'L0_ffn_b2': _L0_ffn_in['b2'], 'L1_xattn_Wq': _L1_xattn_in['Wq'], 'L1_xattn_bq': _L1_xattn_in['bq'], 'L1_xattn_Wk': _L1_xattn_in['Wk'], 'L1_xattn_bk': _L1_xattn_in['bk'], 'L1_xattn_Wv': _L1_xattn_in['Wv'], 'L1_xattn_bv': _L1_xattn_in['bv'], 'L1_xattn_Wo': _L1_xattn_in['Wo'], 'L1_xattn_bo': _L1_xattn_in['bo'], 'L1_attn_Wqkv': _L1_attn_in['Wqkv'], 'L1_attn_bqkv': _L1_attn_in['bqkv'], 'L1_attn_Wout': _L1_attn_in['Wout'], 'L1_attn_bout': _L1_attn_in['bout'], 'L1_ffn_gate_w': _L1_ffn_in['gate_w'], 'L1_ffn_gate_b': _L1_ffn_in['gate_b'], 'L1_ffn_ew1': _L1_ffn_in['ew1'], 'L1_ffn_ew3': _L1_ffn_in['ew3'], 'L1_ffn_ew2': _L1_ffn_in['ew2'], 'L1_ffn_sw1': _L1_ffn_in['sw1'], 'L1_ffn_sw3': _L1_ffn_in['sw3'], 'L1_ffn_sw2': _L1_ffn_in['sw2']}

def reference(x, ctx_1024, mask_Bx1xSxS2_ik1, L0_xattn_w_q, L0_xattn_w_kv, L0_xattn_w_out, L0_xattn_b_out, L0_attn_wq_w, L0_attn_wq_b, L0_attn_wk_w, L0_attn_wk_b, L0_attn_wv_w, L0_attn_wv_b, L0_ffn_gate_w, L0_ffn_gate_b, L0_ffn_w1, L0_ffn_b1, L0_ffn_w2, L0_ffn_b2, L1_xattn_Wq, L1_xattn_bq, L1_xattn_Wk, L1_xattn_bk, L1_xattn_Wv, L1_xattn_bv, L1_xattn_Wo, L1_xattn_bo, L1_attn_Wqkv, L1_attn_bqkv, L1_attn_Wout, L1_attn_bout, L1_ffn_gate_w, L1_ffn_gate_b, L1_ffn_ew1, L1_ffn_ew3, L1_ffn_ew2, L1_ffn_sw1, L1_ffn_sw3, L1_ffn_sw2):
    import jax
    import jax.numpy as jnp

    def _L0_xattn_ref(x, latents, w_q, w_kv, w_out, b_out):
        import jax, jax.numpy as jnp
        import numpy as np
        DIM = 128
        NUM_HEADS = 16
        HEAD_DIM = DIM // NUM_HEADS
        SCALE = HEAD_DIM ** (-0.5)
        B, L, _ = latents.shape
        S = x.shape[1]
        q = latents @ w_q.T
        kv = x @ w_kv.T
        k, v = jnp.split(kv, 2, axis=-1)
        q = q.reshape(B, L, NUM_HEADS, HEAD_DIM)
        k = k.reshape(B, S, NUM_HEADS, HEAD_DIM)
        v = v.reshape(B, S, NUM_HEADS, HEAD_DIM)
        attn = jnp.einsum('blhd,bshd->bhls', q, k) * SCALE
        attn = jax.nn.softmax(attn, axis=-1)
        out = jnp.einsum('bhls,bshd->blhd', attn, v)
        out = out.reshape(B, L, DIM)
        return out @ w_out.T + b_out

    def _L0_attn_ref(x, wq_w, wq_b, wk_w, wk_b, wv_w, wv_b):
        import jax, jax.numpy as jnp
        import numpy as np
        B, S, D, H = (2, 256, 128, 16)
        HD = D // H

        def _rope_cos_sin(seq_len, head_dim, base=10000.0):
            i = jnp.arange(head_dim // 2, dtype=jnp.float32)
            theta = base ** (-2.0 * i / head_dim)
            m = jnp.arange(seq_len, dtype=jnp.float32)
            ang = jnp.outer(m, theta)
            return (jnp.cos(ang), jnp.sin(ang))

        def _apply_rope(x, cos, sin):
            xr = x[..., 0::2]
            xi = x[..., 1::2]
            c = cos[None, :, None, :]
            s = sin[None, :, None, :]
            out_r = xr * c - xi * s
            out_i = xr * s + xi * c
            return jnp.stack([out_r, out_i], axis=-1).reshape(x.shape)
        bs, seq_len, dim = x.shape
        xq = (x @ wq_w.T + wq_b).reshape(bs, seq_len, H, HD)
        xk = (x @ wk_w.T + wk_b).reshape(bs, seq_len, H, HD)
        xv = (x @ wv_w.T + wv_b).reshape(bs, seq_len, H, HD)
        cos, sin = _rope_cos_sin(seq_len, HD)
        xq = _apply_rope(xq, cos, sin)
        xk = _apply_rope(xk, cos, sin)
        q = xq.transpose(0, 2, 1, 3)
        k = xk.transpose(0, 2, 1, 3)
        v = xv.transpose(0, 2, 1, 3)
        scores = jnp.einsum('bhqd,bhkd->bhqk', q, k) / np.sqrt(HD)
        attn = jax.nn.softmax(scores.astype(jnp.float32), axis=-1)
        out = jnp.einsum('bhqk,bhkd->bhqd', attn, v)
        return out.transpose(0, 2, 1, 3).reshape(bs, seq_len, dim)

    def _L0_ffn_ref(x, gate_w, gate_b, w1, b1, w2, b2):
        import jax, jax.numpy as jnp
        import numpy as np
        B, S, D, H, E = (4, 256, 128, 512, 8)
        b, s, d = x.shape
        xf = x.reshape(-1, d)
        logits = xf @ gate_w.T + gate_b
        top1 = jnp.argmax(logits, axis=-1)
        out = jnp.zeros_like(xf)
        n_experts = w1.shape[0]
        for e in range(n_experts):
            h = jax.nn.relu(xf @ w1[e].T + b1[e])
            y = h @ w2[e].T + b2[e]
            out = out + jnp.where((top1 == e)[:, None], y, jnp.zeros((), y.dtype))
        return out.reshape(b, s, d)

    def _L1_xattn_ref(query, key_, value, mask, Wq, bq, Wk, bk, Wv, bv, Wo, bo):
        import jax, jax.numpy as jnp
        import numpy as np
        D_MODEL = 128
        N_HEAD = 16
        B, S = (4, 256)

        def _split_heads(x):
            b, l, d = x.shape
            return x.reshape(b, l, N_HEAD, d // N_HEAD).transpose(0, 2, 1, 3)
        q = _split_heads(query @ Wq + bq)
        k = _split_heads(key_ @ Wk + bk)
        v = _split_heads(value @ Wv + bv)
        dh = q.shape[-1]
        score = jnp.einsum('bhqd,bhkd->bhqk', q, k) / jnp.sqrt(jnp.float32(dh))
        score = jnp.where(mask == 0, jnp.float32(-1000000000.0), score)
        attn = jax.nn.softmax(score, axis=-1)
        out = jnp.einsum('bhqk,bhkd->bhqd', attn, v)
        b, h, l, d = out.shape
        out = out.transpose(0, 2, 1, 3).reshape(b, l, h * d)
        return out @ Wo + bo

    def _L1_attn_ref(x, Wqkv, bqkv, Wout, bout):
        import jax, jax.numpy as jnp
        import numpy as np
        EMBED_DIM = 128
        NUM_HEADS = 16
        HEAD_DIM = EMBED_DIM // NUM_HEADS
        SCALE = 1.0 / np.sqrt(HEAD_DIM)
        B, S, D = x.shape
        qkv = (x @ Wqkv + bqkv).reshape(B, S, 3, NUM_HEADS, HEAD_DIM)
        qkv = jnp.transpose(qkv, (2, 0, 3, 1, 4))
        q, k, v = (qkv[0] * SCALE, qkv[1], qkv[2])
        scores = jnp.einsum('bhqd,bhkd->bhqk', q, k)
        attn = jax.nn.softmax(scores, axis=-1)
        out = jnp.einsum('bhqk,bhkd->bhqd', attn, v)
        out = jnp.transpose(out, (0, 2, 1, 3)).reshape(B, S, D)
        return out @ Wout + bout

    def _L1_ffn_ref(x, gate_w, gate_b, ew1, ew3, ew2, sw1, sw3, sw2):
        import math
        import jax, jax.numpy as jnp
        import numpy as np
        B, T, D, H, E, K, S = (4, 512, 128, 256, 16, 2, 2)
        ROUTE_SCALE = 1.0

        def _swiglu(x, w1, w3, w2):
            return jax.nn.silu(x @ w1) * (x @ w3) @ w2
        Bx, Tx, Dx = x.shape
        flat = x.reshape(-1, Dx)
        N = flat.shape[0]
        n_experts = gate_w.shape[1]
        logits = flat @ gate_w
        scores = jax.nn.softmax(logits.astype(jnp.float32), -1) + gate_b
        _, topi = jax.lax.top_k(scores, K)
        weights = jnp.take_along_axis(logits, topi, axis=-1) * ROUTE_SCALE
        weights = weights.astype(flat.dtype)
        capacity = math.ceil(N * K / n_experts * 1.25)

        def per_expert(gid, w1, w3, w2):
            match = topi == gid
            assigned = match.any(-1)
            w_tok = jnp.sum(jnp.where(match, weights, 0.0), -1)
            wm = jnp.where(assigned, w_tok, -jnp.inf)
            vals, idx = jax.lax.top_k(wm, capacity)
            valid = assigned[idx]
            xs = flat[idx]
            y = _swiglu(xs, w1, w3, w2) * jnp.where(valid, vals, 0.0)[:, None]
            return (idx, y)
        idxs, ys = jax.vmap(per_expert)(jnp.arange(n_experts), ew1, ew3, ew2)
        out = jnp.zeros_like(flat).at[idxs.reshape(-1)].add(ys.reshape(-1, Dx))
        shared = jax.vmap(lambda w1, w3, w2: _swiglu(flat, w1, w3, w2))(sw1, sw3, sw2)
        out = out + shared.mean(0)
        return out.reshape(Bx, Tx, Dx)
    x = x + _L0_xattn_ref(ctx_1024, _layernorm(x, axis=-1), L0_xattn_w_q, L0_xattn_w_kv, L0_xattn_w_out, L0_xattn_b_out)
    x = x + _L0_attn_ref(_layernorm(x, axis=-1), L0_attn_wq_w, L0_attn_wq_b, L0_attn_wk_w, L0_attn_wk_b, L0_attn_wv_w, L0_attn_wv_b)
    x = x + _L0_ffn_ref(_layernorm(x, axis=-1), L0_ffn_gate_w, L0_ffn_gate_b, L0_ffn_w1, L0_ffn_b1, L0_ffn_w2, L0_ffn_b2)
    x = x + _L1_xattn_ref(_layernorm(x, axis=-1), ctx_1024, ctx_1024, mask_Bx1xSxS2_ik1, L1_xattn_Wq, L1_xattn_bq, L1_xattn_Wk, L1_xattn_bk, L1_xattn_Wv, L1_xattn_bv, L1_xattn_Wo, L1_xattn_bo)
    x = x + _L1_attn_ref(_layernorm(x, axis=-1), L1_attn_Wqkv, L1_attn_bqkv, L1_attn_Wout, L1_attn_bout)
    x = x + _L1_ffn_ref(_layernorm(x, axis=-1), L1_ffn_gate_w, L1_ffn_gate_b, L1_ffn_ew1, L1_ffn_ew3, L1_ffn_ew2, L1_ffn_sw1, L1_ffn_sw3, L1_ffn_sw2)
    return x

_drawn_inputs = setup_inputs


def setup_inputs(seed=0):
    import zlib

    import numpy as np

    out = dict(_drawn_inputs(seed))
    spreads = {'L1_ffn_gate_b': (0.0, 0.8)}
    factors = {'L0_xattn_b_out': 4.409,
     'L0_attn_wq_b': 30.137,
     'L0_attn_wk_b': 8.0,
     'L0_attn_wv_b': 7.399,
     'L0_ffn_b1': 3.769,
     'L0_ffn_b2': 3.006,
     'L1_xattn_bq': 8.0,
     'L1_xattn_bk': 64.0,
     'L1_xattn_bv': 3.279,
     'L1_xattn_bo': 3.661,
     'L1_attn_bqkv': 8.0,
     'L1_attn_Wout': 2.889,
     'L1_attn_bout': 3.871,
     'L1_ffn_gate_w': 8.0,
     'L1_ffn_ew1': 8.0,
     'L1_ffn_ew3': 8.0,
     'L1_ffn_ew2': 8.0,
     'L1_ffn_sw1': 8.0,
     'L1_ffn_sw3': 8.0,
     'L1_ffn_sw2': 8.0}
    for name, (base, spread) in spreads.items():
        noise = np.random.default_rng([zlib.crc32(name.encode()), seed]).standard_normal(out[name].shape)
        drawn = base * np.exp(spread * noise) if base else spread * noise
        out[name] = jnp.asarray(drawn.astype(out[name].dtype))
    for name, factor in factors.items():
        out[name] = (out[name] * factor).astype(out[name].dtype)
    return out
```

```python
from contextlib import ExitStack

import numpy as np

import concourse.bass as bass
from concourse import mybir

F32 = mybir.dt.float32
BF16 = mybir.dt.bfloat16
I32 = mybir.dt.int32
U32 = mybir.dt.uint32
ALU = mybir.AluOpType
ACT = mybir.ActivationFunctionType
AX = mybir.AxisListType

D = 128
L = 64
NH = 16
HD = D // NH
NP = NH // 2
S = 6272
T = 128
CT = 7
C = CT * T
NC = S // C
NT = S // T
HC = C // 2
SCALE = HD ** -0.5
EPS = 1e-5
TERMS = [(0, 0), (1, 0), (0, 1), (1, 1), (0, 2), (2, 0)]
NR = len(TERMS) * 2 * HD
NS = NR + 3
MASKED = -float(2 ** 30)
E0, H0 = 8, 512
K0 = H0 // 128
E1, H1 = 16, 256
K1 = H1 // 128
NSH = 2
NE1 = E1 + NSH
CAP = 10
NOT_ASSIGNED = -1e30

MATS = {}
_at = 0
for _n, _w in (("wq0", D), ("wk0", D), ("wv0", D), ("wo0", D), ("wqkv0", 3 * D), ("wq1", D), ("wk1", D), ("wv1", D),
               ("wo1", D), ("wqkv1", 3 * D), ("wout1", D), ("gate0", E0), ("gate1", E1)):
    MATS[_n] = (_at, _at + _w)
    _at += _w
NMAT = _at
ROWS = {}
_at = 0
for _n, _w in (("bo0", D), ("bqkv0", 3 * D), ("bq1", D), ("bv1", D), ("bo1", D), ("bqkv1", 3 * D), ("bout1", D),
               ("gb0", E0), ("gb1", E1), ("b2", E0 * D)):
    ROWS[_n] = (_at, _at + _w)
    _at += _w
NROW = _at
CONS = {}
_at = 0
for _n, _w in (("ident", D), ("head", NH), ("qsel", 6), ("cos2", HD), ("nsin", HD // 2), ("sin", HD // 2), ("iota", E1),
               ("bk1", 1), ("b1", E0 * K0)):
    CONS[_n] = (_at, _at + _w)
    _at += _w
NCON = _at
PV = [(j, slice(27 * j, 27 * j + 27), slice(3 * L * j, 3 * L * (j + 1)), slice(0, 3 * L)) for j in range(4)]
PV += [(j, slice(108 + 9 * j, 117 + 9 * j), slice((12 + j) * L, (13 + j) * L), slice(3 * L, 4 * L)) for j in range(4)]


def perceiver(nc, x_in, ctx_t, mask, mats_in, rows_in, cons_in, f0w1, f0w2, f1w13, f1w2, out, last_stage=6):
    ctx = ExitStack()
    with ctx:
        def sb(name, shape, dt=F32):
            return ctx.enter_context(nc.sbuf_tensor(name, shape, dt))

        def sem(name):
            return ctx.enter_context(nc.semaphore(name))

        mats = sb("mats", [128, NMAT])
        rows = sb("rows", [1, NROW])
        cons = sb("cons", [128, NCON])
        mat = {n: mats[:, a:b] for n, (a, b) in MATS.items()}
        row = {n: rows[0:1, a:b] for n, (a, b) in ROWS.items()}
        con = {n: cons[:, a:b] for n, (a, b) in CONS.items()}
        ident = con["ident"]
        identb = sb("identb", [128, D], BF16)
        ident8 = sb("ident8", [L, 8, L], BF16)
        ones = sb("ones", [128, D])
        zeros = sb("zeros", [128, 256])
        neg_half = sb("neg_half", [L, 1])
        shift_pick = sb("shift_pick", [128, 3, NS], BF16)
        w12 = sb("w12", [128, E0 * H0 + E0 * K0 * D])
        w1 = w12[:, 0:E0 * H0].rearrange("p (e h) -> p e h", e=E0)
        w2 = w12[:, E0 * H0:].rearrange("p (e d) -> p e d", d=D)
        w2s = w12[:, 0:NE1 * K1 * D].rearrange("p (e d) -> p e d", d=D)
        x = sb("x", [L, D])
        bn = sb("bn", [L, 6])
        mu_var = sb("mu_var", [L, 2])
        var_eps = sb("var_eps", [L, 1])
        rstd = sb("rstd", [L, 1])
        xn = sb("xn", [L, D])
        xnT = sb("xnT", [D, L])
        ctx_c = sb("ctx_c", [128, 2, C])
        kf = sb("kf", [128, 2, C])
        kr = sb("kr", [128, 2, C])
        kparts = sb("kparts", [128, 3, S], BF16)
        kstack = sb("kstack", [128, 2, NP, C], BF16)
        valid_ident = sb("valid_ident", [L, L])
        qb1 = sb("qb1", [NR, NP * L], BF16)
        qb2 = sb("qb2", [NR, NP * L], BF16)
        qb3 = sb("qb3", [NR, NP * L], BF16)
        scratch = sb("scratch", [128, 3 * NH * L])
        qr1 = scratch[0:NR, 0:NP * L]
        qr2 = scratch[0:NR, NP * L:2 * NP * L]
        q_sb = scratch[0:L, 2 * NP * L:2 * NP * L + NP * NR].rearrange("p (u t r) -> p u t r", u=NP, t=len(TERMS))
        qmix = sb("qmix", [NR, 2, NP * L], BF16)
        qstack = sb("qstack", [128, NP, 2, L], BF16)
        row_max = sb("row_max", [128, NC, NP])
        run_max = sb("run_max", [128, 2, NP])
        negm = sb("negm", [128, NP])
        negm_r1 = sb("negm_r1", [128, NP])
        negm_r2 = sb("negm_r2", [128, NP])
        mpart = sb("mpart", [128, 3, NP], BF16)
        mdiag = scratch[:, 0:3 * NP * 64].bitcast(BF16).rearrange("p (k u m) -> p k u m", k=3, u=NP)
        probs = sb("probs", [128, 2, NH * L])
        vaug = sb("vaug", [128, 2, NH, HD + 1])
        bv_all = sb("bv_all", [128, D])
        mask_raw = kr[:, :, :].bitcast(I32)
        mask_add = sb("mask_add", [128, S], BF16)
        mask_c = sb("mask_c", [128, 2, C], BF16)
        masked_out = sb("masked_out", [128, 2, C], BF16)
        mask_max = sb("mask_max", [128, NC])
        row_open = sb("row_open", [L, 2])
        o_sb = sb("o_sb", [128, 4 * L])
        rec = sb("rec", [L, NH])
        ao = sb("ao", [L, D])
        aoT = sb("aoT", [D, L])
        qk = sb("qk", [L, 2 * D])
        rope_a = sb("rope_a", [L, 2 * D])
        rope_b = sb("rope_b", [L, 2 * D])
        qkT = sb("qkT", [D, 2, L])
        kbd = scratch[:, 0:NH * L].rearrange("p (h l) -> p h l", h=NH)
        qbd = scratch[:, NH * L:2 * NH * L].rearrange("p (h l) -> p h l", h=NH)
        sa_negm = sb("sa_negm", [L, NH])
        sa_diag = scratch[0:L, 2 * NH * L:3 * NH * L].rearrange("p (h l) -> p h l", h=NH)
        lg = sb("lg", [L, E1])
        top8 = sb("top8", [L, 8])
        top_i = sb("top_i", [L, 8], U32)
        top_f = sb("top_f", [L, 8])
        hot = sb("hot", [L, 2, E1])
        h0 = probs[:, :, :].rearrange("p a b -> p (a b)").rearrange("p (b e k l) -> p b e k l", b=4, e=2, k=K0)
        sm = sb("sm", [L, 8])
        sc = sb("sc", [L, E1])
        gb1_all = sb("gb1_all", [L, E1])
        wm = sb("wm", [L, E1])
        wmT = sb("wmT", [E1, L])
        cut1 = sb("cut1", [E1, L])
        cut2 = sb("cut2", [E1, L])
        ranks = sb("ranks", [E1, 2, 8])
        gT = sb("gT", [E1, L])
        gates = sb("gates", [L, E1])
        big = kparts[:, :, :].rearrange("p a b -> p (a b)").bitcast(F32)
        w1s = big[:, 0:NE1 * H1].rearrange("p (e h) -> p e h", e=NE1)
        w3s = big[:, NE1 * H1:2 * NE1 * H1].rearrange("p (e h) -> p e h", e=NE1)
        act1 = sb("act1", [128, 2, 2, K1, L])
        h1 = sb("h1", [128, 2, 2, K1, L])

        PS = ctx.enter_context(nc.psum_tensor("PS", [128, 8, 512], F32))

        x_in_sem = sem("x_loaded")
        cons_in_sem = sem("cons_loaded")
        mats_sem = sem("mats_loaded")
        w0_sem = sem("mlp0_loaded")
        w1_sem = sem("mlp1_loaded")
        ctx_in = [sem("ctx_in_even"), sem("ctx_in_odd")]
        ks_in = [sem("kstack_in_even"), sem("kstack_in_odd")]
        raw_in = [sem("mask_raw_in_even"), sem("mask_raw_in_odd")]
        mc_in = [sem("mask_in_even"), sem("mask_in_odd")]
        out_sem = sem("out_stored")
        const_ready = sem("const_ready")
        dve_step = sem("dve_step")
        var_ready, rstd_ready, xn_ready = sem("var_ready"), sem("rstd_ready"), sem("xn_ready")
        xnT_ps, xnT_ready = sem("xnT_ps"), sem("xnT_ready")
        q_ps, q_ready, qrep_ps, qb1_ready, qstack_ready = (sem(n) for n in
            ("q_ps", "q_ready", "qrep_ps", "qb1_ready", "qstack_ready"))
        k_ps, kf_ready, k1_ready, kr_ready, k2_ready, k3_ready = (sem(n) for n in
            ("k_ps", "kf_ready", "k1_ready", "kr_ready", "k2_ready", "k3_ready"))
        a_ps, a_used = sem("a_ps"), sem("a_used")
        mdiag_ready, shift_ps, shift_ready = sem("mdiag_ready"), sem("shift_ps"), sem("shift_ready")
        v_ps, v_ready, s_ps, p_ready, pv_done = (sem(n) for n in ("v_ps", "v_ready", "s_ps", "p_ready", "pv_done"))
        bv_ps, bv_ready = sem("bv_ps"), sem("bv_ready")
        mask_ready = sem("mask_ready")
        osb_ready, oT_ps, ao_ready, aoT_ps, aoT_ready, proj_ps = (sem(n) for n in
            ("osb_ready", "oT_ps", "ao_ready", "aoT_ps", "aoT_ready", "proj_ps"))
        qkv_ps, qk_ready, qkT_ps, kbd_ready, qbd_ready, srow_ps, diag_ready, st_ps, sp_ready, sa_pv = (sem(n) for n in
            ("qkv_ps", "qk_ready", "qkT_ps", "kbd_ready", "qbd_ready", "srow_ps", "diag_ready", "st_ps", "sp_ready", "sa_pv"))
        g_ps, h_ps, hb_ready, h_ready, y_ps, y_used = (sem(n) for n in
            ("gate_ps", "h_ps", "hb_ready", "h_ready", "y_ps", "y_used"))
        lg_ready, exp_ready, wm_ready, wmT_ps, gT_ready, g1_ps = (sem(n) for n in
            ("lg_ready", "exp_ready", "wm_ready", "wmT_ps", "gT_ready", "gates_ps"))
        m_ps, silu_ready, m_ready, z_ps, z_used = (sem(n) for n in ("m_ps", "silu_ready", "m_ready", "z_ps", "z_used"))
        x_final = sem("x_final")

        def arrived(par, ph, i):
            return ph * (4, 3)[par] + i + 1

        def over_chunks(eng, step):
            step(0, 0)
            step(0, 1)
            with eng.Fori(1, NC // 2) as i:
                step(i, 0)
                step(i, 1)
            step(NC // 2, 0)

        def written_out(step):
            for c in range(NC):
                step(c // 2, c % 2)

        def once(eng, value):
            return value if isinstance(value, int) else eng.snap(value)

        block = ctx.enter_context(nc.Block())

        @block.sync
        def _(sp):
            sp.dma_start(x[:, :], x_in).then_inc(x_in_sem, 16)
            sp.dma_start(cons[:, :], cons_in).then_inc(cons_in_sem, 16)
            sp.dma_start(mats[:, :], mats_in).then_inc(mats_sem, 16)
            sp.dma_start(rows[:, :], rows_in).then_inc(mats_sem, 16)

            def load_ctx(at, par):
                sp.dma_start(ctx_c[:, par, :], ctx_t[:, bass.ds(at, C)]).then_inc(ctx_in[par], 16)

            def restack(at, par):
                for t, (kp, _) in enumerate(TERMS):
                    sp.dma_start(kstack[2 * HD * t:2 * HD * (t + 1), par, :, :],
                                 kparts[:, kp, bass.ds(at, C)]).then_inc(ks_in[par], 16)

            def load_mask(at, par):
                sp.dma_start(mask_c[:, par, :], mask_add[:, bass.ds(at, C)]).then_inc(mc_in[par], 16)

            for l in range(2):
                def chunk_a(i, par):
                    c = 2 * i + par
                    second = not isinstance(i, int) or i > 0
                    at = once(sp, c * C)
                    split = once(sp, c + (NC * l + 1))
                    if second:
                        projected = once(sp, c + (NC * l - 1))
                        scored = once(sp, NP * c + (NC * NP * l - NP))
                        sp.wait_ge(k_ps, projected)
                    elif l:
                        sp.wait_ge(v_ps, NT)
                    load_ctx(at, par)
                    sp.wait_ge(k3_ready, split)
                    if second:
                        sp.wait_ge(a_ps, scored)
                    elif l:
                        sp.wait_ge(s_ps, NT)
                    if l:
                        if second:
                            sp.wait_ge(a_used, scored)
                        sp.wait_ge(mask_ready, NC)
                        load_mask(at, par)
                    restack(at, par)
                over_chunks(sp, chunk_a)
                if l == 0:
                    sp.dma_start(w1, f0w1).then_inc(w0_sem, 16)
                    sp.dma_start(w2, f0w2).then_inc(w0_sem, 16)

                def chunk_b(i, par):
                    c = 2 * i + par
                    second = not isinstance(i, int) or i > 0
                    at = once(sp, c * C)
                    if second:
                        tiles = once(sp, CT * c + (NT * l - CT))
                        converted = once(sp, c - 1)
                        sp.wait_ge(v_ps, tiles)
                        sp.wait_ge(s_ps, tiles)
                    else:
                        sp.wait_ge(k_ps, NC * (l + 1))
                        sp.wait_ge(a_ps, NC * NP * (l + 1))
                    load_ctx(at, par)
                    restack(at, par)
                    if l:
                        if not second:
                            sp.wait_ge(a_used, NC * NP * 2)
                        load_mask(at, par)
                    else:
                        if second:
                            sp.wait_ge(mask_ready, converted)
                        for half in range(2):
                            sp.dma_start(mask_raw[L * half:L * (half + 1), par, :],
                                         mask[:, bass.ds(at, C)]).then_inc(raw_in[par], 16)
                over_chunks(sp, chunk_b)
            sp.wait_ge(s_ps, 2 * NT)
            sp.dma_start(w1s, f1w13[:, 0]).then_inc(w1_sem, 16)
            sp.dma_start(w3s, f1w13[:, 1]).then_inc(w1_sem, 16)
            sp.dma_start(w2s, f1w2).then_inc(w1_sem, 16)
            sp.wait_ge(x_final, 1)
            sp.dma_start(out, x[:, :]).then_inc(out_sem, 16)
            sp.wait_ge(out_sem, 16)

        @block.gpsimd
        def _(pool):
            def power(n):
                pool.wait_ge(var_ready, n + 1)
                nc.gpsimd.tensor_tensor(out=rstd[:, :], in0=var_eps[:, :], in1=neg_half[:, :],
                                        op=ALU.pow).then_inc(rstd_ready, 1)

            def split_k(l):
                def first_residue(i, par):
                    pool.wait_ge(k1_ready, NC * l + 2 * i + par + 1)
                    nc.gpsimd.tensor_tensor(out=kr[:, par, :], in0=kf[:, par, :],
                                            in1=kparts[:, 0, bass.ds((2 * i + par) * C, C)],
                                            op=ALU.subtract).then_inc(kr_ready, 1)

                def third_part(i, par):
                    pool.wait_ge(k2_ready, NC * l + 2 * i + par + 1)
                    nc.gpsimd.tensor_tensor(out=kparts[:, 2, bass.ds((2 * i + par) * C, C)], in0=kr[:, par, :],
                                            in1=kparts[:, 1, bass.ds((2 * i + par) * C, C)],
                                            op=ALU.subtract).then_inc(k3_ready, 1)

                def step(i, par):
                    first_residue(i, par)
                    third_part(i, par)
                over_chunks(pool, step)

            power(0)
            split_k(0)
            for n in (1, 2, 3):
                power(n)
            split_k(1)
            for n in (4, 5):
                power(n)

        @block.scalar
        def _(act):
            def qb1_copy(l):
                act.wait_ge(qrep_ps, l + 1)
                nc.scalar.activation(qb1[:, :], PS[0:NR, 6, :], ACT.Copy).then_inc(qb1_ready, 1)

            def split_k(l):
                def step(i, par):
                    c = 2 * i + par
                    act.wait_ge(k_ps, NC * l + c + 1)
                    src = PS[:, 0:2, 0:HC]
                    dst = kf[:, par, :].rearrange("p (h c) -> p h c", h=2)
                    if l:
                        nc.scalar.activation(dst, src, ACT.Identity, bias=con["bk1"]).then_inc(kf_ready, 1)
                    else:
                        nc.scalar.activation(dst, src, ACT.Copy).then_inc(kf_ready, 1)
                    act.wait_ge(kf_ready, NC * l + c + 1)
                    nc.scalar.activation(kparts[:, 0, bass.ds(c * C, C)], kf[:, par, :], ACT.Copy).then_inc(k1_ready, 1)
                    act.wait_ge(kr_ready, NC * l + c + 1)
                    nc.scalar.activation(kparts[:, 1, bass.ds(c * C, C)], kr[:, par, :], ACT.Copy).then_inc(k2_ready, 1)
                over_chunks(act, step)

            def shift(l):
                act.wait_ge(shift_ps, l + 1)
                nc.scalar.activation(qstack[NR:NS, :, :, :].rearrange("p a b c -> p (a b c)"),
                                     PS[NR:NS, 0:2, :].rearrange("p a b -> p (a b)"),
                                     ACT.Copy).then_inc(shift_ready, 1)

            def exps(l):
                def step(i, par):
                    for k in range(CT):
                        t = (2 * i + par) * CT + k
                        b = (par + k) % 2
                        act.wait_ge(s_ps, NT * l + t + 1)
                        if not isinstance(i, int) or t >= 2:
                            act.wait_ge(pv_done, NT * l + t - 1)
                        nc.scalar.activation(probs[:, b, :], PS[:, 2 * b:2 * b + 2, :].rearrange("p a b -> p (a b)"),
                                             ACT.Exp, scale=SCALE).then_inc(p_ready, 1)
                over_chunks(act, step)

            def sa_exp(s):
                act.wait_ge(st_ps, s + 1)
                nc.scalar.activation(probs[0:L, 0, :], PS[0:L, 0:2, :].rearrange("p a b -> p (a b)"),
                                     ACT.Exp, scale=SCALE).then_inc(sp_ready, 1)

            qb1_copy(0)
            split_k(0)
            shift(0)
            exps(0)
            sa_exp(0)
            for e in range(E0):
                act.wait_ge(hb_ready, e + 1)
                nc.scalar.activation(h0[:, e // 2, e % 2, :, :], h0[:, e // 2, e % 2, :, :],
                                     ACT.Relu).then_inc(h_ready, 1)
            qb1_copy(1)
            act.wait_ge(ks_in[0], 16 * len(TERMS) * 8)
            act.wait_ge(ks_in[1], 16 * len(TERMS) * 6)
            split_k(1)
            shift(1)
            exps(1)
            sa_exp(1)
            act.wait_ge(lg_ready, 1)
            nc.scalar.activation(sc[:, :], lg[:, :], ACT.Exp, bias=sm[:, 0:1], accum_out=sm[:, 1:2]).then_inc(exp_ready, 1)
            for b in range(NE1 // 2):
                act.wait_ge(m_ps, b + 1)
                if b >= 2:
                    act.wait_ge(m_ready, b - 1)
                nc.scalar.activation(act1[:, b % 2], PS[:, b % 4, :].rearrange("p (e w k l) -> p e w k l", e=2, w=2, k=K1)[:, :, 0],
                                     ACT.Silu).then_inc(silu_ready, 1)

        @block.vector
        def _(dve):
            count = [0]

            def link(ins):
                count[0] += 1
                ins.then_inc(dve_step, 1)
                dve.wait_ge(dve_step, count[0])

            def layernorm(n):
                link(nc.vector.bn_stats(out=bn[:, :], in_=x[:, :]))
                link(nc.vector.bn_aggr(out=mu_var[:, :], in_=bn[:, :]))
                nc.vector.tensor_scalar_add(var_eps[:, :], mu_var[:, 1:2], EPS).then_inc(var_ready, 1)
                dve.wait_ge(rstd_ready, n + 1)
                nc.vector.tensor_scalar(xn[:, :], x[:, :], mu_var[:, 0:1], rstd[:, 0:1], ALU.subtract,
                                        ALU.mult).then_inc(xn_ready, 1)
                dve.wait_ge(xnT_ps, n + 1)
                nc.vector.tensor_copy(xnT[:, :], PS[:, 7, 0:L]).then_inc(xnT_ready, 1)

            def queries(l):
                dve.wait_ge(q_ps, l + 1)
                src = PS[0:L, 7, 0:D].rearrange("p (u r) -> p u r", u=NP)
                nc.vector.tensor_copy(q_sb, src[:, :, None, :].to_broadcast([L, NP, len(TERMS), 2 * HD])).then_inc(q_ready, 1)
                dve.wait_ge(qb1_ready, l + 1)
                link(nc.vector.tensor_tensor(out=qr1[:, :], in0=PS[0:NR, 6, :], in1=qb1[:, :], op=ALU.subtract))
                link(nc.vector.tensor_copy(qb2[:, :], qr1[:, :]))
                link(nc.vector.tensor_tensor(out=qr2[:, :], in0=qr1[:, :], in1=qb2[:, :], op=ALU.subtract))
                link(nc.vector.tensor_copy(qb3[:, :], qr2[:, :]))
                qsel = con["qsel"]
                nc.vector.tensor_scalar(qmix[:, 0, :], qb1[:, :], qsel[0:NR, 0:1], None, ALU.mult)
                link(nc.vector.tensor_scalar(qmix[:, 1, :], qb1[:, :], qsel[0:NR, 1:2], None, ALU.mult))
                for part, src in ((1, qb2), (2, qb3)):
                    for hh in range(2):
                        if part == 1:
                            o = qmix[:, hh, :]
                            a, b = src[:, :], qmix[:, hh, :]
                        else:
                            o = qstack[0:NR, :, hh, :]
                            a = src[:, :].rearrange("p (a l) -> p a l", a=NP)
                            b = qmix[:, hh, :].rearrange("p (a l) -> p a l", a=NP)
                        ins = nc.vector.scalar_tensor_tensor(out=o, in0=a, scalar=qsel[0:NR, 2 * part + hh:2 * part + hh + 1],
                                                             in1=b, op0=ALU.mult, op1=ALU.add)
                    if part == 1:
                        link(ins)
                    else:
                        ins.then_inc(qstack_ready, 1)

            def maxima(l):
                def step(i, par):
                    c = 2 * i + par
                    if l:
                        dve.wait_ge(mc_in[par], 16 * (i + 1))
                    for u in range(NP):
                        n = NC * NP * l + NP * c + u
                        dve.wait_ge(a_ps, n + 1)
                        scores = PS[:, 2 + 2 * (u % 2):4 + 2 * (u % 2), 0:HC]
                        if l:
                            dve.wait_ge(a_used, n - 1)
                            nc.vector.tensor_tensor_reduce(
                                out=masked_out[:, u % 2, :].rearrange("p (h c) -> p h c", h=2), in0=scores,
                                in1=mask_c[:, par, :].rearrange("p (h c) -> p h c", h=2), scale=1.0,
                                scalar=run_max[:, 1 - par, u:u + 1], op0=ALU.add, op1=ALU.max,
                                accum_out=run_max[:, par, u:u + 1]).then_inc(a_used, 1)
                        else:
                            nc.vector.tensor_reduce(out=row_max[:, bass.ds(c, 1), u:u + 1].rearrange("p a b -> p (a b)"), in_=scores, axis=AX.XY,
                                                    op=ALU.max).then_inc(a_used, 1)
                if l:
                    written_out(step)
                else:
                    over_chunks(dve, step)

            def shift_parts(l):
                dve.wait_ge(a_used, NC * NP * (l + 1))
                if l:
                    link(nc.vector.tensor_scalar(negm[:, :], run_max[:, 0, :], -1.0, None, ALU.mult))
                else:
                    link(nc.vector.tensor_reduce(out=negm[:, :], in_=row_max[:, :, :].rearrange("p c u -> p u c"),
                                                 axis=AX.X, op=ALU.max, negate=True))
                link(nc.vector.tensor_copy(mpart[:, 0, :], negm[:, :]))
                link(nc.vector.tensor_tensor(out=negm_r1[:, :], in0=negm[:, :], in1=mpart[:, 0, :], op=ALU.subtract))
                link(nc.vector.tensor_copy(mpart[:, 1, :], negm_r1[:, :]))
                link(nc.vector.tensor_tensor(out=mpart[:, 2, :], in0=negm_r1[:, :], in1=mpart[:, 1, :], op=ALU.subtract))
                for part in range(3):
                    nc.vector.tensor_tensor(out=mdiag[:, part], in0=mpart[:, part, :, None].to_broadcast([128, NP, 128]),
                                            in1=identb[:, None, :].to_broadcast([128, NP, 128]),
                                            op=ALU.mult).then_inc(mdiag_ready, 1)

            def values(l):
                def step(i, par):
                    if l == 0:
                        c = 2 * i + par
                        dve.wait_ge(raw_in[par], 32 * (i + 1))
                        nc.vector.tensor_scalar(mask_add[:, bass.ds(c * C, C)], mask_raw[:, par, :], 0.0, MASKED,
                                                ALU.is_equal, ALU.mult).then_inc(mask_ready, 1)
                        dve.wait_ge(mask_ready, c + 1)
                        nc.vector.tensor_reduce(out=mask_max[:, bass.ds(c, 1)], in_=mask_add[:, bass.ds(c * C, C)],
                                                axis=AX.X, op=ALU.max)
                    for k in range(CT):
                        t = (2 * i + par) * CT + k
                        b = (par + k) % 2
                        dve.wait_ge(v_ps, NT * l + t + 1)
                        if not isinstance(i, int) or t >= 2:
                            dve.wait_ge(pv_done, NT * l + t - 1)
                        src = PS[:, 5 + b, 0:D].rearrange("p (h d) -> p h d", h=NH)
                        if l:
                            nc.vector.tensor_tensor(out=vaug[:, b, :, 0:HD], in0=src,
                                                    in1=bv_all[:, :].rearrange("p (h d) -> p h d", h=NH),
                                                    op=ALU.add).then_inc(v_ready, 1)
                        else:
                            nc.vector.tensor_copy(vaug[:, b, :, 0:HD], src).then_inc(v_ready, 1)
                over_chunks(dve, step)

            def finish(f, done, n):
                dve.wait_ge(done, n)
                nc.vector.tensor_copy(o_sb[:, :], PS[:, 4, 0:4 * L]).then_inc(osb_ready, 1)
                dve.wait_ge(oT_ps, f + 1)
                base = PS[0:L, 7, 0:1]
                p0 = base.ap[0]

                def view(off, dims):
                    return bass.AP(tensor=base.tensor, offset=base.offset + off, ap=[[p0[0], p0[1]]] + dims)
                nc.vector.reciprocal(rec[:, 0:12].rearrange("p (j a) -> p j a", a=3), view(8, [[32, 4], [137, 3]]))
                link(nc.vector.reciprocal(rec[:, 12:16], view(3 * 128 + 8, [[32, 4]])))
                nc.vector.tensor_tensor(out=ao[:, 0:12 * HD].rearrange("p (j a d) -> p j a d", a=3, d=HD),
                                        in0=view(0, [[32, 4], [137, 3], [1, HD]]),
                                        in1=rec[:, 0:12].rearrange("p (j a) -> p j a", a=3)[:, :, :, None].to_broadcast([L, 4, 3, HD]),
                                        op=ALU.mult)
                nc.vector.tensor_tensor(out=ao[:, 12 * HD:].rearrange("p (j d) -> p j d", d=HD),
                                        in0=view(3 * 128, [[32, 4], [1, HD]]),
                                        in1=rec[:, 12:16, None].to_broadcast([L, 4, HD]), op=ALU.mult).then_inc(ao_ready, 1)

            def add_projected(n):
                dve.wait_ge(aoT_ps, n + 1)
                nc.vector.tensor_copy(aoT[:, :], PS[:, 6, 0:L]).then_inc(aoT_ready, 1)
                dve.wait_ge(proj_ps, n + 1)
                link(nc.vector.tensor_tensor(out=x[:, :], in0=x[:, :], in1=PS[0:L, 7, 0:D], op=ALU.add))

            def self_attention(s):
                dve.wait_ge(qkv_ps, s + 1)
                if s == 0:
                    src = PS[0:L, 0, 0:2 * D].rearrange("p (h d) -> p h d", d=HD)
                    a = rope_a[:, :].rearrange("p (h d) -> p h d", d=HD)
                    b = rope_b[:, :].rearrange("p (h d) -> p h d", d=HD)
                    wide_h = [L, 2 * NH, HD]
                    half_h = [L, 2 * NH, HD // 2]
                    nc.vector.tensor_tensor(out=a, in0=src, in1=con["cos2"][0:L, None, :].to_broadcast(wide_h), op=ALU.mult)
                    nc.vector.tensor_tensor(out=b[:, :, 0::2], in0=src[:, :, 1::2],
                                            in1=con["nsin"][0:L, None, :].to_broadcast(half_h), op=ALU.mult)
                    link(nc.vector.tensor_tensor(out=b[:, :, 1::2], in0=src[:, :, 0::2],
                                                 in1=con["sin"][0:L, None, :].to_broadcast(half_h), op=ALU.mult))
                    nc.vector.tensor_tensor(out=qk[:, :], in0=rope_a[:, :], in1=rope_b[:, :], op=ALU.add)
                else:
                    nc.vector.tensor_copy(qk[:, :], PS[0:L, 0, 0:2 * D])
                nc.vector.tensor_copy(vaug[0:L, 0, :, 0:HD],
                                      PS[0:L, 0, 2 * D:3 * D].rearrange("p (h d) -> p h d", d=HD)).then_inc(qk_ready, 1)
                dve.wait_ge(qkT_ps, s + 1)
                link(nc.vector.tensor_copy(qkT[:, :, :], PS[:, 1, 0:2 * L].rearrange("p (a l) -> p a l", a=2)))
                full = [D, NH, L]
                nc.vector.tensor_tensor(out=kbd[:, :, :], in0=qkT[:, 1, None, :].to_broadcast(full),
                                        in1=con["head"][:, :, None].to_broadcast(full), op=ALU.mult).then_inc(kbd_ready, 1)
                nc.vector.tensor_tensor(out=qbd[:, :, :], in0=qkT[:, 0, None, :].to_broadcast(full),
                                        in1=con["head"][:, :, None].to_broadcast(full), op=ALU.mult).then_inc(qbd_ready, 1)
                dve.wait_ge(srow_ps, s + 1)
                link(nc.vector.tensor_reduce(out=sa_negm[:, :], in_=PS[0:L, 2:4, :].rearrange("p a (h l) -> p (a h) l", l=L),
                                             axis=AX.X, op=ALU.max, negate=True))
                nc.vector.tensor_tensor(out=sa_diag[:, :, :], in0=sa_negm[:, :, None].to_broadcast([L, NH, L]),
                                        in1=ident[0:L, None, 0:L].to_broadcast([L, NH, L]),
                                        op=ALU.mult).then_inc(diag_ready, 1)

            def mlp0():
                dve.wait_ge(g_ps, 1)
                link(nc.vector.tensor_copy(lg[:, 0:E0], PS[0:L, 0, 0:E0]))
                link(nc.vector.max(out=top8[:, :], in_=lg[:, 0:E0]))
                link(nc.vector.max_index(out=top_i[:, :], in_max=top8[:, :], in_values=lg[:, 0:E0]))
                link(nc.vector.tensor_copy(top_f[:, :], top_i[:, :]))
                link(nc.vector.tensor_scalar(hot[:, 0, :], con["iota"][0:L, :], top_f[:, 0:1], None, ALU.is_equal))
                b1 = con["b1"].rearrange("p (e k) -> p e k", e=E0)
                for b in range(E0 // 2):
                    dve.wait_ge(h_ps, b + 1)
                    for e in range(2):
                        nc.vector.tensor_tensor(
                            out=h0[:, b, e, :, :],
                            in0=PS[:, 1 + b, 256 * e:256 * e + 256].rearrange("p (k l) -> p k l", k=K0),
                            in1=b1[:, 2 * b + e, :, None].to_broadcast([128, K0, L]), op=ALU.add).then_inc(hb_ready, 1)
                for e in range(E0):
                    if e % 4 == 0:
                        dve.wait_ge(y_ps, e // 4 + 1)
                    link(nc.vector.scalar_tensor_tensor(out=x[:, :], in0=PS[0:L, 5 + e // 4, D * (e % 4):D * (e % 4 + 1)],
                                                        scalar=hot[:, 0, e:e + 1], in1=x[:, :], op0=ALU.mult, op1=ALU.add))

            def mlp1():
                dve.wait_ge(g_ps, 2)
                nc.vector.tensor_copy(gb1_all[:, :], PS[0:L, 0, E1:2 * E1])
                link(nc.vector.tensor_copy(lg[:, :], PS[0:L, 0, 0:E1]))
                nc.vector.tensor_reduce(out=sm[:, 0:1], in_=lg[:, :], axis=AX.X, op=ALU.max, negate=True).then_inc(lg_ready, 1)
                dve.wait_ge(exp_ready, 1)
                link(nc.vector.reciprocal(sm[:, 2:3], sm[:, 1:2]))
                link(nc.vector.scalar_tensor_tensor(out=sc[:, :], in0=sc[:, :], scalar=sm[:, 2:3], in1=gb1_all[:, :],
                                                    op0=ALU.mult, op1=ALU.add))
                link(nc.vector.max(out=top8[:, :], in_=sc[:, :]))
                link(nc.vector.max_index(out=top_i[:, :], in_max=top8[:, :], in_values=sc[:, :]))
                link(nc.vector.tensor_copy(top_f[:, :], top_i[:, :]))
                nc.vector.tensor_scalar(hot[:, 0, :], con["iota"][0:L, :], top_f[:, 0:1], None, ALU.is_equal)
                link(nc.vector.tensor_scalar(hot[:, 1, :], con["iota"][0:L, :], top_f[:, 1:2], None, ALU.is_equal))
                link(nc.vector.tensor_tensor(out=hot[:, 0, :], in0=hot[:, 0, :], in1=hot[:, 1, :], op=ALU.add))
                link(nc.vector.tensor_tensor(out=wm[:, :], in0=lg[:, :], in1=hot[:, 0, :], op=ALU.mult))
                link(nc.vector.tensor_scalar(hot[:, 1, :], hot[:, 0, :], -NOT_ASSIGNED, NOT_ASSIGNED, ALU.mult, ALU.add))
                nc.vector.tensor_tensor(out=wm[:, :], in0=wm[:, :], in1=hot[:, 1, :], op=ALU.add).then_inc(wm_ready, 1)
                dve.wait_ge(wmT_ps, 1)
                link(nc.vector.tensor_copy(wmT[:, :], PS[0:E1, 6, 0:L]))
                link(nc.vector.max(out=ranks[:, 0, :], in_=wmT[:, :]))
                link(nc.vector.match_replace(out=cut1[:, :], in_to_replace=ranks[:, 0, :], in_values=wmT[:, :],
                                             imm_value=NOT_ASSIGNED))
                link(nc.vector.max(out=ranks[:, 1, :], in_=cut1[:, :]))
                link(nc.vector.memset(ranks[:, 1, CAP - 8:8], NOT_ASSIGNED))
                link(nc.vector.match_replace(out=cut2[:, :], in_to_replace=ranks[:, 1, :], in_values=cut1[:, :],
                                             imm_value=NOT_ASSIGNED))
                link(nc.vector.tensor_tensor(out=cut1[:, :], in0=wmT[:, :], in1=cut2[:, :], op=ALU.not_equal))
                nc.vector.tensor_tensor(out=gT[:, :], in0=wmT[:, :], in1=cut1[:, :], op=ALU.mult).then_inc(gT_ready, 1)
                dve.wait_ge(g1_ps, 1)
                link(nc.vector.tensor_copy(gates[:, :], PS[0:L, 6, 128:128 + E1]))

                def accumulate(e):
                    if e % 4 == 0 or e == E1:
                        dve.wait_ge(z_ps, e // 4 + 1)
                    weight = gates[:, e:e + 1] if e < E1 else 1.0 / NSH
                    ins = nc.vector.scalar_tensor_tensor(out=x[:, :], in0=PS[0:L, 4 + (e // 4) % 2, D * (e % 4):D * (e % 4 + 1)],
                                                         scalar=weight, in1=x[:, :], op0=ALU.mult, op1=ALU.add)
                    if e == E1:
                        ins.then_inc(x_final, 1)
                    else:
                        link(ins)
                    if e % 4 == 3:
                        nc.vector.tensor_copy(sm[:, 3:4], sm[:, 2:3]).then_inc(z_used, 1)

                for b in range(NE1 // 2):
                    dve.wait_ge(silu_ready, b + 1)
                    if b >= 2:
                        dve.wait_ge(z_ps, (b - 2) // 2 + 1) if b % 2 == 1 else None
                    nc.vector.tensor_tensor(out=h1[:, b % 2],
                                            in0=PS[:, b % 4, :].rearrange("p (e w k l) -> p e w k l", e=2, w=2, k=K1)[:, :, 1],
                                            in1=act1[:, b % 2], op=ALU.mult).then_inc(m_ready, 1)
                    if b % 2 == 1 and b >= 3:
                        for e in range(2 * (b - 3), 2 * (b - 3) + 4):
                            accumulate(e)
                for e in range(E1 - 4, E1 + 1):
                    accumulate(e)

            dve.wait_ge(cons_in_sem, 16)
            nc.vector.tensor_copy(identb[:, :], ident)
            nc.vector.tensor_copy(ident8[:, :, :], ident[0:L, None, 0:L].to_broadcast([L, 8, L]))
            nc.vector.memset(ones[:, :], 1.0)
            nc.vector.memset(zeros[:, :], 0.0)
            nc.vector.memset(neg_half[:, :], -0.5)
            link(nc.vector.memset(shift_pick[:, :, :], 0.0))
            for part in range(3):
                nc.vector.memset(shift_pick[:, part, NR + part:NR + part + 1], 1.0)
            nc.vector.memset(run_max[:, :, :], -3.0e38)
            nc.vector.memset(kstack[NR:NS, :, :, :], 1.0)
            link(nc.vector.memset(vaug[:, :, :, HD:HD + 1], 1.0))
            nc.vector.tensor_copy(valid_ident[:, :], ident[0:L, 0:L]).then_inc(const_ready, 1)
            dve.wait_ge(x_in_sem, 16)
            layernorm(0)
            queries(0)
            dve.wait_ge(bv_ps, 1)
            nc.vector.tensor_copy(bv_all[:, :], PS[:, 7, D:2 * D]).then_inc(bv_ready, 1)
            maxima(0)
            shift_parts(0)
            values(0)
            finish(0, pv_done, NT)
            add_projected(0)
            layernorm(1)
            self_attention(0)
            finish(1, sa_pv, 1)
            dve.wait_ge(ao_ready, 2)
            link(nc.vector.tensor_tensor(out=x[:, :], in0=x[:, :], in1=ao[:, :], op=ALU.add))
            layernorm(2)
            mlp0()
            link(nc.vector.tensor_reduce(out=row_open[:, 0:1], in_=mask_max[0:L, :], axis=AX.X, op=ALU.max))
            link(nc.vector.tensor_scalar(row_open[:, 1:2], row_open[:, 0:1], 0.0, None, ALU.is_equal))
            link(nc.vector.tensor_scalar(valid_ident[:, :], ident[0:L, 0:L], row_open[:, 1:2], None, ALU.mult))
            layernorm(3)
            queries(1)
            maxima(1)
            shift_parts(1)
            values(1)
            finish(2, pv_done, 2 * NT)
            add_projected(1)
            layernorm(4)
            self_attention(1)
            finish(3, sa_pv, 2)
            add_projected(2)
            layernorm(5)
            mlp1()

        @block.tensor
        def _(pe):
            def transposed_norm(n):
                pe.wait_ge(xn_ready, n + 1)
                nc.tensor.transpose(PS[:, 7, 0:L], xn[:, :], ident[0:L, 0:L]).then_inc(xnT_ps, 1)
                pe.wait_ge(xnT_ready, n + 1)

            def with_bias(dst, lhsT, w, bias, signal):
                nc.tensor.matmul(dst, lhsT, w, start=True, stop=False)
                nc.tensor.matmul(dst, ones[0:1, 0:L], bias, start=False, stop=True).then_inc(signal, 1)

            def queries(l):
                if l:
                    with_bias(PS[0:L, 7, 0:D], xnT[:, :], mat["wq1"], row["bq1"], q_ps)
                else:
                    nc.tensor.matmul(PS[0:L, 7, 0:D], xnT[:, :], mat["wq0"], start=True, stop=True).then_inc(q_ps, 1)
                pe.wait_ge(q_ready, l + 1)
                for p in range(NP):
                    ins = nc.tensor.matmul(PS[0:NR, 6, p * L:(p + 1) * L],
                                           q_sb[:, p].rearrange("p t r -> p (t r)"),
                                           valid_ident[:, :], start=True, stop=True)
                ins.then_inc(qrep_ps, 1)

            def project_k(l, i, par):
                c = 2 * i + par
                pe.wait_ge(ctx_in[par], 16 * arrived(par, 2 * l, i))
                if not isinstance(i, int) or c > 0:
                    pe.wait_ge(kf_ready, NC * l + c)
                for h in range(2):
                    ins = nc.tensor.matmul(PS[:, h, 0:HC], mat[f"wk{l}"], ctx_c[:, par, h * HC:(h + 1) * HC],
                                           start=True, stop=True)
                ins.then_inc(k_ps, 1)

            def pass_a(l):
                project_k(l, 0, 0)

                def step(i, par):
                    c = 2 * i + par
                    if not isinstance(i, int) or c + 1 < NC:
                        project_k(l, i + par, 1 - par)
                    if isinstance(i, int) and c == 0:
                        pe.wait_ge(qstack_ready, l + 1)
                    pe.wait_ge(ks_in[par], 16 * len(TERMS) * arrived(par, 2 * l, i))
                    for u in range(NP):
                        n = NP * c + u
                        if not isinstance(i, int) or n >= 2:
                            pe.wait_ge(a_used, NC * NP * l + n - 1)
                        for h in range(2):
                            ins = nc.tensor.matmul(PS[:, 2 + 2 * (u % 2) + h, 0:HC],
                                                   qstack[0:NR, u, :, :].rearrange("p a b -> p (a b)"),
                                                   kstack[0:NR, par, u, h * HC:(h + 1) * HC], start=True, stop=True)
                        ins.then_inc(a_ps, 1)
                over_chunks(pe, step)

            def shift(l):
                pe.wait_ge(mdiag_ready, 3 * (l + 1))
                pe.wait_ge(kf_ready, NC * (l + 1))
                for h in range(2):
                    for part in range(3):
                        ins = nc.tensor.matmul(PS[0:NS, h, :], shift_pick[:, part, :],
                                               mdiag[:, part, 4 * h:4 * h + 4, :].rearrange("p a b -> p (a b)"),
                                               start=(part == 0), stop=(part == 2))
                ins.then_inc(shift_ps, 1)

            def clear_sums():
                nc.tensor.matmul(PS[:, 4, 0:4 * L], zeros[:, 0:128], zeros[:, :], start=True, stop=True)

            def pv(weights, moving, rows_):
                for n, (j, wc, mc, oc) in enumerate(PV):
                    k = wc.stop - wc.start
                    ins = nc.tensor.matmul(PS[32 * j:32 * j + k, 4, oc], weights[:, wc], moving[:, mc],
                                           start=False, stop=True, skip_group_check=True)
                return ins

            def pass_b(l):
                def scores(i, par, k):
                    t = (2 * i + par) * CT + k
                    b = (par + k) % 2
                    late = not isinstance(i, int) or t >= 2
                    if k == 0:
                        pe.wait_ge(ctx_in[par], 16 * arrived(par, 2 * l + 1, i))
                    if late:
                        pe.wait_ge(v_ready, NT * l + t - 1)
                    nc.tensor.matmul(PS[:, 5 + b, 0:D], ctx_c[:, par, k * T:(k + 1) * T], mat[f"wv{l}"],
                                     start=True, stop=True).then_inc(v_ps, 1)
                    if k == 0:
                        pe.wait_ge(ks_in[par], 16 * len(TERMS) * arrived(par, 2 * l + 1, i))
                        if l:
                            pe.wait_ge(mc_in[par], 16 * arrived(par, 1, i))
                    if late:
                        pe.wait_ge(p_ready, NT * l + t - 1)
                    for h in range(2):
                        if l:
                            nc.tensor.matmul(PS[:, 2 * b + h, :], mask_c[0:L, par, k * T:(k + 1) * T],
                                             ident8[:, :, :].rearrange("p a b -> p (a b)"), start=True, stop=True)
                        for u in range(4 * h, 4 * h + 4):
                            ins = nc.tensor.matmul(PS[:, 2 * b + h, 128 * (u % 4):128 * (u % 4 + 1)],
                                                   kstack[0:NS, par, u, k * T:(k + 1) * T],
                                                   qstack[0:NS, u, :, :].rearrange("p a b -> p (a b)"),
                                                   start=not l, stop=True, skip_group_check=True)
                    ins.then_inc(s_ps, 1)

                clear_sums()
                pe.wait_ge(shift_ready, l + 1)
                scores(0, 0, 0)

                def step(i, par):
                    for k in range(CT):
                        t = (2 * i + par) * CT + k
                        b = (par + k) % 2
                        if k + 1 < CT:
                            scores(i, par, k + 1)
                        elif not isinstance(i, int) or t + 1 < NT:
                            scores(i + par, 1 - par, 0)
                        pe.wait_ge(v_ready, NT * l + t + 1)
                        pe.wait_ge(p_ready, NT * l + t + 1)
                        pv(vaug[:, b, :, :].rearrange("p h d -> p (h d)"), probs[:, b, :], 128).then_inc(pv_done, 1)
                over_chunks(pe, step)

            def finish(f):
                pe.wait_ge(osb_ready, f + 1)
                for a in range(4):
                    ins = nc.tensor.transpose(PS[0:L, 7, a * 128:(a + 1) * 128], o_sb[:, a * L:(a + 1) * L], ident)
                ins.then_inc(oT_ps, 1)
                pe.wait_ge(ao_ready, f + 1)

            def project_out(n, w, bias):
                nc.tensor.transpose(PS[:, 6, 0:L], ao[:, :], ident[0:L, 0:L]).then_inc(aoT_ps, 1)
                pe.wait_ge(aoT_ready, n + 1)
                with_bias(PS[0:L, 7, 0:D], aoT[:, :], w, bias, proj_ps)

            def self_attention(s):
                with_bias(PS[0:L, 0, 0:3 * D], xnT[:, :], mat[f"wqkv{s}"], row[f"bqkv{s}"], qkv_ps)
                pe.wait_ge(qk_ready, s + 1)
                for a in range(2):
                    ins = nc.tensor.transpose(PS[:, 1, a * L:(a + 1) * L], qk[:, a * D:(a + 1) * D], ident[0:L, 0:L])
                ins.then_inc(qkT_ps, 1)
                pe.wait_ge(kbd_ready, s + 1)
                for h in range(2):
                    ins = nc.tensor.matmul(PS[0:L, 2 + h, :], qkT[:, 0, :],
                                           kbd[:, 8 * h:8 * h + 8, :].rearrange("p a b -> p (a b)"), start=True, stop=True)
                ins.then_inc(srow_ps, 1)
                pe.wait_ge(qbd_ready, s + 1)
                for h in range(2):
                    nc.tensor.matmul(PS[0:L, h, :], qkT[:, 1, :],
                                     qbd[:, 8 * h:8 * h + 8, :].rearrange("p a b -> p (a b)"), start=True, stop=False)
                pe.wait_ge(diag_ready, s + 1)
                for h in range(2):
                    ins = nc.tensor.matmul(PS[0:L, h, :], ones[0:L, 0:L],
                                           sa_diag[:, 8 * h:8 * h + 8, :].rearrange("p a b -> p (a b)"), start=False, stop=True)
                ins.then_inc(st_ps, 1)
                clear_sums()
                pe.wait_ge(sp_ready, s + 1)
                pv(vaug[0:L, 0, :, :].rearrange("p h d -> p (h d)"), probs[0:L, 0, :], L).then_inc(sa_pv, 1)

            def mlp0():
                with_bias(PS[0:L, 0, 0:E0], xnT[:, :], mat["gate0"], row["gb0"], g_ps)
                pe.wait_ge(w0_sem, 32)
                for e in range(E0):
                    for k in range(K0):
                        ins = nc.tensor.matmul(PS[:, 1 + e // 2, 256 * (e % 2) + k * L:256 * (e % 2) + (k + 1) * L],
                                               w1[:, e, k * 128:(k + 1) * 128], xnT[:, :], start=True, stop=True)
                    if e % 2:
                        ins.then_inc(h_ps, 1)
                for e in range(E0):
                    pe.wait_ge(h_ready, e + 1)
                    dst = PS[0:L, 5 + e // 4, D * (e % 4):D * (e % 4 + 1)]
                    for k in range(K0):
                        nc.tensor.matmul(dst, h0[:, e // 2, e % 2, k, :], w2[:, e * K0 + k, :], start=(k == 0), stop=False)
                    ins = nc.tensor.matmul(dst, ones[0:1, 0:L], row["b2"][:, e * D:(e + 1) * D], start=False, stop=True)
                    if e % 4 == 3:
                        ins.then_inc(y_ps, 1)

            def mlp1():
                nc.tensor.matmul(PS[0:L, 0, E1:2 * E1], ones[0:1, 0:L], row["gb1"], start=True, stop=True)
                nc.tensor.matmul(PS[0:L, 0, 0:E1], xnT[:, :], mat["gate1"], start=True, stop=True).then_inc(g_ps, 1)
                pe.wait_ge(wm_ready, 1)
                nc.tensor.transpose(PS[0:E1, 6, 0:L], wm[:, :], ident[0:L, 0:L]).then_inc(wmT_ps, 1)
                pe.wait_ge(gT_ready, 1)
                nc.tensor.transpose(PS[0:L, 6, 128:128 + E1], gT[:, :], ident[0:E1, 0:E1]).then_inc(g1_ps, 1)
                pe.wait_ge(w1_sem, 48)

                def up(b):
                    if b >= 4:
                        pe.wait_ge(m_ready, b - 3)
                    for e in range(2):
                        for w, ws in enumerate((w1s, w3s)):
                            for k in range(K1):
                                at = 256 * e + 128 * w + k * L
                                ins = nc.tensor.matmul(PS[:, b % 4, at:at + L], ws[:, 2 * b + e, k * 128:(k + 1) * 128],
                                                       xnT[:, :], start=True, stop=True)
                    ins.then_inc(m_ps, 1)

                def down(b):
                    pe.wait_ge(m_ready, b + 1)
                    for e in (2 * b, 2 * b + 1):
                        y = min(e, E1)
                        if e % 4 == 0 and 8 <= e:
                            pe.wait_ge(z_used, e // 4 - 1)
                        for k in range(K1):
                            ins = nc.tensor.matmul(PS[0:L, 4 + (y // 4) % 2, D * (y % 4):D * (y % 4 + 1)],
                                                   h1[:, b % 2, e % 2, k, :], w2s[:, e * K1 + k, :],
                                                   start=(k == 0 and e <= E1), stop=(k == K1 - 1 and e != E1))
                        if e % 4 == 3 or e == NE1 - 1:
                            ins.then_inc(z_ps, 1)

                up(0)
                for b in range(NE1 // 2):
                    if b + 1 < NE1 // 2:
                        up(b + 1)
                    down(b)

            pe.wait_ge(const_ready, 1)
            transposed_norm(0)
            pe.wait_ge(mats_sem, 32)
            queries(0)
            nc.tensor.matmul(PS[:, 7, D:2 * D], ones[0:1, :], row["bv1"], start=True, stop=True).then_inc(bv_ps, 1)
            pe.wait_ge(bv_ready, 1)
            pass_a(0)
            shift(0)
            pass_b(0)
            finish(0)
            project_out(0, mat["wo0"], row["bo0"])
            transposed_norm(1)
            self_attention(0)
            finish(1)
            transposed_norm(2)
            mlp0()
            transposed_norm(3)
            queries(1)
            pass_a(1)
            shift(1)
            pass_b(1)
            finish(2)
            project_out(1, mat["wo1"], row["bo1"])
            transposed_norm(4)
            self_attention(1)
            finish(3)
            project_out(2, mat["wout1"], row["bout1"])
            transposed_norm(5)
            mlp1()


def constants():
    con = np.zeros((128, CONS["bk1"][0]), np.float32)

    def put(name, a):
        at = CONS[name][0]
        con[:a.shape[0], at:at + a.shape[1]] = a
    put("ident", np.eye(128, dtype=np.float32))
    put("head", (np.arange(D)[:, None] // HD == np.arange(NH)[None, :]).astype(np.float32))
    sel = np.zeros((NR, 6), np.float32)
    for r in range(NR):
        t, hh = r // (2 * HD), (r // HD) % 2
        sel[r, 2 * TERMS[t][1] + hh] = 1
    put("qsel", sel)
    theta = np.float32(10000.0) ** (np.float32(-2.0) * np.arange(HD // 2, dtype=np.float32) / np.float32(HD))
    ang = np.outer(np.arange(L, dtype=np.float32), theta.astype(np.float32)).astype(np.float32)
    put("cos2", np.repeat(np.cos(ang), 2, axis=1))
    put("nsin", -np.sin(ang))
    put("sin", np.sin(ang))
    put("iota", np.tile(np.arange(E1, dtype=np.float32), (L, 1)))
    return con


def kernel(**inputs):
    import concourse.bacc as bacc
    from concourse.bass_utils import run_bass_kernel_spmd

    a = {k: np.asarray(v) for k, v in inputs.items()}

    def by_pair(w):
        return w.reshape(w.shape[0], NP, 2, HD).transpose(0, 2, 3, 1).reshape(w.shape[0], D)

    mats = np.concatenate([
        a["L0_xattn_w_q"].T, by_pair(a["L0_xattn_w_kv"][:D].T), a["L0_xattn_w_kv"][D:].T, a["L0_xattn_w_out"].T,
        a["L0_attn_wq_w"].T, a["L0_attn_wk_w"].T, a["L0_attn_wv_w"].T,
        a["L1_xattn_Wq"], by_pair(a["L1_xattn_Wk"]), a["L1_xattn_Wv"], a["L1_xattn_Wo"],
        a["L1_attn_Wqkv"], a["L1_attn_Wout"], a["L0_ffn_gate_w"].T, a["L1_ffn_gate_w"]], axis=1)
    rows = np.concatenate([
        a["L0_xattn_b_out"], a["L0_attn_wq_b"], a["L0_attn_wk_b"], a["L0_attn_wv_b"], a["L1_xattn_bq"], a["L1_xattn_bv"],
        a["L1_xattn_bo"], a["L1_attn_bqkv"], a["L1_attn_bout"], a["L0_ffn_gate_b"], a["L1_ffn_gate_b"],
        a["L0_ffn_b2"].reshape(-1)])[None, :]
    cons = np.concatenate([constants(), by_pair(a["L1_xattn_bk"][None, :]).T,
                           a["L0_ffn_b1"].reshape(E0 * K0, 128).T], axis=1)
    arrays = {
        "x_in": a["x"][0],
        "ctx_t": a["ctx_1024"][0].T,
        "mask_in": a["mask_Bx1xSxS2_ik1"][0, 0],
        "mats_in": mats,
        "rows_in": rows,
        "cons_in": cons,
        "f0w1": a["L0_ffn_w1"].transpose(2, 0, 1),
        "f0w2": a["L0_ffn_w2"].reshape(E0, D, K0, 128).transpose(3, 0, 2, 1).reshape(128, E0 * K0, D),
        "f1w13": np.stack([np.concatenate([a["L1_ffn_ew1"], a["L1_ffn_sw1"]]).transpose(1, 0, 2),
                           np.concatenate([a["L1_ffn_ew3"], a["L1_ffn_sw3"]]).transpose(1, 0, 2)], axis=1),
        "f1w2": np.concatenate([a["L1_ffn_ew2"], a["L1_ffn_sw2"]]).reshape(NE1, K1, 128, D)
                .transpose(2, 0, 1, 3).reshape(128, NE1 * K1, D),
    }
    arrays = {k: np.ascontiguousarray(v) for k, v in arrays.items()}
    nc = bacc.Bacc("TRN2", target_bir_lowering=False, num_devices=1)
    args = [nc.dram_tensor(k, v.shape, mybir.dt.from_np(v.dtype), kind="ExternalInput").ap() for k, v in arrays.items()]
    args.append(nc.dram_tensor("x_out", (L, D), F32, kind="ExternalOutput").ap())
    perceiver(nc, *args)
    r = run_bass_kernel_spmd(nc, [arrays], core_ids=[0])
    return r.results[0]["x_out"].reshape(1, L, D)
```

```python
from contextlib import ExitStack

import numpy as np

import concourse.bass as bass
from concourse import mybir

F32 = mybir.dt.float32
BF16 = mybir.dt.bfloat16
I32 = mybir.dt.int32
U32 = mybir.dt.uint32
ALU = mybir.AluOpType
ACT = mybir.ActivationFunctionType
AX = mybir.AxisListType

D = 128
L = 64
NH = 16
HD = D // NH
NP = NH // 2
S = 6272
T = 128
CT = 7
C = CT * T
NC = S // C
NT = S // T
HC = C // 2
PIECES = 4
SCALE = HD ** -0.5
EPS = 1e-5
TERMS = [(0, 0), (1, 0), (0, 1), (1, 1), (0, 2), (2, 0)]
NR = len(TERMS) * 2 * HD
NS = NR + 3
MASKED = -float(2 ** 30)
E0, H0 = 8, 512
K0 = H0 // 128
E1, H1 = 16, 256
K1 = H1 // 128
NSH = 2
NE1 = E1 + NSH
CAP = 10
NOT_ASSIGNED = -1e30

MATS = {}
_at = 0
for _n, _w in (("wq0", D), ("wk0", D), ("wv0", D), ("wo0", D), ("wqkv0", 3 * D), ("wq1", D), ("wk1", D), ("wv1", D),
               ("wo1", D), ("wqkv1", 3 * D), ("wout1", D), ("gate0", E0), ("gate1", E1)):
    MATS[_n] = (_at, _at + _w)
    _at += _w
NMAT = _at
ROWS = {}
_at = 0
for _n, _w in (("bo0", D), ("bqkv0", 3 * D), ("bq1", D), ("bv1", D), ("bo1", D), ("bqkv1", 3 * D), ("bout1", D),
               ("gb0", E0), ("gb1", E1), ("b2", E0 * D)):
    ROWS[_n] = (_at, _at + _w)
    _at += _w
NROW = _at
CONS = {}
_at = 0
for _n, _w in (("ident", D), ("head", NH), ("qsel", 6), ("cos2", HD), ("nsin", HD // 2), ("sin", HD // 2), ("iota", E1),
               ("bk1", 1), ("b1", E0 * K0)):
    CONS[_n] = (_at, _at + _w)
    _at += _w
NCON = _at
PV = [(j, slice(27 * j, 27 * j + 27), slice(3 * L * j, 3 * L * (j + 1)), slice(0, 3 * L)) for j in range(4)]
PV += [(j, slice(108 + 9 * j, 117 + 9 * j), slice((12 + j) * L, (13 + j) * L), slice(3 * L, 4 * L)) for j in range(4)]


def perceiver(nc, x_in, ctx_t, mask, mats_in, rows_in, cons_in, f0w1, f0w2, f1w13, f1w2, out, last_stage=6):
    ctx = ExitStack()
    with ctx:
        def sb(name, shape, dt=F32):
            return ctx.enter_context(nc.sbuf_tensor(name, shape, dt))

        def sem(name):
            return ctx.enter_context(nc.semaphore(name))

        mats = sb("mats", [128, NMAT])
        rows = sb("rows", [1, NROW])
        cons = sb("cons", [128, NCON])
        mat = {n: mats[:, a:b] for n, (a, b) in MATS.items()}
        row = {n: rows[0:1, a:b] for n, (a, b) in ROWS.items()}
        con = {n: cons[:, a:b] for n, (a, b) in CONS.items()}
        ident = con["ident"]
        identb = sb("identb", [128, D], BF16)
        ident8 = sb("ident8", [128, 8, L], BF16)
        ones = sb("ones", [128, D])
        zeros = sb("zeros", [128, 256])
        neg_half = sb("neg_half", [L, 1])
        shift_pick = sb("shift_pick", [128, 3, NS], BF16)
        w12 = sb("w12", [128, E0 * H0 + E0 * K0 * D])
        w1 = w12[:, 0:E0 * H0].rearrange("p (e h) -> p e h", e=E0)
        w2 = w12[:, E0 * H0:].rearrange("p (e d) -> p e d", d=D)
        w2s = w12[:, 0:NE1 * K1 * D].rearrange("p (e d) -> p e d", d=D)
        x = sb("x", [L, D])
        bn = sb("bn", [L, 6])
        mu_var = sb("mu_var", [L, 2])
        var_eps = sb("var_eps", [L, 1])
        rstd = sb("rstd", [L, 1])
        xn = sb("xn", [L, D])
        xnT = sb("xnT", [D, L])
        ctx_c = sb("ctx_c", [128, 2, C])
        kf = sb("kf", [128, 2, C])
        kr = sb("kr", [128, 2, C])
        kparts = sb("kparts", [128, 3, S], BF16)
        kstack = sb("kstack", [128, 2, NP, C], BF16)
        valid_ident = sb("valid_ident", [L, L])
        qb1 = sb("qb1", [NR, NP * L], BF16)
        qb2 = sb("qb2", [NR, NP * L], BF16)
        qb3 = sb("qb3", [NR, NP * L], BF16)
        scratch = sb("scratch", [128, 3 * NH * L])
        qr1 = scratch[0:NR, 0:NP * L]
        qr2 = scratch[0:NR, NP * L:2 * NP * L]
        q_sb = scratch[0:L, 2 * NP * L:2 * NP * L + NP * NR].rearrange("p (u t r) -> p u t r", u=NP, t=len(TERMS))
        qmix = sb("qmix", [NR, 2, NP * L], BF16)
        qstack = sb("qstack", [128, NP, 2, L], BF16)
        row_max = sb("row_max", [128, NC, NP])
        run_max = sb("run_max", [128, 2, NP])
        negm = sb("negm", [128, NP])
        negm_r1 = sb("negm_r1", [128, NP])
        negm_r2 = sb("negm_r2", [128, NP])
        mpart = sb("mpart", [128, 3, NP], BF16)
        mdiag = scratch[:, 0:3 * NP * 64].bitcast(BF16).rearrange("p (k u m) -> p k u m", k=3, u=NP)
        probs = sb("probs", [128, 2, NH * L])
        vaug = sb("vaug", [128, 2, NH, HD + 1])
        bv_all = sb("bv_all", [128, D])
        mask_raw = kr[:, :, :].bitcast(I32)
        mask_add = sb("mask_add", [128, S], BF16)
        mask_c = sb("mask_c", [128, 2, C], BF16)
        masked_out = sb("masked_out", [128, 2, C], BF16)
        mask_max = sb("mask_max", [128, NC])
        row_open = sb("row_open", [L, 2])
        o_sb = sb("o_sb", [128, 4 * L])
        rec = sb("rec", [L, NH])
        ao = sb("ao", [L, D])
        aoT = sb("aoT", [D, L])
        qk = sb("qk", [L, 2 * D])
        rope_a = sb("rope_a", [L, 2 * D])
        rope_b = sb("rope_b", [L, 2 * D])
        qkT = sb("qkT", [D, 2, L])
        kbd = scratch[:, 0:NH * L].rearrange("p (h l) -> p h l", h=NH)
        qbd = scratch[:, NH * L:2 * NH * L].rearrange("p (h l) -> p h l", h=NH)
        sa_negm = sb("sa_negm", [L, NH])
        sa_diag = scratch[0:L, 2 * NH * L:3 * NH * L].rearrange("p (h l) -> p h l", h=NH)
        lg = sb("lg", [L, E1])
        top8 = sb("top8", [L, 8])
        top_i = sb("top_i", [L, 8], U32)
        top_f = sb("top_f", [L, 8])
        hot = sb("hot", [L, 2, E1])
        h0 = probs[:, :, :].rearrange("p a b -> p (a b)").rearrange("p (b e k l) -> p b e k l", b=4, e=2, k=K0)
        sm = sb("sm", [L, 8])
        sc = sb("sc", [L, E1])
        gb1_all = sb("gb1_all", [L, E1])
        wm = sb("wm", [L, E1])
        wmT = sb("wmT", [E1, L])
        cut1 = sb("cut1", [E1, L])
        cut2 = sb("cut2", [E1, L])
        ranks = sb("ranks", [E1, 2, 8])
        gT = sb("gT", [E1, L])
        gates = sb("gates", [L, E1])
        big = kparts[:, :, :].rearrange("p a b -> p (a b)").bitcast(F32)
        w1s = big[:, 0:NE1 * H1].rearrange("p (e h) -> p e h", e=NE1)
        w3s = big[:, NE1 * H1:2 * NE1 * H1].rearrange("p (e h) -> p e h", e=NE1)
        act1 = sb("act1", [128, 2, 2, K1, L])
        h1 = sb("h1", [128, 2, 2, K1, L])

        PS = ctx.enter_context(nc.psum_tensor("PS", [128, 8, 512], F32))

        x_in_sem = sem("x_loaded")
        cons_in_sem = sem("cons_loaded")
        first_mats_sem = sem("first_mats_loaded")
        mats_sem = sem("mats_loaded")
        w0_sem = sem("mlp0_loaded")
        w1_sem = sem("mlp1_loaded")
        ctx_in = [sem("ctx_in_even"), sem("ctx_in_odd")]
        ks_in = [sem("kstack_in_even"), sem("kstack_in_odd")]
        raw_in = [sem("mask_raw_in_even"), sem("mask_raw_in_odd")]
        mc_in = [sem("mask_in_even"), sem("mask_in_odd")]
        out_sem = sem("out_stored")
        const_ready = sem("const_ready")
        dve_step = sem("dve_step")
        var_ready, rstd_ready, xn_ready = sem("var_ready"), sem("rstd_ready"), sem("xn_ready")
        xnT_ps, xnT_ready = sem("xnT_ps"), sem("xnT_ready")
        q_ps, q_ready, qrep_ps, qb1_ready, qstack_ready = (sem(n) for n in
            ("q_ps", "q_ready", "qrep_ps", "qb1_ready", "qstack_ready"))
        k_ps, kf_ready, k1_ready, kr_ready, k2_ready, k3_ready = (sem(n) for n in
            ("k_ps", "kf_ready", "k1_ready", "kr_ready", "k2_ready", "k3_ready"))
        a_ps, a_used = sem("a_ps"), sem("a_used")
        mdiag_ready, shift_ps, shift_ready = sem("mdiag_ready"), sem("shift_ps"), sem("shift_ready")
        v_ps, v_ready, s_ps, p_ready, pv_done = (sem(n) for n in ("v_ps", "v_ready", "s_ps", "p_ready", "pv_done"))
        bv_ps, bv_ready = sem("bv_ps"), sem("bv_ready")
        mask_ready = sem("mask_ready")
        osb_ready, oT_ps, ao_ready, aoT_ps, aoT_ready, proj_ps = (sem(n) for n in
            ("osb_ready", "oT_ps", "ao_ready", "aoT_ps", "aoT_ready", "proj_ps"))
        qkv_ps, qk_ready, qkT_ps, kbd_ready, qbd_ready, srow_ps, diag_ready, st_ps, sp_ready, sa_pv = (sem(n) for n in
            ("qkv_ps", "qk_ready", "qkT_ps", "kbd_ready", "qbd_ready", "srow_ps", "diag_ready", "st_ps", "sp_ready", "sa_pv"))
        g_ps, h_ps, hb_ready, h_ready, y_ps, y_used = (sem(n) for n in
            ("gate_ps", "h_ps", "hb_ready", "h_ready", "y_ps", "y_used"))
        lg_ready, exp_ready, wm_ready, wmT_ps, gT_ready, g1_ps = (sem(n) for n in
            ("lg_ready", "exp_ready", "wm_ready", "wmT_ps", "gT_ready", "gates_ps"))
        m_ps, silu_ready, m_ready, z_ps, z_used = (sem(n) for n in ("m_ps", "silu_ready", "m_ready", "z_ps", "z_used"))
        x_final = sem("x_final")

        ALL, LATER = ((NC + 1) // 2, NC // 2), ((NC - 1) // 2, NC // 2 - 1)

        def ctx_loads(par, ph, half):
            return half + 1 if ph == 0 else ALL[par] + (ph - 1) * LATER[par] + half

        def stack_loads(par, ph, half):
            before = (0, ALL[par], ALL[par] + LATER[par], 2 * ALL[par] + LATER[par])[ph]
            return before + half + (1 if ph % 2 == 0 else 0)

        def mask_loads(par, ph, half):
            return half + 1 if ph == 2 else ALL[par] + half

        def over_chunks(eng, step, first=True):
            if first:
                step(0, 0, 0)
            with eng.Fori(0, (NC - 3) // 2) as i:
                step(2 * i + 1, 1, i)
                step(2 * i + 2, 0, i + 1)
            step(NC - 2, 1, NC // 2 - 1)
            step(NC - 1, 0, NC // 2)

        def over_later_chunks(eng, step):
            with eng.Fori(1, NC // 2) as i:
                step(2 * i, 0, i)
                step(2 * i + 1, 1, i)
            step(NC - 1, 0, NC // 2)

        def written_out(step):
            for c in range(NC):
                step(c, c % 2, c // 2)

        def known(c, value):
            return isinstance(c, int) and c == value

        def once(eng, value):
            return value if isinstance(value, int) else eng.snap(value)

        block = ctx.enter_context(nc.Block())

        @block.sync
        def _(sp):
            sp.dma_start(x[:, :], x_in).then_inc(x_in_sem, 16)
            sp.dma_start(cons[:, :], cons_in).then_inc(cons_in_sem, 16)
            sp.dma_start(mats[:, 0:2 * D], mats_in[:, 0:2 * D]).then_inc(first_mats_sem, 16)

            def load_ctx(at, par):
                sp.dma_start(ctx_c[:, par, :], ctx_t[:, bass.ds(at, C)]).then_inc(ctx_in[par], 16)

            load_ctx(0, 0)
            load_ctx(C, 1)
            sp.dma_start(mats[:, 2 * D:], mats_in[:, 2 * D:]).then_inc(mats_sem, 16)
            sp.dma_start(rows[:, :], rows_in).then_inc(mats_sem, 16)

            def restack(at, par, parts=(0, 1, 2)):
                for t, (kp, _) in enumerate(TERMS):
                    if kp in parts:
                        sp.dma_start(kstack[2 * HD * t:2 * HD * (t + 1), par, :, :],
                                     kparts[:, kp, bass.ds(at, C)]).then_inc(ks_in[par], 16)

            def load_mask(at, par):
                sp.dma_start(mask_c[:, par, :], mask_add[:, bass.ds(at, C)]).then_inc(mc_in[par], 16)

            def settled():
                sp.wait_ge(cons_in_sem, 16)

            def load_raw(at, par):
                for half in range(2):
                    sp.dma_start(mask_raw[L * half:L * (half + 1), par, :],
                                 mask[:, bass.ds(at, C)]).then_inc(raw_in[par], 16)

            for l in range(2):
                def chunk_a(c, par, half):
                    at = once(sp, c * C)
                    ahead = once(sp, (c + 2) * C)
                    split = once(sp, c + (NC * l + 1))
                    scored = once(sp, NP * c + (NC * NP * l - NP + 1))
                    if not isinstance(c, int) or c + 2 < NC:
                        sp.wait_ge(k_ps, split)
                        load_ctx(ahead, par)
                    if l:
                        if known(c, 0):
                            sp.wait_ge(mask_ready, NC)
                        else:
                            sp.wait_ge(a_used, scored)
                        load_mask(at, par)
                    settled()
                    sp.wait_ge(k1_ready, split)
                    if known(c, 0):
                        if l:
                            sp.wait_ge(s_ps, NT)
                    else:
                        sp.wait_ge(a_ps, scored)
                    restack(at, par, (0,))
                    settled()
                    sp.wait_ge(k2_ready, split)
                    restack(at, par, (1,))
                    settled()
                    sp.wait_ge(k3_ready, split)
                    restack(at, par, (2,))

                over_chunks(sp, chunk_a)
                if l == 0:
                    load_raw((NC - 1) * C, 0)
                    load_raw((NC - 2) * C, 1)
                    sp.dma_start(w1, f0w1).then_inc(w0_sem, 16)
                    sp.dma_start(w2, f0w2).then_inc(w0_sem, 16)
                else:
                    sp.wait_ge(y_ps, 2)
                    sp.dma_start(w2s, f1w2).then_inc(w1_sem, 16)

                def chunk_b(c, par, half):
                    at = once(sp, c * -C + (NC - 1) * C)
                    tiles = once(sp, CT * c + (NT * l - CT))
                    converted = once(sp, c - 1)
                    settled()
                    sp.wait_ge(v_ps, tiles)
                    sp.wait_ge(s_ps, tiles)
                    load_ctx(at, par)
                    restack(at, par)
                    if l:
                        load_mask(at, par)
                    else:
                        sp.wait_ge(mask_ready, converted)
                        load_raw(at, par)

                over_later_chunks(sp, chunk_b)
            for par in range(2):
                sp.wait_ge(ks_in[par], 16 * len(TERMS) * 2 * (ALL[par] + LATER[par]))
            sp.dma_start(w1s, f1w13[:, 0]).then_inc(w1_sem, 16)
            sp.dma_start(w3s, f1w13[:, 1]).then_inc(w1_sem, 16)
            sp.wait_ge(x_final, 1)
            sp.dma_start(out, x[:, :]).then_inc(out_sem, 16)
            sp.wait_ge(out_sem, 16)

        @block.gpsimd
        def _(pool):
            def power(n):
                pool.wait_ge(var_ready, n + 1)
                nc.gpsimd.tensor_tensor(out=rstd[:, :], in0=var_eps[:, :], in1=neg_half[:, :],
                                        op=ALU.pow).then_inc(rstd_ready, 1)

            def split_k(l):
                def step(c, par, half):
                    part = [kparts[:, k, bass.ds(c * C, C)] for k in range(3)]
                    pool.wait_ge(k1_ready, NC * l + c + 1)
                    nc.gpsimd.tensor_tensor(out=kr[:, par, :], in0=kf[:, par, :], in1=part[0],
                                            op=ALU.subtract).then_inc(kr_ready, 1)
                    pool.wait_ge(k2_ready, NC * l + c + 1)
                    nc.gpsimd.tensor_tensor(out=part[2], in0=kr[:, par, :], in1=part[1],
                                            op=ALU.subtract).then_inc(k3_ready, 1)
                return step

            power(0)
            over_chunks(pool, split_k(0))
            power(1)
            split_k(1)(0, 0, 0)
            split_k(1)(1, 1, 0)
            power(2)
            power(3)
            over_later_chunks(pool, split_k(1))
            for n in (4, 5):
                power(n)

        @block.scalar
        def _(act):
            def qb1_copy(l):
                act.wait_ge(qrep_ps, l + 1)
                nc.scalar.activation(qb1[:, :], PS[0:NR, 6, :], ACT.Copy).then_inc(qb1_ready, 1)

            def split_k(l):
                def step(c, par, half):
                    act.wait_ge(k_ps, NC * l + c + 1)
                    src = PS[:, 0:2, 0:HC]
                    dst = kf[:, par, :].rearrange("p (h c) -> p h c", h=2)
                    if l:
                        nc.scalar.activation(dst, src, ACT.Identity, bias=con["bk1"]).then_inc(kf_ready, 1)
                    else:
                        nc.scalar.activation(dst, src, ACT.Copy).then_inc(kf_ready, 1)
                    act.wait_ge(kf_ready, NC * l + c + 1)
                    nc.scalar.activation(kparts[:, 0, bass.ds(c * C, C)], kf[:, par, :], ACT.Copy).then_inc(k1_ready, 1)
                    act.wait_ge(kr_ready, NC * l + c + 1)
                    nc.scalar.activation(kparts[:, 1, bass.ds(c * C, C)], kr[:, par, :], ACT.Copy).then_inc(k2_ready, 1)
                return step

            def shift(l):
                act.wait_ge(shift_ps, l + 1)
                nc.scalar.activation(qstack[NR:NS, :, :, :].rearrange("p a b c -> p (a b c)"),
                                     PS[NR:NS, 0:2, :].rearrange("p a b -> p (a b)"),
                                     ACT.Copy).then_inc(shift_ready, 1)

            def exps(l):
                def step(c, par, half):
                    for k in range(CT):
                        t = c * CT + k
                        b = (par + k) % 2
                        act.wait_ge(s_ps, NT * l + t + 1)
                        if not isinstance(t, int) or t >= 2:
                            act.wait_ge(pv_done, NT * l + t - 1)
                        nc.scalar.activation(probs[:, b, :], PS[:, 2 * b:2 * b + 2, :].rearrange("p a b -> p (a b)"),
                                             ACT.Exp, scale=SCALE).then_inc(p_ready, 1)
                over_chunks(act, step)

            def sa_exp(s):
                act.wait_ge(st_ps, s + 1)
                nc.scalar.activation(probs[0:L, 0, :], PS[0:L, 0:2, :].rearrange("p a b -> p (a b)"),
                                     ACT.Exp, scale=SCALE).then_inc(sp_ready, 1)

            split_k(0)(0, 0, 0)
            qb1_copy(0)
            over_chunks(act, split_k(0), first=False)
            shift(0)
            exps(0)
            for par in range(2):
                act.wait_ge(ks_in[par], 16 * len(TERMS) * (ALL[par] + LATER[par]))
            split_k(1)(0, 0, 0)
            split_k(1)(1, 1, 0)
            sa_exp(0)
            for e in range(E0):
                act.wait_ge(hb_ready, e + 1)
                nc.scalar.activation(h0[:, e // 2, e % 2, :, :], h0[:, e // 2, e % 2, :, :],
                                     ACT.Relu).then_inc(h_ready, 1)
            qb1_copy(1)
            over_later_chunks(act, split_k(1))
            shift(1)
            exps(1)
            sa_exp(1)
            act.wait_ge(lg_ready, 1)
            nc.scalar.activation(sc[:, :], lg[:, :], ACT.Exp, bias=sm[:, 0:1], accum_out=sm[:, 1:2]).then_inc(exp_ready, 1)
            for b in range(NE1 // 2):
                act.wait_ge(m_ps, b + 1)
                if b >= 2:
                    act.wait_ge(m_ready, b - 1)
                nc.scalar.activation(act1[:, b % 2], PS[:, b % 4, :].rearrange("p (e w k l) -> p e w k l", e=2, w=2, k=K1)[:, :, 0],
                                     ACT.Silu).then_inc(silu_ready, 1)

        @block.vector
        def _(dve):
            count = [0]

            def link(ins):
                count[0] += 1
                ins.then_inc(dve_step, 1)
                dve.wait_ge(dve_step, count[0])

            def layernorm(n):
                link(nc.vector.bn_stats(out=bn[:, :], in_=x[:, :]))
                link(nc.vector.bn_aggr(out=mu_var[:, :], in_=bn[:, :]))
                nc.vector.tensor_scalar_add(var_eps[:, :], mu_var[:, 1:2], EPS).then_inc(var_ready, 1)
                dve.wait_ge(rstd_ready, n + 1)
                nc.vector.tensor_scalar(xn[:, :], x[:, :], mu_var[:, 0:1], rstd[:, 0:1], ALU.subtract,
                                        ALU.mult).then_inc(xn_ready, 1)
                dve.wait_ge(xnT_ps, n + 1)
                nc.vector.tensor_copy(xnT[:, :], PS[:, 7, 0:L]).then_inc(xnT_ready, 1)

            def queries(l):
                dve.wait_ge(q_ps, l + 1)
                src = PS[0:L, 7, 0:D].rearrange("p (u r) -> p u r", u=NP)
                nc.vector.tensor_copy(q_sb, src[:, :, None, :].to_broadcast([L, NP, len(TERMS), 2 * HD])).then_inc(q_ready, 1)
                dve.wait_ge(qb1_ready, l + 1)
                link(nc.vector.tensor_tensor(out=qr1[:, :], in0=PS[0:NR, 6, :], in1=qb1[:, :], op=ALU.subtract))
                link(nc.vector.tensor_copy(qb2[:, :], qr1[:, :]))
                link(nc.vector.tensor_tensor(out=qr2[:, :], in0=qr1[:, :], in1=qb2[:, :], op=ALU.subtract))
                link(nc.vector.tensor_copy(qb3[:, :], qr2[:, :]))
                qsel = con["qsel"]
                nc.vector.tensor_scalar(qmix[:, 0, :], qb1[:, :], qsel[0:NR, 0:1], None, ALU.mult)
                link(nc.vector.tensor_scalar(qmix[:, 1, :], qb1[:, :], qsel[0:NR, 1:2], None, ALU.mult))
                for part, src in ((1, qb2), (2, qb3)):
                    for hh in range(2):
                        if part == 1:
                            o = qmix[:, hh, :]
                            a, b = src[:, :], qmix[:, hh, :]
                        else:
                            o = qstack[0:NR, :, hh, :]
                            a = src[:, :].rearrange("p (a l) -> p a l", a=NP)
                            b = qmix[:, hh, :].rearrange("p (a l) -> p a l", a=NP)
                        ins = nc.vector.scalar_tensor_tensor(out=o, in0=a, scalar=qsel[0:NR, 2 * part + hh:2 * part + hh + 1],
                                                             in1=b, op0=ALU.mult, op1=ALU.add)
                    if part == 1:
                        link(ins)
                    else:
                        ins.then_inc(qstack_ready, 1)

            def maxima(l):
                def step(c, par, half):
                    if l:
                        dve.wait_ge(mc_in[par], 16 * mask_loads(par, 2, half))
                    for u in range(NP):
                        n = NC * NP * l + NP * c + u
                        dve.wait_ge(a_ps, n + 1)
                        scores = PS[:, 2 + 2 * (u % 2):4 + 2 * (u % 2), 0:HC]
                        if l:
                            dve.wait_ge(a_used, n - 1)
                            nc.vector.tensor_tensor_reduce(
                                out=masked_out[:, u % 2, :].rearrange("p (h c) -> p h c", h=2), in0=scores,
                                in1=mask_c[:, par, :].rearrange("p (h c) -> p h c", h=2), scale=1.0,
                                scalar=run_max[:, 1 - par, u:u + 1], op0=ALU.add, op1=ALU.max,
                                accum_out=run_max[:, par, u:u + 1]).then_inc(a_used, 1)
                        else:
                            nc.vector.tensor_reduce(out=row_max[:, bass.ds(c, 1), u:u + 1].rearrange("p a b -> p (a b)"), in_=scores, axis=AX.XY,
                                                    op=ALU.max).then_inc(a_used, 1)
                if l:
                    written_out(step)
                else:
                    over_chunks(dve, step)

            def shift_parts(l):
                dve.wait_ge(a_used, NC * NP * (l + 1))
                if l:
                    link(nc.vector.tensor_scalar(negm[:, :], run_max[:, 0, :], -1.0, None, ALU.mult))
                else:
                    link(nc.vector.tensor_reduce(out=negm[:, :], in_=row_max[:, :, :].rearrange("p c u -> p u c"),
                                                 axis=AX.X, op=ALU.max, negate=True))
                link(nc.vector.tensor_copy(mpart[:, 0, :], negm[:, :]))
                link(nc.vector.tensor_tensor(out=negm_r1[:, :], in0=negm[:, :], in1=mpart[:, 0, :], op=ALU.subtract))
                link(nc.vector.tensor_copy(mpart[:, 1, :], negm_r1[:, :]))
                link(nc.vector.tensor_tensor(out=mpart[:, 2, :], in0=negm_r1[:, :], in1=mpart[:, 1, :], op=ALU.subtract))
                for part in range(3):
                    nc.vector.tensor_tensor(out=mdiag[:, part], in0=mpart[:, part, :, None].to_broadcast([128, NP, 128]),
                                            in1=identb[:, None, :].to_broadcast([128, NP, 128]),
                                            op=ALU.mult).then_inc(mdiag_ready, 1)

            def values(l):
                def step(c, par, half):
                    if l == 0:
                        at = bass.ds((NC - 1) * C - c * C, C)
                        dve.wait_ge(raw_in[par], 32 * (half + 1))
                        nc.vector.tensor_scalar(mask_add[:, at], mask_raw[:, par, :], 0.0, MASKED,
                                                ALU.is_equal, ALU.mult).then_inc(mask_ready, 1)
                        dve.wait_ge(mask_ready, c + 1)
                        nc.vector.tensor_reduce(out=mask_max[:, bass.ds(c, 1)], in_=mask_add[:, at],
                                                axis=AX.X, op=ALU.max)
                    for k in range(CT):
                        t = c * CT + k
                        b = (par + k) % 2
                        dve.wait_ge(v_ps, NT * l + t + 1)
                        if not isinstance(t, int) or t >= 2:
                            dve.wait_ge(pv_done, NT * l + t - 1)
                        src = PS[:, 5 + b, 0:D].rearrange("p (h d) -> p h d", h=NH)
                        if l:
                            nc.vector.tensor_tensor(out=vaug[:, b, :, 0:HD], in0=src,
                                                    in1=bv_all[:, :].rearrange("p (h d) -> p h d", h=NH),
                                                    op=ALU.add).then_inc(v_ready, 1)
                        else:
                            nc.vector.tensor_copy(vaug[:, b, :, 0:HD], src).then_inc(v_ready, 1)
                over_chunks(dve, step)

            def finish(f, done, n):
                dve.wait_ge(done, n)
                nc.vector.tensor_copy(o_sb[:, :], PS[:, 4, 0:4 * L]).then_inc(osb_ready, 1)
                dve.wait_ge(oT_ps, f + 1)
                base = PS[0:L, 7, 0:1]
                p0 = base.ap[0]

                def view(off, dims):
                    return bass.AP(tensor=base.tensor, offset=base.offset + off, ap=[[p0[0], p0[1]]] + dims)
                nc.vector.reciprocal(rec[:, 0:12].rearrange("p (j a) -> p j a", a=3), view(8, [[32, 4], [137, 3]]))
                link(nc.vector.reciprocal(rec[:, 12:16], view(3 * 128 + 8, [[32, 4]])))
                nc.vector.tensor_tensor(out=ao[:, 0:12 * HD].rearrange("p (j a d) -> p j a d", a=3, d=HD),
                                        in0=view(0, [[32, 4], [137, 3], [1, HD]]),
                                        in1=rec[:, 0:12].rearrange("p (j a) -> p j a", a=3)[:, :, :, None].to_broadcast([L, 4, 3, HD]),
                                        op=ALU.mult)
                nc.vector.tensor_tensor(out=ao[:, 12 * HD:].rearrange("p (j d) -> p j d", d=HD),
                                        in0=view(3 * 128, [[32, 4], [1, HD]]),
                                        in1=rec[:, 12:16, None].to_broadcast([L, 4, HD]), op=ALU.mult).then_inc(ao_ready, 1)

            def add_projected(n):
                dve.wait_ge(aoT_ps, n + 1)
                nc.vector.tensor_copy(aoT[:, :], PS[:, 6, 0:L]).then_inc(aoT_ready, 1)
                dve.wait_ge(proj_ps, n + 1)
                link(nc.vector.tensor_tensor(out=x[:, :], in0=x[:, :], in1=PS[0:L, 7, 0:D], op=ALU.add))

            def self_attention(s):
                dve.wait_ge(qkv_ps, s + 1)
                if s == 0:
                    src = PS[0:L, 0, 0:2 * D].rearrange("p (h d) -> p h d", d=HD)
                    a = rope_a[:, :].rearrange("p (h d) -> p h d", d=HD)
                    b = rope_b[:, :].rearrange("p (h d) -> p h d", d=HD)
                    wide_h = [L, 2 * NH, HD]
                    half_h = [L, 2 * NH, HD // 2]
                    nc.vector.tensor_tensor(out=a, in0=src, in1=con["cos2"][0:L, None, :].to_broadcast(wide_h), op=ALU.mult)
                    nc.vector.tensor_tensor(out=b[:, :, 0::2], in0=src[:, :, 1::2],
                                            in1=con["nsin"][0:L, None, :].to_broadcast(half_h), op=ALU.mult)
                    link(nc.vector.tensor_tensor(out=b[:, :, 1::2], in0=src[:, :, 0::2],
                                                 in1=con["sin"][0:L, None, :].to_broadcast(half_h), op=ALU.mult))
                    nc.vector.tensor_tensor(out=qk[:, :], in0=rope_a[:, :], in1=rope_b[:, :], op=ALU.add)
                else:
                    nc.vector.tensor_copy(qk[:, :], PS[0:L, 0, 0:2 * D])
                nc.vector.tensor_copy(vaug[0:L, 0, :, 0:HD],
                                      PS[0:L, 0, 2 * D:3 * D].rearrange("p (h d) -> p h d", d=HD)).then_inc(qk_ready, 1)
                dve.wait_ge(qkT_ps, s + 1)
                link(nc.vector.tensor_copy(qkT[:, :, :], PS[:, 1, 0:2 * L].rearrange("p (a l) -> p a l", a=2)))
                full = [D, NH, L]
                nc.vector.tensor_tensor(out=kbd[:, :, :], in0=qkT[:, 1, None, :].to_broadcast(full),
                                        in1=con["head"][:, :, None].to_broadcast(full), op=ALU.mult).then_inc(kbd_ready, 1)
                nc.vector.tensor_tensor(out=qbd[:, :, :], in0=qkT[:, 0, None, :].to_broadcast(full),
                                        in1=con["head"][:, :, None].to_broadcast(full), op=ALU.mult).then_inc(qbd_ready, 1)
                dve.wait_ge(srow_ps, s + 1)
                link(nc.vector.tensor_reduce(out=sa_negm[:, :], in_=PS[0:L, 2:4, :].rearrange("p a (h l) -> p (a h) l", l=L),
                                             axis=AX.X, op=ALU.max, negate=True))
                nc.vector.tensor_tensor(out=sa_diag[:, :, :], in0=sa_negm[:, :, None].to_broadcast([L, NH, L]),
                                        in1=ident[0:L, None, 0:L].to_broadcast([L, NH, L]),
                                        op=ALU.mult).then_inc(diag_ready, 1)

            def mlp0():
                dve.wait_ge(g_ps, 1)
                link(nc.vector.tensor_copy(lg[:, 0:E0], PS[0:L, 0, 0:E0]))
                link(nc.vector.max(out=top8[:, :], in_=lg[:, 0:E0]))
                link(nc.vector.max_index(out=top_i[:, :], in_max=top8[:, :], in_values=lg[:, 0:E0]))
                link(nc.vector.tensor_copy(top_f[:, :], top_i[:, :]))
                link(nc.vector.tensor_scalar(hot[:, 0, :], con["iota"][0:L, :], top_f[:, 0:1], None, ALU.is_equal))
                b1 = con["b1"].rearrange("p (e k) -> p e k", e=E0)
                for b in range(E0 // 2):
                    dve.wait_ge(h_ps, b + 1)
                    for e in range(2):
                        nc.vector.tensor_tensor(
                            out=h0[:, b, e, :, :],
                            in0=PS[:, 1 + b, 256 * e:256 * e + 256].rearrange("p (k l) -> p k l", k=K0),
                            in1=b1[:, 2 * b + e, :, None].to_broadcast([128, K0, L]), op=ALU.add).then_inc(hb_ready, 1)
                for e in range(E0):
                    if e % 4 == 0:
                        dve.wait_ge(y_ps, e // 4 + 1)
                    link(nc.vector.scalar_tensor_tensor(out=x[:, :], in0=PS[0:L, 5 + e // 4, D * (e % 4):D * (e % 4 + 1)],
                                                        scalar=hot[:, 0, e:e + 1], in1=x[:, :], op0=ALU.mult, op1=ALU.add))

            def mlp1():
                dve.wait_ge(g_ps, 2)
                nc.vector.tensor_copy(gb1_all[:, :], PS[0:L, 0, E1:2 * E1])
                link(nc.vector.tensor_copy(lg[:, :], PS[0:L, 0, 0:E1]))
                nc.vector.tensor_reduce(out=sm[:, 0:1], in_=lg[:, :], axis=AX.X, op=ALU.max, negate=True).then_inc(lg_ready, 1)
                dve.wait_ge(exp_ready, 1)
                link(nc.vector.reciprocal(sm[:, 2:3], sm[:, 1:2]))
                link(nc.vector.scalar_tensor_tensor(out=sc[:, :], in0=sc[:, :], scalar=sm[:, 2:3], in1=gb1_all[:, :],
                                                    op0=ALU.mult, op1=ALU.add))
                link(nc.vector.max(out=top8[:, :], in_=sc[:, :]))
                link(nc.vector.max_index(out=top_i[:, :], in_max=top8[:, :], in_values=sc[:, :]))
                link(nc.vector.tensor_copy(top_f[:, :], top_i[:, :]))
                nc.vector.tensor_scalar(hot[:, 0, :], con["iota"][0:L, :], top_f[:, 0:1], None, ALU.is_equal)
                link(nc.vector.tensor_scalar(hot[:, 1, :], con["iota"][0:L, :], top_f[:, 1:2], None, ALU.is_equal))
                link(nc.vector.tensor_tensor(out=hot[:, 0, :], in0=hot[:, 0, :], in1=hot[:, 1, :], op=ALU.add))
                link(nc.vector.tensor_tensor(out=wm[:, :], in0=lg[:, :], in1=hot[:, 0, :], op=ALU.mult))
                link(nc.vector.tensor_scalar(hot[:, 1, :], hot[:, 0, :], -NOT_ASSIGNED, NOT_ASSIGNED, ALU.mult, ALU.add))
                nc.vector.tensor_tensor(out=wm[:, :], in0=wm[:, :], in1=hot[:, 1, :], op=ALU.add).then_inc(wm_ready, 1)
                dve.wait_ge(wmT_ps, 1)
                link(nc.vector.tensor_copy(wmT[:, :], PS[0:E1, 6, 0:L]))
                link(nc.vector.max(out=ranks[:, 0, :], in_=wmT[:, :]))
                link(nc.vector.match_replace(out=cut1[:, :], in_to_replace=ranks[:, 0, :], in_values=wmT[:, :],
                                             imm_value=NOT_ASSIGNED))
                link(nc.vector.max(out=ranks[:, 1, :], in_=cut1[:, :]))
                link(nc.vector.memset(ranks[:, 1, CAP - 8:8], NOT_ASSIGNED))
                link(nc.vector.match_replace(out=cut2[:, :], in_to_replace=ranks[:, 1, :], in_values=cut1[:, :],
                                             imm_value=NOT_ASSIGNED))
                link(nc.vector.tensor_tensor(out=cut1[:, :], in0=wmT[:, :], in1=cut2[:, :], op=ALU.not_equal))
                nc.vector.tensor_tensor(out=gT[:, :], in0=wmT[:, :], in1=cut1[:, :], op=ALU.mult).then_inc(gT_ready, 1)
                dve.wait_ge(g1_ps, 1)
                link(nc.vector.tensor_copy(gates[:, :], PS[0:L, 6, 128:128 + E1]))

                def accumulate(e):
                    if e % 4 == 0 or e == E1:
                        dve.wait_ge(z_ps, e // 4 + 1)
                    weight = gates[:, e:e + 1] if e < E1 else 1.0 / NSH
                    ins = nc.vector.scalar_tensor_tensor(out=x[:, :], in0=PS[0:L, 4 + (e // 4) % 2, D * (e % 4):D * (e % 4 + 1)],
                                                         scalar=weight, in1=x[:, :], op0=ALU.mult, op1=ALU.add)
                    if e == E1:
                        ins.then_inc(x_final, 1)
                    else:
                        link(ins)
                    if e % 4 == 3:
                        nc.vector.tensor_copy(sm[:, 3:4], sm[:, 2:3]).then_inc(z_used, 1)

                for b in range(NE1 // 2):
                    dve.wait_ge(silu_ready, b + 1)
                    if b >= 2:
                        dve.wait_ge(z_ps, (b - 2) // 2 + 1) if b % 2 == 1 else None
                    nc.vector.tensor_tensor(out=h1[:, b % 2],
                                            in0=PS[:, b % 4, :].rearrange("p (e w k l) -> p e w k l", e=2, w=2, k=K1)[:, :, 1],
                                            in1=act1[:, b % 2], op=ALU.mult).then_inc(m_ready, 1)
                    if b % 2 == 1 and b >= 3:
                        for e in range(2 * (b - 3), 2 * (b - 3) + 4):
                            accumulate(e)
                for e in range(E1 - 4, E1 + 1):
                    accumulate(e)

            dve.wait_ge(cons_in_sem, 16)
            nc.vector.tensor_copy(identb[:, :], ident)
            nc.vector.tensor_copy(ident8[:, :, :], ident[:, None, 0:L].to_broadcast([128, 8, L]))
            nc.vector.memset(ones[:, :], 1.0)
            nc.vector.memset(zeros[:, :], 0.0)
            nc.vector.memset(neg_half[:, :], -0.5)
            link(nc.vector.memset(shift_pick[:, :, :], 0.0))
            for part in range(3):
                nc.vector.memset(shift_pick[:, part, NR + part:NR + part + 1], 1.0)
            nc.vector.memset(run_max[:, :, :], -3.0e38)
            link(nc.vector.memset(vaug[:, :, :, HD:HD + 1], 1.0))
            nc.vector.tensor_copy(valid_ident[:, :], ident[0:L, 0:L]).then_inc(const_ready, 1)
            dve.wait_ge(x_in_sem, 16)
            layernorm(0)
            queries(0)
            dve.wait_ge(bv_ps, 1)
            nc.vector.tensor_copy(bv_all[:, :], PS[:, 7, D:2 * D]).then_inc(bv_ready, 1)
            nc.vector.memset(kstack[NR:NS, :, :, :].rearrange("p a b c -> p (a b c)").bitcast(U32),
                             0x3F803F80).then_inc(const_ready, 1)
            maxima(0)
            shift_parts(0)
            values(0)
            finish(0, pv_done, NT)
            add_projected(0)
            layernorm(1)
            self_attention(0)
            finish(1, sa_pv, 1)
            dve.wait_ge(ao_ready, 2)
            link(nc.vector.tensor_tensor(out=x[:, :], in0=x[:, :], in1=ao[:, :], op=ALU.add))
            layernorm(2)
            mlp0()
            link(nc.vector.tensor_reduce(out=row_open[:, 0:1], in_=mask_max[0:L, :], axis=AX.X, op=ALU.max))
            link(nc.vector.tensor_scalar(row_open[:, 1:2], row_open[:, 0:1], 0.0, None, ALU.is_equal))
            link(nc.vector.tensor_scalar(valid_ident[:, :], ident[0:L, 0:L], row_open[:, 1:2], None, ALU.mult))
            layernorm(3)
            queries(1)
            maxima(1)
            shift_parts(1)
            values(1)
            finish(2, pv_done, 2 * NT)
            add_projected(1)
            layernorm(4)
            self_attention(1)
            finish(3, sa_pv, 2)
            add_projected(2)
            layernorm(5)
            mlp1()

        @block.tensor
        def _(pe):
            def transposed_norm(n):
                pe.wait_ge(xn_ready, n + 1)
                nc.tensor.transpose(PS[:, 7, 0:L], xn[:, :], ident[0:L, 0:L]).then_inc(xnT_ps, 1)
                pe.wait_ge(xnT_ready, n + 1)

            def with_bias(dst, lhsT, w, bias, signal):
                nc.tensor.matmul(dst, lhsT, w, start=True, stop=False)
                nc.tensor.matmul(dst, ones[0:1, 0:L], bias, start=False, stop=True).then_inc(signal, 1)

            def queries(l):
                if l:
                    with_bias(PS[0:L, 7, 0:D], xnT[:, :], mat["wq1"], row["bq1"], q_ps)
                else:
                    nc.tensor.matmul(PS[0:L, 7, 0:D], xnT[:, :], mat["wq0"], start=True, stop=True).then_inc(q_ps, 1)
                pe.wait_ge(q_ready, l + 1)
                for p in range(NP):
                    ins = nc.tensor.matmul(PS[0:NR, 6, p * L:(p + 1) * L],
                                           q_sb[:, p].rearrange("p t r -> p (t r)"),
                                           valid_ident[:, :], start=True, stop=True)
                ins.then_inc(qrep_ps, 1)

            def project_k(l, c, par, half, piece=0, pieces=1):
                if piece == 0:
                    pe.wait_ge(ctx_in[par], 16 * ctx_loads(par, 2 * l, half))
                    if not known(c, 0) or l:
                        pe.wait_ge(kf_ready, NC * l + c)
                width = C // max(pieces, 2)
                for at in range(C * piece // pieces, C * (piece + 1) // pieces, width):
                    ins = nc.tensor.matmul(PS[:, at // HC, at % HC:at % HC + width], mat[f"wk{l}"],
                                           ctx_c[:, par, at:at + width], start=True, stop=True)
                if piece == pieces - 1:
                    ins.then_inc(k_ps, 1)

            def pass_a(l):
                def step(c, par, half):
                    if known(c, 0):
                        pe.wait_ge(qstack_ready, l + 1)
                    pe.wait_ge(ks_in[par], 16 * len(TERMS) * stack_loads(par, 2 * l, half))
                    for u in range(NP):
                        n = NP * c + u
                        if not isinstance(n, int) or n >= 2:
                            pe.wait_ge(a_used, NC * NP * l + n - 1)
                        for h in range(2):
                            ins = nc.tensor.matmul(PS[:, 2 + 2 * (u % 2) + h, 0:HC],
                                                   qstack[0:NR, u, :, :].rearrange("p a b -> p (a b)"),
                                                   kstack[0:NR, par, u, h * HC:(h + 1) * HC], start=True, stop=True)
                        ins.then_inc(a_ps, 1)
                        if u < PIECES and (not isinstance(c, int) or c + 2 < NC):
                            project_k(l, c + 2, par, half + 1, u, PIECES)
                over_chunks(pe, step)

            def shift(l):
                pe.wait_ge(mdiag_ready, 3 * (l + 1))
                pe.wait_ge(kf_ready, NC * (l + 1))
                for h in range(2):
                    for part in range(3):
                        ins = nc.tensor.matmul(PS[0:NS, h, :], shift_pick[:, part, :],
                                               mdiag[:, part, 4 * h:4 * h + 4, :].rearrange("p a b -> p (a b)"),
                                               start=(part == 0), stop=(part == 2))
                ins.then_inc(shift_ps, 1)

            def clear_sums():
                nc.tensor.matmul(PS[:, 4, 0:4 * L], zeros[:, 0:128], zeros[:, :], start=True, stop=True)

            def pv(weights, moving, rows_):
                for n, (j, wc, mc, oc) in enumerate(PV):
                    k = wc.stop - wc.start
                    ins = nc.tensor.matmul(PS[32 * j:32 * j + k, 4, oc], weights[:, wc], moving[:, mc],
                                           start=False, stop=True, skip_group_check=True)
                return ins

            def pass_b(l):
                def scores(c, par, half, k):
                    t = c * CT + k
                    b = (par + k) % 2
                    late = not isinstance(t, int) or t >= 2
                    if k == 0:
                        pe.wait_ge(ctx_in[par], 16 * ctx_loads(par, 2 * l + 1, half))
                    if late:
                        pe.wait_ge(v_ready, NT * l + t - 1)
                    nc.tensor.matmul(PS[:, 5 + b, 0:D], ctx_c[:, par, k * T:(k + 1) * T], mat[f"wv{l}"],
                                     start=True, stop=True).then_inc(v_ps, 1)
                    if k == 0:
                        pe.wait_ge(ks_in[par], 16 * len(TERMS) * stack_loads(par, 2 * l + 1, half))
                        if l:
                            pe.wait_ge(mc_in[par], 16 * mask_loads(par, 3, half))
                    if late:
                        pe.wait_ge(p_ready, NT * l + t - 1)
                    for h in range(2):
                        if l:
                            nc.tensor.matmul(PS[:, 2 * b + h, :], mask_c[:, par, k * T:(k + 1) * T],
                                             ident8[:, :, :].rearrange("p a b -> p (a b)"), start=True, stop=True)
                        for u in range(4 * h, 4 * h + 4):
                            ins = nc.tensor.matmul(PS[:, 2 * b + h, 128 * (u % 4):128 * (u % 4 + 1)],
                                                   kstack[0:NS, par, u, k * T:(k + 1) * T],
                                                   qstack[0:NS, u, :, :].rearrange("p a b -> p (a b)"),
                                                   start=not l, stop=True, skip_group_check=True)
                    ins.then_inc(s_ps, 1)

                clear_sums()
                pe.wait_ge(shift_ready, l + 1)
                scores(0, 0, 0, 0)

                def step(c, par, half):
                    for k in range(CT):
                        t = c * CT + k
                        b = (par + k) % 2
                        if k + 1 < CT:
                            scores(c, par, half, k + 1)
                        elif not isinstance(t, int) or t + 1 < NT:
                            scores(c + 1, 1 - par, half + par, 0)
                        pe.wait_ge(v_ready, NT * l + t + 1)
                        pe.wait_ge(p_ready, NT * l + t + 1)
                        pv(vaug[:, b, :, :].rearrange("p h d -> p (h d)"), probs[:, b, :], 128).then_inc(pv_done, 1)
                over_chunks(pe, step)

            def finish(f):
                pe.wait_ge(osb_ready, f + 1)
                for a in range(4):
                    ins = nc.tensor.transpose(PS[0:L, 7, a * 128:(a + 1) * 128], o_sb[:, a * L:(a + 1) * L], ident)
                ins.then_inc(oT_ps, 1)
                pe.wait_ge(ao_ready, f + 1)

            def project_out(n, w, bias):
                nc.tensor.transpose(PS[:, 6, 0:L], ao[:, :], ident[0:L, 0:L]).then_inc(aoT_ps, 1)
                pe.wait_ge(aoT_ready, n + 1)
                with_bias(PS[0:L, 7, 0:D], aoT[:, :], w, bias, proj_ps)

            def self_attention(s):
                with_bias(PS[0:L, 0, 0:3 * D], xnT[:, :], mat[f"wqkv{s}"], row[f"bqkv{s}"], qkv_ps)
                pe.wait_ge(qk_ready, s + 1)
                for a in range(2):
                    ins = nc.tensor.transpose(PS[:, 1, a * L:(a + 1) * L], qk[:, a * D:(a + 1) * D], ident[0:L, 0:L])
                ins.then_inc(qkT_ps, 1)
                pe.wait_ge(kbd_ready, s + 1)
                for h in range(2):
                    ins = nc.tensor.matmul(PS[0:L, 2 + h, :], qkT[:, 0, :],
                                           kbd[:, 8 * h:8 * h + 8, :].rearrange("p a b -> p (a b)"), start=True, stop=True)
                ins.then_inc(srow_ps, 1)
                pe.wait_ge(qbd_ready, s + 1)
                for h in range(2):
                    nc.tensor.matmul(PS[0:L, h, :], qkT[:, 1, :],
                                     qbd[:, 8 * h:8 * h + 8, :].rearrange("p a b -> p (a b)"), start=True, stop=False)
                pe.wait_ge(diag_ready, s + 1)
                for h in range(2):
                    ins = nc.tensor.matmul(PS[0:L, h, :], ones[0:L, 0:L],
                                           sa_diag[:, 8 * h:8 * h + 8, :].rearrange("p a b -> p (a b)"), start=False, stop=True)
                ins.then_inc(st_ps, 1)
                clear_sums()
                pe.wait_ge(sp_ready, s + 1)
                pv(vaug[0:L, 0, :, :].rearrange("p h d -> p (h d)"), probs[0:L, 0, :], L).then_inc(sa_pv, 1)

            def mlp0():
                with_bias(PS[0:L, 0, 0:E0], xnT[:, :], mat["gate0"], row["gb0"], g_ps)
                pe.wait_ge(w0_sem, 32)
                for e in range(E0):
                    for k in range(K0):
                        ins = nc.tensor.matmul(PS[:, 1 + e // 2, 256 * (e % 2) + k * L:256 * (e % 2) + (k + 1) * L],
                                               w1[:, e, k * 128:(k + 1) * 128], xnT[:, :], start=True, stop=True)
                    if e % 2:
                        ins.then_inc(h_ps, 1)
                for e in range(E0):
                    pe.wait_ge(h_ready, e + 1)
                    dst = PS[0:L, 5 + e // 4, D * (e % 4):D * (e % 4 + 1)]
                    for k in range(K0):
                        nc.tensor.matmul(dst, h0[:, e // 2, e % 2, k, :], w2[:, e * K0 + k, :], start=(k == 0), stop=False)
                    ins = nc.tensor.matmul(dst, ones[0:1, 0:L], row["b2"][:, e * D:(e + 1) * D], start=False, stop=True)
                    if e % 4 == 3:
                        ins.then_inc(y_ps, 1)

            def mlp1():
                nc.tensor.matmul(PS[0:L, 0, E1:2 * E1], ones[0:1, 0:L], row["gb1"], start=True, stop=True)
                nc.tensor.matmul(PS[0:L, 0, 0:E1], xnT[:, :], mat["gate1"], start=True, stop=True).then_inc(g_ps, 1)
                pe.wait_ge(wm_ready, 1)
                nc.tensor.transpose(PS[0:E1, 6, 0:L], wm[:, :], ident[0:L, 0:L]).then_inc(wmT_ps, 1)
                pe.wait_ge(gT_ready, 1)
                nc.tensor.transpose(PS[0:L, 6, 128:128 + E1], gT[:, :], ident[0:E1, 0:E1]).then_inc(g1_ps, 1)
                pe.wait_ge(w1_sem, 48)

                def up(b):
                    if b >= 4:
                        pe.wait_ge(m_ready, b - 3)
                    for e in range(2):
                        for w, ws in enumerate((w1s, w3s)):
                            for k in range(K1):
                                at = 256 * e + 128 * w + k * L
                                ins = nc.tensor.matmul(PS[:, b % 4, at:at + L], ws[:, 2 * b + e, k * 128:(k + 1) * 128],
                                                       xnT[:, :], start=True, stop=True)
                    ins.then_inc(m_ps, 1)

                def down(b):
                    pe.wait_ge(m_ready, b + 1)
                    for e in (2 * b, 2 * b + 1):
                        y = min(e, E1)
                        if e % 4 == 0 and 8 <= e:
                            pe.wait_ge(z_used, e // 4 - 1)
                        for k in range(K1):
                            ins = nc.tensor.matmul(PS[0:L, 4 + (y // 4) % 2, D * (y % 4):D * (y % 4 + 1)],
                                                   h1[:, b % 2, e % 2, k, :], w2s[:, e * K1 + k, :],
                                                   start=(k == 0 and e <= E1), stop=(k == K1 - 1 and e != E1))
                        if e % 4 == 3 or e == NE1 - 1:
                            ins.then_inc(z_ps, 1)

                up(0)
                for b in range(NE1 // 2):
                    if b + 1 < NE1 // 2:
                        up(b + 1)
                    down(b)

            pe.wait_ge(first_mats_sem, 16)
            project_k(0, 0, 0, 0)
            pe.wait_ge(const_ready, 1)
            transposed_norm(0)
            queries(0)
            project_k(0, 1, 1, 0)
            pe.wait_ge(mats_sem, 32)
            nc.tensor.matmul(PS[:, 7, D:2 * D], ones[0:1, :], row["bv1"], start=True, stop=True).then_inc(bv_ps, 1)
            pe.wait_ge(bv_ready, 1)
            pass_a(0)
            shift(0)
            pe.wait_ge(const_ready, 2)
            pass_b(0)
            project_k(1, 0, 0, 0)
            finish(0)
            project_k(1, 1, 1, 0)
            project_out(0, mat["wo0"], row["bo0"])
            transposed_norm(1)
            pe.wait_ge(kf_ready, NC + 2)
            self_attention(0)
            finish(1)
            transposed_norm(2)
            mlp0()
            transposed_norm(3)
            queries(1)
            pass_a(1)
            shift(1)
            pass_b(1)
            finish(2)
            project_out(1, mat["wo1"], row["bo1"])
            transposed_norm(4)
            self_attention(1)
            finish(3)
            project_out(2, mat["wout1"], row["bout1"])
            transposed_norm(5)
            mlp1()


def constants():
    con = np.zeros((128, CONS["bk1"][0]), np.float32)

    def put(name, a):
        at = CONS[name][0]
        con[:a.shape[0], at:at + a.shape[1]] = a
    put("ident", np.eye(128, dtype=np.float32))
    put("head", (np.arange(D)[:, None] // HD == np.arange(NH)[None, :]).astype(np.float32))
    sel = np.zeros((NR, 6), np.float32)
    for r in range(NR):
        t, hh = r // (2 * HD), (r // HD) % 2
        sel[r, 2 * TERMS[t][1] + hh] = 1
    put("qsel", sel)
    theta = np.float32(10000.0) ** (np.float32(-2.0) * np.arange(HD // 2, dtype=np.float32) / np.float32(HD))
    ang = np.outer(np.arange(L, dtype=np.float32), theta.astype(np.float32)).astype(np.float32)
    put("cos2", np.repeat(np.cos(ang), 2, axis=1))
    put("nsin", -np.sin(ang))
    put("sin", np.sin(ang))
    put("iota", np.tile(np.arange(E1, dtype=np.float32), (L, 1)))
    return con


def kernel(**inputs):
    import concourse.bacc as bacc
    from concourse.bass_utils import run_bass_kernel_spmd

    a = {k: np.asarray(v) for k, v in inputs.items()}

    def by_pair(w):
        return w.reshape(w.shape[0], NP, 2, HD).transpose(0, 2, 3, 1).reshape(w.shape[0], D)

    mats = np.concatenate([
        a["L0_xattn_w_q"].T, by_pair(a["L0_xattn_w_kv"][:D].T), a["L0_xattn_w_kv"][D:].T, a["L0_xattn_w_out"].T,
        a["L0_attn_wq_w"].T, a["L0_attn_wk_w"].T, a["L0_attn_wv_w"].T,
        a["L1_xattn_Wq"], by_pair(a["L1_xattn_Wk"]), a["L1_xattn_Wv"], a["L1_xattn_Wo"],
        a["L1_attn_Wqkv"], a["L1_attn_Wout"], a["L0_ffn_gate_w"].T, a["L1_ffn_gate_w"]], axis=1)
    rows = np.concatenate([
        a["L0_xattn_b_out"], a["L0_attn_wq_b"], a["L0_attn_wk_b"], a["L0_attn_wv_b"], a["L1_xattn_bq"], a["L1_xattn_bv"],
        a["L1_xattn_bo"], a["L1_attn_bqkv"], a["L1_attn_bout"], a["L0_ffn_gate_b"], a["L1_ffn_gate_b"],
        a["L0_ffn_b2"].reshape(-1)])[None, :]
    cons = np.concatenate([constants(), by_pair(a["L1_xattn_bk"][None, :]).T,
                           a["L0_ffn_b1"].reshape(E0 * K0, 128).T], axis=1)
    arrays = {
        "x_in": a["x"][0],
        "ctx_t": a["ctx_1024"][0].T,
        "mask_in": a["mask_Bx1xSxS2_ik1"][0, 0],
        "mats_in": mats,
        "rows_in": rows,
        "cons_in": cons,
        "f0w1": a["L0_ffn_w1"].transpose(2, 0, 1),
        "f0w2": a["L0_ffn_w2"].reshape(E0, D, K0, 128).transpose(3, 0, 2, 1).reshape(128, E0 * K0, D),
        "f1w13": np.stack([np.concatenate([a["L1_ffn_ew1"], a["L1_ffn_sw1"]]).transpose(1, 0, 2),
                           np.concatenate([a["L1_ffn_ew3"], a["L1_ffn_sw3"]]).transpose(1, 0, 2)], axis=1),
        "f1w2": np.concatenate([a["L1_ffn_ew2"], a["L1_ffn_sw2"]]).reshape(NE1, K1, 128, D)
                .transpose(2, 0, 1, 3).reshape(128, NE1 * K1, D),
    }
    arrays = {k: np.ascontiguousarray(v) for k, v in arrays.items()}
    nc = bacc.Bacc("TRN2", target_bir_lowering=False, num_devices=1)
    args = [nc.dram_tensor(k, v.shape, mybir.dt.from_np(v.dtype), kind="ExternalInput").ap() for k, v in arrays.items()]
    args.append(nc.dram_tensor("x_out", (L, D), F32, kind="ExternalOutput").ap())
    perceiver(nc, *args)
    r = run_bass_kernel_spmd(nc, [arrays], core_ids=[0])
    return r.results[0]["x_out"].reshape(1, L, D)
```

```python
from contextlib import ExitStack

import numpy as np

import concourse.bass as bass
from concourse import mybir

F32 = mybir.dt.float32
BF16 = mybir.dt.bfloat16
I32 = mybir.dt.int32
U32 = mybir.dt.uint32
ALU = mybir.AluOpType
ACT = mybir.ActivationFunctionType
AX = mybir.AxisListType

D = 128
L = 64
NH = 16
HD = D // NH
NP = NH // 2
S = 6272
T = 128
CT = 7
C = CT * T
NC = S // C
NT = S // T
NV = NH * (HD + 1)
VHALF = [(0, 4), (4, CT)]
HC = C // 2
KHALF = [(0, 512), (512, C)]
PIECE = 128
SCALE = HD ** -0.5
EPS = 1e-5
TERMS = [(0, 0), (1, 0), (0, 1), (1, 1), (0, 2), (2, 0)]
Q2_ROWS, Q3_ROWS = slice(32, 64), slice(64, 80)
NR = len(TERMS) * 2 * HD
NS = NR + 3
MASKED = -float(2 ** 30)
E0, H0 = 8, 512
K0 = H0 // 128
W0 = E0 * H0 + E0 * K0 * D
E1, H1 = 16, 256
K1 = H1 // 128
UP_BANKS = (0, 1, 2, 7)
NSH = 2
NE1 = E1 + NSH
CAP = 10
NOT_ASSIGNED = -1e30

MATS = {}
_at = 0
for _n, _w in (("wk0", D), ("wv0", D), ("wo0", D), ("wqkv0", 3 * D), ("wk1", D), ("wv1", D),
               ("wo1", D), ("wqkv1", 3 * D), ("wout1", D), ("gate0", E0), ("gate1", E1)):
    MATS[_n] = (_at, _at + _w)
    _at += _w
NMAT = _at
ROWS = {}
_at = 0
for _n, _w in (("bo0", D), ("bqkv0", 3 * D), ("bv1", D), ("bo1", D), ("bqkv1", 3 * D), ("bout1", D),
               ("gb0", E0), ("gb1", E1)):
    ROWS[_n] = (_at, _at + _w)
    _at += _w
NROW = _at
CONS = {}
_at = 0
for _n, _w in (("ident", D), ("fold", L), ("head", NH), ("hsel", 2), ("cos2", HD), ("nsin", HD // 2), ("sin", HD // 2), ("iota", E1),
               ("bk1", 1), ("b2", D), ("bq1", NR)):
    CONS[_n] = (_at, _at + _w)
    _at += _w
NCON = _at
PV = [(j, slice(27 * j, 27 * j + 27), slice(3 * L * j, 3 * L * (j + 1)), slice(0, 3 * L)) for j in range(4)]
PV += [(j, slice(108 + 9 * j, 117 + 9 * j), slice((12 + j) * L, (13 + j) * L), slice(3 * L, 4 * L)) for j in range(4)]


def perceiver(nc, x_in, ctx_t, mask, mask_cols, wq_in, b1_in, mats_in, rows_in, cons_in, f0w12, f1w13, f1w2, out):
    ctx = ExitStack()
    with ctx:
        def sb(name, shape, dt=F32):
            return ctx.enter_context(nc.sbuf_tensor(name, shape, dt))

        def sem(name):
            return ctx.enter_context(nc.semaphore(name))

        mats = sb("mats", [128, NMAT])
        rows = sb("rows", [1, NROW])
        cons = sb("cons", [128, NCON])
        mat = {n: mats[:, a:b] for n, (a, b) in MATS.items()}
        row = {n: rows[0:1, a:b] for n, (a, b) in ROWS.items()}
        con = {n: cons[:, a:b] for n, (a, b) in CONS.items()}
        ident = con["ident"]
        identb = sb("identb", [128, D], BF16)
        ones = sb("ones", [128, D])
        zeros = sb("zeros", [128, 256])
        neg_half = sb("neg_half", [L, 1])
        shift_rows = sb("shift_rows", [3 * NP, 2 * L], BF16)
        w12 = sb("w12", [128, W0])
        w1 = w12[:, 0:E0 * H0].rearrange("p (e h) -> p e h", e=E0)
        w2 = w12[:, E0 * H0:].rearrange("p (e d) -> p e d", d=D)
        w2s = w12[:, 0:NE1 * K1 * D].rearrange("p (e d) -> p e d", d=D)
        x = sb("x", [L, D])
        bn = sb("bn", [L, 6])
        mu_var = sb("mu_var", [L, 2])
        var_eps = sb("var_eps", [L, 1])
        rstd = sb("rstd", [L, 1])
        xn = sb("xn", [L, D])
        xnT = sb("xnT", [D, L])
        ctx_c = sb("ctx_c", [128, 2, C])
        kfr = sb("kfr", [128, 4 * C])
        kf = kfr[:, 0:2 * C].rearrange("p (b c) -> p b c", b=2)
        kr = kfr[:, 2 * C:4 * C].rearrange("p (b c) -> p b c", b=2)
        kparts = sb("kparts", [128, 3, S], BF16)
        kstack = sb("kstack", [128, 2, NP, C], BF16)
        valid_ident = sb("valid_ident", [L, L])
        qb1 = sb("qb1", [NR, NP * L], BF16)
        scratch = sb("scratch", [128, NH * L + NP * L])
        q_rest = scratch[:, 0:NP * L]
        qb2 = sb("qb2", [128, NP * L], BF16)
        wq = sb("wq", [128, NP * NR])
        open_row = sb("open_row", [NP, NP, L])
        qstack = sb("qstack", [128, NP, 2, L], BF16)
        row_max = sb("row_max", [128, NC, NP])
        run_max = sb("run_max", [128, 2, NP])
        negm = sb("negm", [128, NP])
        negm_r1 = sb("negm_r1", [128, NP])
        mpart = sb("mpart", [128, 3, NP], BF16)
        probs = sb("probs", [128, 3, NH * L])
        v_all = w12[:, 0:NT * NV]
        v_c_or_b1 = sb("v_c_or_b1", [128, max(2 * CT * NV, E0 // 2 * H0)])
        v_c = v_c_or_b1[:, 0:2 * CT * NV].rearrange("p (b n) -> p b n", b=2)
        b1 = v_c_or_b1[:, 0:E0 // 2 * H0].rearrange("p (a n) -> p a n", n=H0)
        bv_all = sb("bv_all", [128, D])
        mask_raw = kr[:, :, :].bitcast(I32)
        mask_raw_t = kf[:, :, :].bitcast(I32)
        mask_t = sb("mask_t", [128, NT * L], BF16)
        open_scores = kfr[:, 0:3 * NH * L].rearrange("p (b n) -> p b n", b=3)
        mask_add = sb("mask_add", [128, S], BF16)
        mask_c = sb("mask_c", [128, 2, C], BF16)
        masked_out = sb("masked_out", [128, 2, C], BF16)
        mask_max = sb("mask_max", [128, NC])
        row_open = sb("row_open", [L, 2])
        o_sb = sb("o_sb", [128, 4 * L])
        rec = sb("rec", [L, NH])
        ao = sb("ao", [L, D])
        aoT = sb("aoT", [D, L])
        qk = sb("qk", [L, 2 * D])
        rope_a = sb("rope_a", [L, 2 * D])
        rope_b = sb("rope_b", [L, 2 * D])
        qkT = sb("qkT", [D, 2, L])
        kbd = scratch[:, 0:NH * L].rearrange("p (h l) -> p h l", h=NH)
        sa_negm = sb("sa_negm", [128, NP])
        shifted = scratch[:, NH * L:NH * L + NP * L]
        sa_probs = probs[:, 0, 0:NP * L]
        sa_probsT = probs[:, 1, 0:NP * L]
        vbd = sb("vbd", [128, NP, 2, HD + 1])
        lg = sb("lg", [L, E1])
        top8 = sb("top8", [L, 8])
        top_i = sb("top_i", [L, 8], U32)
        top_f = sb("top_f", [L, 8])
        hot = sb("hot", [L, 2, E1])
        sm = sb("sm", [L, 8])
        sc = sb("sc", [L, E1])
        gb1_all = sb("gb1_all", [L, E1])
        wm = sb("wm", [L, E1])
        wmT = sb("wmT", [E1, L])
        cut1 = sb("cut1", [E1, L])
        cut2 = sb("cut2", [E1, L])
        ranks = sb("ranks", [E1, 2, 8])
        gT = sb("gT", [E1, L])
        big = kparts[:, :, :].rearrange("p a b -> p (a b)").bitcast(F32)
        w13s = big[:, 0:2 * NE1 * H1].rearrange("p (e h) -> p e h", e=NE1)
        flat = probs[:, :, :].rearrange("p a b -> p (a b)")
        raw0 = flat[:, 0:2 * H0].rearrange("p (b n) -> p b n", b=2)
        h0 = flat[:, 2 * H0:4 * H0].rearrange("p (b n) -> p b n", b=2)
        act1 = flat[:, 0:2 * H1].rearrange("p (b n) -> p b n", b=2)
        h1 = flat[:, 2 * H1:4 * H1].rearrange("p (b n) -> p b n", b=2)
        h1T = flat[:, 4 * H1:6 * H1].rearrange("p (b n) -> p b n", b=2)
        chosenT = sb("chosenT", [E0, L])
        pair_gates = sb("pair_gates", [128, NE1 // 2])
        pair_sum = sb("pair_sum", [128, D])

        PS = ctx.enter_context(nc.psum_tensor("PS", [128, 8, 512], F32))

        x_in_sem = sem("x_loaded")
        cons_in_sem = sem("cons_loaded")
        first_mats_sem = sem("first_mats_loaded")
        mats_sem = sem("mats_loaded")
        wq_sem = sem("wq_loaded")
        w0_sem = sem("mlp0_loaded")
        b1_sem = sem("b1_loaded")
        w1_sem, w2_sem = sem("mlp1_in_loaded"), sem("mlp1_out_loaded")
        ctx_in = [sem("ctx_in_even"), sem("ctx_in_odd")]
        ks_in = [sem("kstack_in_even"), sem("kstack_in_odd")]
        raw_in = [sem("mask_raw_in_even"), sem("mask_raw_in_odd")]
        mc_in = [sem("mask_in_even"), sem("mask_in_odd")]
        v_in = [sem("v_in_even"), sem("v_in_odd")]
        v_ones_ready = sem("v_ones_ready")
        out_sem = sem("out_stored")
        const_ready = sem("const_ready")
        dve_step = sem("dve_step")
        var_ready, rstd_ready, xn_ready = sem("var_ready"), sem("rstd_ready"), sem("xn_ready")
        xnT_ps, xnT_ready = sem("xnT_ps"), sem("xnT_ready")
        qrep_ps, qb1_ready, qstack_ready, open_known, open_ps, open_row_ready = (sem(n) for n in
            ("qrep_ps", "qb1_ready", "qstack_ready", "open_known", "open_ps", "open_row_ready"))
        k_ps, kf_ready, k1_ready, kr_ready, k2_ready, k3_ready = (sem(n) for n in
            ("k_ps", "kf_ready", "k1_ready", "kr_ready", "k2_ready", "k3_ready"))
        a_ps, a_used = sem("a_ps"), sem("a_used")
        mpart_ready, shift_ps, shift_rows_ready, shift_in = (sem(n) for n in
            ("mpart_ready", "shift_ps", "shift_rows_ready", "shift_in"))
        v_ps, v_ready, s_ps, p_ready, pv_done = (sem(n) for n in ("v_ps", "v_ready", "s_ps", "p_ready", "pv_done"))
        bv_ps, bv_ready, ao_biased = sem("bv_ps"), sem("bv_ready"), sem("ao_biased")
        mask_ready, open_ready = sem("mask_ready"), sem("open_ready")
        osb_ready, oT_ps, ao_ready, aoT_ps, aoT_ready, proj_ps = (sem(n) for n in
            ("osb_ready", "oT_ps", "ao_ready", "aoT_ps", "aoT_ready", "proj_ps"))
        qk_ps, sv_ps, qk_ready, vbd_ready, qkT_ps, kbd_ready = (sem(n) for n in
            ("qk_ps", "sv_ps", "qk_ready", "vbd_ready", "qkT_ps", "kbd_ready"))
        ss_ps, shifted_ready, sp_ready, spT_ps, spT_ready, sa_pv = (sem(n) for n in
            ("self_scores_ps", "shifted_ready", "sp_ready", "spT_ps", "spT_ready", "sa_pv"))
        g_ps, chosen_ready, chosenT_ps, chosenT_ready, pair_ps, sum_ready, sum_ps = (sem(n) for n in
            ("gate_ps", "chosen_ready", "chosenT_ps", "chosenT_ready", "pair_gates_ps", "pair_sum_ready", "sum_ps"))
        h_ps, raw0_ready, hT_ps, h_ready, y_ps, y_used = (sem(n) for n in
            ("h_ps", "raw0_ready", "hT_ps", "h_ready", "y_ps", "y_used"))
        lg_ready, exp_ready, wm_ready, wmT_ps, gT_ready = (sem(n) for n in
            ("lg_ready", "exp_ready", "wm_ready", "wmT_ps", "gT_ready"))
        m_ps, silu_ready, m_ready, mT_ps, mT_ready, z_ps = (sem(n) for n in
            ("m_ps", "silu_ready", "m_ready", "mT_ps", "mT_ready", "z_ps"))
        x_final = sem("x_final")

        ALL, LATER = ((NC + 1) // 2, NC // 2), ((NC - 1) // 2, NC // 2 - 1)

        def ctx_loads(par, ph, half):
            return (ph // 2) * ALL[par] + half + 1

        def stack_loads(par, ph, half):
            before = (0, ALL[par], ALL[par] + LATER[par], 2 * ALL[par] + LATER[par])[ph]
            return before + half + (1 if ph % 2 == 0 else 0)

        def over_chunks(eng, step):
            step(0, 0, 0)
            with eng.Fori(0, (NC - 3) // 2) as i:
                step(2 * i + 1, 1, i)
                step(2 * i + 2, 0, i + 1)
            step(NC - 2, 1, NC // 2 - 1)
            step(NC - 1, 0, NC // 2)

        def over_later_chunks(eng, step):
            with eng.Fori(1, NC // 2) as i:
                step(2 * i, 0, i)
                step(2 * i + 1, 1, i)
            step(NC - 1, 0, NC // 2)

        def written_out(step):
            for c in range(NC):
                step(c, c % 2, c // 2)

        def known(c, value):
            return isinstance(c, int) and c == value

        def ring(par, k):
            return (CT * par + k) % 3

        def ring_age(par, k):
            return next(n for n in range(1, 2 * CT) if (CT * par + k - n) % (2 * CT) % 3 == ring(par, k))

        def v_bank(l, c):
            return 4 if known(c, 0) else 2 if known(c, 1) and l else 6

        def score_banks(n):
            return (slice(0, 2), slice(2, 4), slice(5, 7))[n]

        def once(eng, value):
            return value if isinstance(value, int) else eng.snap(value)

        block = ctx.enter_context(nc.Block())

        @block.sync
        def _(sp):
            sp.dma_start(x[:, :], x_in).then_inc(x_in_sem, 16)
            sp.dma_start(cons[:, :], cons_in).then_inc(cons_in_sem, 16)
            sp.dma_start(mats[:, 0:2 * D], mats_in[:, 0:2 * D]).then_inc(first_mats_sem, 16)

            def load_ctx(at, par):
                sp.dma_start(ctx_c[:, par, :], ctx_t[:, bass.ds(at, C)]).then_inc(ctx_in[par], 16)

            load_ctx(0, 0)
            sp.dma_start(wq[:, :], wq_in[0]).then_inc(wq_sem, 16)
            load_ctx(C, 1)
            sp.dma_start(mats[:, 2 * D:], mats_in[:, 2 * D:]).then_inc(mats_sem, 16)
            sp.dma_start(rows[:, :], rows_in).then_inc(mats_sem, 16)

            def restack(at, par, parts=(0, 1, 2)):
                for t, (kp, _) in enumerate(TERMS):
                    if kp in parts:
                        sp.dma_start(kstack[2 * HD * t:2 * HD * (t + 1), par, :, :],
                                     kparts[:, kp, bass.ds(at, C)]).then_inc(ks_in[par], 16)

            def load_mask(at, par):
                sp.dma_start(mask_c[:, par, :], mask_add[:, bass.ds(at, C)]).then_inc(mc_in[par], 16)

            def load_v(at, par):
                sp.dma_start(v_c[:, par, :], v_all[:, bass.ds(at, CT * NV)]).then_inc(v_in[par], 16)

            def settled():
                sp.wait_ge(cons_in_sem, 16)

            def load_raw(at, at_t, par):
                for half in range(2):
                    sp.dma_start(mask_raw[L * half:L * (half + 1), par, :],
                                 mask[:, bass.ds(at, C)]).then_inc(raw_in[par], 16)
                sp.dma_start(mask_raw_t[:, par, 0:CT * L], mask_cols[:, bass.ds(at_t, CT * L)]).then_inc(raw_in[par], 16)

            for l in range(2):
                def chunk_a(c, par, half):
                    at = once(sp, c * C)
                    ahead = once(sp, (c + 2) * C)
                    split = once(sp, 2 * c + (2 * NC * l + 2))
                    scored = once(sp, NP * c + (NC * NP * l - NP + 1 - l))
                    settled()
                    sp.wait_ge(k1_ready, split)
                    if known(c, 0):
                        if l:
                            sp.wait_ge(s_ps, NT)
                    else:
                        sp.wait_ge(a_ps, scored)
                    restack(at, par, (0,))
                    if l:
                        settled()
                        if known(c, 0):
                            sp.wait_ge(mask_ready, NC)
                        else:
                            sp.wait_ge(a_used, scored)
                        load_mask(at, par)
                    settled()
                    sp.wait_ge(k2_ready, split)
                    restack(at, par, (1,))
                    settled()
                    sp.wait_ge(k3_ready, split)
                    restack(at, par, (2,))
                    if not isinstance(c, int) or c + 2 < NC:
                        settled()
                        sp.wait_ge(k_ps, split)
                        sp.wait_ge(v_ps, split)
                        load_ctx(ahead, par)

                over_chunks(sp, chunk_a)
                sp.wait_ge(v_ready, 2 * NC * (l + 1))
                sp.wait_ge(v_ones_ready, l + 1)
                load_v((NC - 1) * CT * NV, 0)
                load_v((NC - 2) * CT * NV, 1)
                if l == 0:
                    load_raw((NC - 1) * C, 0, 0)
                    load_raw((NC - 2) * C, CT * L, 1)
                    sp.wait_ge(qrep_ps, 1)
                    sp.dma_start(wq[:, :], wq_in[1]).then_inc(wq_sem, 16)
                    sp.wait_ge(k_ps, 2 * NC)
                    sp.wait_ge(v_ps, 2 * NC)
                    load_ctx(0, 0)
                    load_ctx(C, 1)
                sp.wait_ge(shift_rows_ready, l + 1)
                sp.dma_start(qstack[NR:NS, :, :, :].rearrange("p u a l -> p u (a l)"),
                             shift_rows[:, :]).then_inc(shift_in, 16)

                def chunk_b(c, par, half):
                    at = once(sp, c * -C + (NC - 1) * C)
                    at_t = once(sp, c * (CT * L))
                    tiles = once(sp, CT * c + (NT * l - CT))
                    at_v = once(sp, c * -(CT * NV) + (NC - 1) * CT * NV)
                    settled()
                    sp.wait_ge(s_ps, tiles)
                    restack(at, par)
                    if l == 0:
                        load_raw(at, at_t, par)
                    settled()
                    sp.wait_ge(pv_done, tiles)
                    load_v(at_v, par)

                over_later_chunks(sp, chunk_b)
                for par in range(2):
                    sp.wait_ge(v_in[par], 16 * ALL[par] * (l + 1))
                if l == 0:
                    sp.dma_start(w12[:, :], f0w12).then_inc(w0_sem, 16)
                    sp.wait_ge(pv_done, NT)
                    sp.dma_start(v_c_or_b1[:, 0:E0 // 2 * H0], b1_in).then_inc(b1_sem, 16)
                else:
                    sp.dma_start(w2s, f1w2).then_inc(w2_sem, 16)
            for par in range(2):
                sp.wait_ge(ks_in[par], 16 * len(TERMS) * 2 * (ALL[par] + LATER[par]))
            sp.dma_start(w13s, f1w13).then_inc(w1_sem, 16)
            sp.wait_ge(x_final, 1)
            sp.dma_start(out, x[:, :]).then_inc(out_sem, 16)
            sp.wait_ge(out_sem, 16)

        @block.gpsimd
        def _(pool):
            def power(n):
                pool.wait_ge(var_ready, n + 1)
                nc.gpsimd.tensor_tensor(out=rstd[:, :], in0=var_eps[:, :], in1=neg_half[:, :],
                                        op=ALU.pow).then_inc(rstd_ready, 1)

            def split_k(l):
                def step(c, par, half):
                    done = 2 * c + 2 * NC * l + 1
                    for h, (a, b) in enumerate(KHALF):
                        pool.wait_ge(k1_ready, done + h)
                        nc.gpsimd.tensor_tensor(out=kr[:, par, a:b], in0=kf[:, par, a:b], in1=kparts[:, 0, bass.ds(c * C + a, b - a)],
                                                op=ALU.subtract).then_inc(kr_ready, 1)
                    for h, (a, b) in enumerate(KHALF):
                        pool.wait_ge(k2_ready, done + h)
                        nc.gpsimd.tensor_tensor(out=kparts[:, 2, bass.ds(c * C + a, b - a)], in0=kr[:, par, a:b],
                                                in1=kparts[:, 1, bass.ds(c * C + a, b - a)],
                                                op=ALU.subtract).then_inc(k3_ready, 1)
                return step

            def v_ones(l):
                if l:
                    pool.wait_ge(y_ps, E0 // 2)
                nc.gpsimd.memset(v_all.rearrange("p (n d) -> p n d", d=HD + 1)[:, :, HD:HD + 1], 1.0).then_inc(v_ones_ready, 1)
                pool.wait_ge(v_ones_ready, l + 1)

            v_ones(0)
            power(0)
            over_chunks(pool, split_k(0))
            pool.wait_ge(k3_ready, 2 * NC)
            nc.gpsimd.memset(kstack[NR:NS, :, :, :].rearrange("p a b c -> p (a b c)").bitcast(U32),
                             0x3F803F80).then_inc(const_ready, 1)
            pool.wait_ge(const_ready, 2)
            power(1)
            split_k(1)(0, 0, 0)
            power(2)
            split_k(1)(1, 1, 0)
            power(3)
            v_ones(1)
            over_later_chunks(pool, split_k(1))
            for n in (4, 5):
                power(n)

        @block.scalar
        def _(act):
            def qb1_copy(l):
                act.wait_ge(qrep_ps, l + 1)
                nc.scalar.activation(qb1[:, :], PS[0:NR, 6, :], ACT.Copy).then_inc(qb1_ready, 1)

            def take_v(l, c, h):
                a, b = VHALF[h]
                act.wait_ge(v_ps, 2 * c + 2 * NC * l + 1 + h)
                nc.scalar.activation(
                    v_all[:, bass.ds(c * (CT * NV) + a * NV, (b - a) * NV)].rearrange("p (n d) -> p n d", d=HD + 1)[:, :, 0:HD],
                    PS[:, v_bank(l, c) + h, 0:(b - a) * D].rearrange("p (n d) -> p n d", d=HD),
                    ACT.Copy).then_inc(v_ready, 1)

            def split_k(l, c, par, vc=None):
                done = 2 * c + 2 * NC * l + 1
                for h, (a, b) in enumerate(KHALF):
                    act.wait_ge(k_ps, done + h)
                    if l:
                        nc.scalar.activation(kf[:, par, a:b], PS[:, h, 0:b - a], ACT.Identity,
                                             bias=con["bk1"]).then_inc(kf_ready, 1)
                    else:
                        nc.scalar.activation(kf[:, par, a:b], PS[:, h, 0:b - a], ACT.Copy).then_inc(kf_ready, 1)
                    act.wait_ge(kf_ready, done + h)
                    nc.scalar.activation(kparts[:, 0, bass.ds(c * C + a, b - a)], kf[:, par, a:b],
                                         ACT.Copy).then_inc(k1_ready, 1)
                    if vc is not None and h == 0:
                        take_v(l, vc, 0)
                for h, (a, b) in enumerate(KHALF):
                    if vc is not None and h == 1:
                        take_v(l, vc, 1)
                    act.wait_ge(kr_ready, done + h)
                    nc.scalar.activation(kparts[:, 1, bass.ds(c * C + a, b - a)], kr[:, par, a:b],
                                         ACT.Copy).then_inc(k2_ready, 1)

            def pass_a(l):
                def step(c, par, half):
                    if known(c, 0) and l == 0:
                        take_v(l, 1, 0)
                        take_v(l, 1, 1)
                    if not isinstance(c, int) or c + 2 < NC:
                        split_k(l, c + 2, par, c + 2)
                over_chunks(act, step)

            def exps(l):
                def step(c, par, half):
                    for k in range(CT):
                        t = c * CT + k
                        b = ring(par, k)
                        if l:
                            act.wait_ge(open_ready, t + 1)
                            src = open_scores[:, b]
                        else:
                            act.wait_ge(s_ps, t + 1)
                            src = PS[:, score_banks(b), :].rearrange("p a b -> p (a b)")
                        if not isinstance(t, int) or t >= ring_age(par, k):
                            act.wait_ge(pv_done, NT * l + t + 1 - ring_age(par, k))
                        nc.scalar.activation(probs[:, b, :], src,
                                             ACT.Exp, scale=SCALE).then_inc(p_ready, 1)
                over_chunks(act, step)

            def sa_exp(s):
                for v in range(2):
                    act.wait_ge(shifted_ready, 2 * s + v + 1)
                    nc.scalar.activation(sa_probs[:, 4 * L * v:4 * L * (v + 1)], shifted[:, 4 * L * v:4 * L * (v + 1)],
                                         ACT.Exp, scale=SCALE).then_inc(sp_ready, 1)

            split_k(0, 0, 0)
            qb1_copy(0)
            split_k(0, 1, 1, 0)
            pass_a(0)
            exps(0)
            for par in range(2):
                act.wait_ge(ks_in[par], 16 * len(TERMS) * (ALL[par] + LATER[par]))
            split_k(1, 0, 0)
            sa_exp(0)
            split_k(1, 1, 1)
            for p in range(E0 // 2):
                act.wait_ge(hT_ps, p + 1)
                if p >= 2:
                    act.wait_ge(y_ps, p - 1)
                nc.scalar.activation(h0[:, p % 2], PS[:, 3 + p % 2, :], ACT.Relu).then_inc(h_ready, 1)
            take_v(1, 0, 0)
            take_v(1, 0, 1)
            qb1_copy(1)
            take_v(1, 1, 0)
            take_v(1, 1, 1)
            pass_a(1)
            exps(1)
            sa_exp(1)
            act.wait_ge(lg_ready, 1)
            nc.scalar.activation(sc[:, :], lg[:, :], ACT.Exp, bias=sm[:, 0:1], accum_out=sm[:, 1:2]).then_inc(exp_ready, 1)
            for p in range(NE1 // 2):
                act.wait_ge(m_ps, p + 1)
                if p >= 2:
                    act.wait_ge(m_ready, p - 1)
                nc.scalar.activation(act1[:, p % 2], PS[:, UP_BANKS[p % 4], 0:H1], ACT.Silu).then_inc(silu_ready, 1)

        @block.vector
        def _(dve):
            count = [0]

            def link(ins):
                count[0] += 1
                ins.then_inc(dve_step, 1)
                dve.wait_ge(dve_step, count[0])

            def layernorm(n):
                link(nc.vector.bn_stats(out=bn[:, :], in_=x[:, :]))
                link(nc.vector.bn_aggr(out=mu_var[:, :], in_=bn[:, :]))
                nc.vector.tensor_scalar_add(var_eps[:, :], mu_var[:, 1:2], EPS).then_inc(var_ready, 1)
                dve.wait_ge(rstd_ready, n + 1)
                nc.vector.tensor_scalar(xn[:, :], x[:, :], mu_var[:, 0:1], rstd[:, 0:1], ALU.subtract,
                                        ALU.mult).then_inc(xn_ready, 1)
                dve.wait_ge(xnT_ps, n + 1)
                nc.vector.tensor_copy(xnT[:, :], PS[:, 7, 0:L]).then_inc(xnT_ready, 1)

            def queries(l):
                dve.wait_ge(qb1_ready, l + 1)
                nc.vector.tensor_tensor(out=q_rest[Q3_ROWS], in0=PS[Q3_ROWS, 6, :], in1=qb1[Q3_ROWS, :],
                                        op=ALU.subtract).then_inc(dve_step, 1)
                count[0] += 1
                nc.vector.tensor_tensor(out=qb1[Q2_ROWS, :], in0=PS[Q2_ROWS, 6, :], in1=qb1[Q2_ROWS, :],
                                        op=ALU.subtract).then_inc(dve_step, 1)
                dve.wait_ge(dve_step, count[0])
                count[0] += 1
                link(nc.vector.tensor_copy(qb2[Q3_ROWS, :], q_rest[Q3_ROWS]))
                link(nc.vector.tensor_tensor(out=qb1[Q3_ROWS, :], in0=q_rest[Q3_ROWS], in1=qb2[Q3_ROWS, :],
                                             op=ALU.subtract))
                for hh in range(2):
                    nc.vector.tensor_scalar(qstack[0:NR, :, hh, :], qb1[:, :].rearrange("p (a l) -> p a l", a=NP),
                                            con["hsel"][0:NR, hh:hh + 1], None, ALU.mult).then_inc(qstack_ready, 1)

            def open_latents():
                link(nc.vector.tensor_reduce(out=row_open[:, 0:1], in_=mask_max[0:L, :], axis=AX.X, op=ALU.max))
                link(nc.vector.tensor_scalar(row_open[:, 1:2], row_open[:, 0:1], 0.0, None, ALU.is_equal))
                nc.vector.tensor_scalar(valid_ident[:, :], ident[0:L, 0:L], row_open[:, 1:2], None,
                                        ALU.mult).then_inc(open_known, 1)

            def open_rows():
                dve.wait_ge(open_ps, 1)
                nc.vector.tensor_tensor(out=open_row[:, :, :], in0=PS[0:NP, 7, None, 0:L].to_broadcast([NP, NP, L]),
                                        in1=ident[0:NP, 0:NP, None].to_broadcast([NP, NP, L]),
                                        op=ALU.mult).then_inc(open_row_ready, 1)

            def maxima(l):
                def step(c, par, half):
                    if l:
                        dve.wait_ge(mc_in[par], 16 * (half + 1))
                    for u in range(NP):
                        n = NC * NP * l + NP * c + u
                        dve.wait_ge(a_ps, n + 1)
                        scores = PS[:, 2 + 2 * (u % 2):4 + 2 * (u % 2), 0:HC]
                        if l:
                            dve.wait_ge(a_used, n - 1)
                            nc.vector.tensor_tensor_reduce(
                                out=masked_out[:, u % 2, :].rearrange("p (h c) -> p h c", h=2), in0=scores,
                                in1=mask_c[:, par, :].rearrange("p (h c) -> p h c", h=2), scale=1.0,
                                scalar=run_max[:, 1 - par, u:u + 1], op0=ALU.add, op1=ALU.max,
                                accum_out=run_max[:, par, u:u + 1]).then_inc(a_used, 1)
                        else:
                            nc.vector.tensor_reduce(out=row_max[:, bass.ds(c, 1), u:u + 1].rearrange("p a b -> p (a b)"), in_=scores, axis=AX.XY,
                                                    op=ALU.max).then_inc(a_used, 1)
                if l:
                    written_out(step)
                else:
                    over_chunks(dve, step)

            def shift_parts(l):
                dve.wait_ge(a_used, NC * NP * (l + 1))
                if l:
                    link(nc.vector.tensor_scalar(negm[:, :], run_max[:, 0, :], -1.0, None, ALU.mult))
                else:
                    link(nc.vector.tensor_reduce(out=negm[:, :], in_=row_max[:, :, :].rearrange("p c u -> p u c"),
                                                 axis=AX.X, op=ALU.max, negate=True))
                link(nc.vector.tensor_copy(mpart[:, 0, :], negm[:, :]))
                link(nc.vector.tensor_tensor(out=negm_r1[:, :], in0=negm[:, :], in1=mpart[:, 0, :], op=ALU.subtract))
                link(nc.vector.tensor_copy(mpart[:, 1, :], negm_r1[:, :]))
                nc.vector.tensor_tensor(out=mpart[:, 2, :], in0=negm_r1[:, :], in1=mpart[:, 1, :],
                                        op=ALU.subtract).then_inc(mpart_ready, 1)
                dve.wait_ge(shift_ps, l + 1)
                nc.vector.tensor_copy(shift_rows[:, :], PS[0:3 * NP, 7, 0:2 * L]).then_inc(shift_rows_ready, 1)

            def mask_tile(c, k):
                return mask_t[:, bass.ds((c * CT + k) * L, L)][:, None, :]

            def values(l):
                def step(c, par, half):
                    for k in range(CT):
                        t = c * CT + k
                        b = ring(par, k)
                        if l:
                            if t >= ring_age(par, k):
                                dve.wait_ge(p_ready, NT + t + 1 - ring_age(par, k))
                            dve.wait_ge(s_ps, NT + t + 1)
                            nc.vector.tensor_tensor(
                                out=open_scores[:, b].rearrange("p (h l) -> p h l", l=L),
                                in0=PS[:, score_banks(b), :].rearrange("p a (h l) -> p (a h) l", l=L),
                                in1=mask_tile(c, k).to_broadcast([128, NH, L]),
                                op=ALU.add).then_inc(open_ready, 1)
                        else:
                            if k == 2:
                                dve.wait_ge(raw_in[par], 48 * (half + 1))
                                nc.vector.tensor_scalar(mask_add[:, bass.ds((NC - 1) * C - c * C, C)], mask_raw[:, par, :],
                                                        0.0, MASKED, ALU.is_equal, ALU.mult)
                                nc.vector.tensor_scalar(mask_t[:, bass.ds(c * CT * L, CT * L)], mask_raw_t[:, par, 0:CT * L],
                                                        0.0, MASKED, ALU.is_equal, ALU.mult).then_inc(mask_ready, 1)
                            if k == 4:
                                dve.wait_ge(mask_ready, c + 1)
                                nc.vector.tensor_reduce(out=mask_max[:, bass.ds(c, 1)],
                                                        in_=mask_add[:, bass.ds((NC - 1) * C - c * C, C)],
                                                        axis=AX.X, op=ALU.max)
                written_out(step) if l else over_chunks(dve, step)

            def finish(f, done, n):
                dve.wait_ge(done, n)
                nc.vector.tensor_copy(o_sb[:, :], PS[:, 4, 0:4 * L]).then_inc(osb_ready, 1)
                dve.wait_ge(oT_ps, f + 1)
                base = PS[0:L, 7, 0:1]
                p0 = base.ap[0]

                def view(off, dims):
                    return bass.AP(tensor=base.tensor, offset=base.offset + off, ap=[[p0[0], p0[1]]] + dims)
                nc.vector.reciprocal(rec[:, 0:12].rearrange("p (j a) -> p j a", a=3), view(8, [[32, 4], [137, 3]]))
                link(nc.vector.reciprocal(rec[:, 12:16], view(3 * 128 + 8, [[32, 4]])))
                nc.vector.tensor_tensor(out=ao[:, 0:12 * HD].rearrange("p (j a d) -> p j a d", a=3, d=HD),
                                        in0=view(0, [[32, 4], [137, 3], [1, HD]]),
                                        in1=rec[:, 0:12].rearrange("p (j a) -> p j a", a=3)[:, :, :, None].to_broadcast([L, 4, 3, HD]),
                                        op=ALU.mult)
                nc.vector.tensor_tensor(out=ao[:, 12 * HD:].rearrange("p (j d) -> p j d", d=HD),
                                        in0=view(3 * 128, [[32, 4], [1, HD]]),
                                        in1=rec[:, 12:16, None].to_broadcast([L, 4, HD]), op=ALU.mult).then_inc(ao_ready, 1)

            def add_projected(n):
                dve.wait_ge(aoT_ps, n + 1)
                nc.vector.tensor_copy(aoT[:, :], PS[:, 6, 0:L]).then_inc(aoT_ready, 1)
                dve.wait_ge(proj_ps, n + 1)
                link(nc.vector.tensor_tensor(out=x[:, :], in0=x[:, :], in1=PS[0:L, 7, 0:D], op=ALU.add))

            def self_attention(s):
                dve.wait_ge(qk_ps, s + 1)
                if s == 0:
                    src = PS[0:L, 0, 0:2 * D].rearrange("p (h d) -> p h d", d=HD)
                    a = rope_a[:, :].rearrange("p (h d) -> p h d", d=HD)
                    b = rope_b[:, :].rearrange("p (h d) -> p h d", d=HD)
                    wide_h = [L, 2 * NH, HD]
                    half_h = [L, 2 * NH, HD // 2]
                    nc.vector.tensor_tensor(out=a, in0=src, in1=con["cos2"][0:L, None, :].to_broadcast(wide_h), op=ALU.mult)
                    nc.vector.tensor_tensor(out=b[:, :, 0::2], in0=src[:, :, 1::2],
                                            in1=con["nsin"][0:L, None, :].to_broadcast(half_h), op=ALU.mult)
                    link(nc.vector.tensor_tensor(out=b[:, :, 1::2], in0=src[:, :, 0::2],
                                                 in1=con["sin"][0:L, None, :].to_broadcast(half_h), op=ALU.mult))
                    nc.vector.tensor_tensor(out=qk[:, :], in0=rope_a[:, :], in1=rope_b[:, :], op=ALU.add).then_inc(qk_ready, 1)
                else:
                    nc.vector.tensor_copy(qk[:, :], PS[0:L, 0, 0:2 * D]).then_inc(qk_ready, 1)
                dve.wait_ge(sv_ps, s + 1)
                for j in range(2):
                    ins = nc.vector.tensor_copy(vbd[L * j:L * (j + 1), :, j, 0:HD],
                                                PS[L * j:L * (j + 1), 1, 0:D].rearrange("p (u j d) -> p u j d", u=NP, j=2)[:, :, j])
                ins.then_inc(vbd_ready, 1)
                dve.wait_ge(qkT_ps, s + 1)
                link(nc.vector.tensor_copy(qkT[:, :, :], PS[:, 2, 0:2 * L].rearrange("p (a l) -> p a l", a=2)))
                half = [D, NP, L]
                for a in range(2):
                    nc.vector.tensor_tensor(out=kbd[:, NP * a:NP * (a + 1), :], in0=qkT[:, 1, None, :].to_broadcast(half),
                                            in1=con["head"][:, NP * a:NP * (a + 1), None].to_broadcast(half),
                                            op=ALU.mult).then_inc(kbd_ready, 1)
                dve.wait_ge(ss_ps, s + 1)
                scores = PS[:, 3, :].rearrange("p (h l) -> p h l", l=L)
                link(nc.vector.tensor_reduce(out=sa_negm[:, :], in_=scores, axis=AX.X, op=ALU.max, negate=True))
                for v in range(2):
                    nc.vector.tensor_tensor(out=shifted[:, 4 * L * v:4 * L * (v + 1)].rearrange("p (h l) -> p h l", l=L),
                                            in0=scores[:, 4 * v:4 * v + 4], in1=sa_negm[:, 4 * v:4 * v + 4, None].to_broadcast([128, 4, L]),
                                            op=ALU.add).then_inc(shifted_ready, 1)
                if s == 0:
                    open_latents()
                for v in range(2):
                    dve.wait_ge(spT_ps, 2 * s + v + 1)
                    nc.vector.tensor_copy(sa_probsT[:, 4 * L * v:4 * L * (v + 1)], PS[:, 5 + v, 0:4 * L]).then_inc(spT_ready, 1)
                if s == 0:
                    open_rows()
                dve.wait_ge(sa_pv, s + 1)
                o = PS[0:L, 4, 0:NH * (HD + 1)].rearrange("p (h d) -> p h d", h=NH)
                link(nc.vector.reciprocal(rec[:, :], o[:, :, HD]))
                nc.vector.tensor_tensor(out=ao[:, :].rearrange("p (h d) -> p h d", h=NH), in0=o[:, :, 0:HD],
                                        in1=rec[:, :, None].to_broadcast([L, NH, HD]), op=ALU.mult).then_inc(ao_ready, 1)

            def mlp0():
                dve.wait_ge(g_ps, 1)
                link(nc.vector.tensor_copy(lg[:, 0:E0], PS[0:L, 0, 0:E0]))
                link(nc.vector.max(out=top8[:, :], in_=lg[:, 0:E0]))
                link(nc.vector.max_index(out=top_i[:, :], in_max=top8[:, :], in_values=lg[:, 0:E0]))
                link(nc.vector.tensor_copy(top_f[:, :], top_i[:, :]))
                nc.vector.tensor_scalar(hot[:, 0, :], con["iota"][0:L, :], top_f[:, 0:1], None,
                                        ALU.is_equal).then_inc(chosen_ready, 1)

                def add_bias(p):
                    dve.wait_ge(h_ps, p + 1)
                    if p >= 2:
                        dve.wait_ge(hT_ps, p - 1)
                    nc.vector.tensor_tensor(out=raw0[:, p % 2], in0=PS[:, 1 + p % 2, :], in1=b1[:, p, :],
                                            op=ALU.add).then_inc(raw0_ready, 1)

                def take(p):
                    dve.wait_ge(y_ps, p + 1)
                    y = PS[:, 5 + 2 * (p % 2), D * (p // 2):D * (p // 2 + 1)]
                    if p == 0:
                        ins = nc.vector.tensor_scalar(pair_sum[:, :], y, pair_gates[:, 0:1], None, ALU.mult)
                    else:
                        ins = nc.vector.scalar_tensor_tensor(out=pair_sum[:, :], in0=y, scalar=pair_gates[:, p:p + 1],
                                                             in1=pair_sum[:, :], op0=ALU.mult, op1=ALU.add)
                    ins.then_inc(y_used, 1)
                    dve.wait_ge(y_used, p + 1)

                dve.wait_ge(b1_sem, 16)
                add_bias(0)
                dve.wait_ge(chosenT_ps, 1)
                nc.vector.tensor_copy(chosenT[:, :], PS[0:E0, 0, 128:128 + L]).then_inc(chosenT_ready, 1)
                add_bias(1)
                dve.wait_ge(pair_ps, 1)
                link(nc.vector.tensor_copy(pair_gates[:, 0:E0 // 2], PS[:, 0, 256:256 + E0 // 2]))
                for p in range(E0 // 2):
                    if p + 2 < E0 // 2:
                        add_bias(p + 2)
                    take(p)
                add_folded(1)

            def add_folded(n):
                dve.wait_ge(sum_ps, n)
                link(nc.vector.tensor_tensor(out=x[:, :], in0=x[:, :], in1=PS[0:L, 0, 0:D], op=ALU.add))

            def mlp1():
                dve.wait_ge(g_ps, 2)
                nc.vector.tensor_copy(gb1_all[:, :], PS[0:L, 6, 256 + E1:256 + 2 * E1])
                link(nc.vector.tensor_copy(lg[:, :], PS[0:L, 6, 256:256 + E1]))
                nc.vector.tensor_reduce(out=sm[:, 0:1], in_=lg[:, :], axis=AX.X, op=ALU.max, negate=True).then_inc(lg_ready, 1)
                dve.wait_ge(exp_ready, 1)
                link(nc.vector.reciprocal(sm[:, 2:3], sm[:, 1:2]))
                link(nc.vector.scalar_tensor_tensor(out=sc[:, :], in0=sc[:, :], scalar=sm[:, 2:3], in1=gb1_all[:, :],
                                                    op0=ALU.mult, op1=ALU.add))
                link(nc.vector.max(out=top8[:, :], in_=sc[:, :]))
                link(nc.vector.max_index(out=top_i[:, :], in_max=top8[:, :], in_values=sc[:, :]))
                link(nc.vector.tensor_copy(top_f[:, :], top_i[:, :]))
                nc.vector.tensor_scalar(hot[:, 0, :], con["iota"][0:L, :], top_f[:, 0:1], None, ALU.is_equal)
                link(nc.vector.tensor_scalar(hot[:, 1, :], con["iota"][0:L, :], top_f[:, 1:2], None, ALU.is_equal))
                link(nc.vector.tensor_tensor(out=hot[:, 0, :], in0=hot[:, 0, :], in1=hot[:, 1, :], op=ALU.add))
                link(nc.vector.tensor_tensor(out=wm[:, :], in0=lg[:, :], in1=hot[:, 0, :], op=ALU.mult))
                link(nc.vector.tensor_scalar(hot[:, 1, :], hot[:, 0, :], -NOT_ASSIGNED, NOT_ASSIGNED, ALU.mult, ALU.add))
                nc.vector.tensor_tensor(out=wm[:, :], in0=wm[:, :], in1=hot[:, 1, :], op=ALU.add).then_inc(wm_ready, 1)
                dve.wait_ge(wmT_ps, 1)
                link(nc.vector.tensor_copy(wmT[:, :], PS[0:E1, 6, 0:L]))
                link(nc.vector.max(out=ranks[:, 0, :], in_=wmT[:, :]))
                link(nc.vector.match_replace(out=cut1[:, :], in_to_replace=ranks[:, 0, :], in_values=wmT[:, :],
                                             imm_value=NOT_ASSIGNED))
                link(nc.vector.max(out=ranks[:, 1, :], in_=cut1[:, :]))
                link(nc.vector.memset(ranks[:, 1, CAP - 8:8], NOT_ASSIGNED))
                link(nc.vector.match_replace(out=cut2[:, :], in_to_replace=ranks[:, 1, :], in_values=cut1[:, :],
                                             imm_value=NOT_ASSIGNED))
                link(nc.vector.tensor_tensor(out=cut1[:, :], in0=wmT[:, :], in1=cut2[:, :], op=ALU.not_equal))
                nc.vector.tensor_tensor(out=gT[:, :], in0=wmT[:, :], in1=cut1[:, :], op=ALU.mult).then_inc(gT_ready, 1)
                dve.wait_ge(pair_ps, 2)
                nc.vector.memset(pair_gates[:, E1 // 2:], 1.0 / NSH)
                link(nc.vector.tensor_copy(pair_gates[:, 0:E1 // 2], PS[:, 6, 384:384 + E1 // 2]))

                def gated(p):
                    dve.wait_ge(silu_ready, p + 1)
                    if p >= 2:
                        dve.wait_ge(mT_ps, p - 1)
                    nc.vector.scalar_tensor_tensor(out=h1[:, p % 2], in0=PS[:, UP_BANKS[p % 4], H1:2 * H1],
                                                   scalar=pair_gates[:, p:p + 1], in1=act1[:, p % 2],
                                                   op0=ALU.mult, op1=ALU.mult).then_inc(m_ready, 1)

                gated(0)
                for p in range(NE1 // 2):
                    if p + 1 < NE1 // 2:
                        gated(p + 1)
                    dve.wait_ge(mT_ps, p + 1)
                    if p >= 2:
                        dve.wait_ge(z_ps, p - 1)
                    nc.vector.tensor_copy(h1T[:, p % 2], PS[:, 3 + p % 2, 0:H1]).then_inc(mT_ready, 1)
                dve.wait_ge(z_ps, NE1 // 2)
                nc.vector.tensor_copy(pair_sum[:, :], PS[:, 5, 0:D]).then_inc(sum_ready, 1)
                dve.wait_ge(sum_ps, 2)
                nc.vector.tensor_tensor(out=x[:, :], in0=x[:, :], in1=PS[0:L, 0, 0:D], op=ALU.add).then_inc(x_final, 1)

            dve.wait_ge(cons_in_sem, 16)
            nc.vector.tensor_copy(identb[:, :], ident)
            nc.vector.memset(ones[:, :], 1.0)
            nc.vector.memset(zeros[:, :], 0.0)
            nc.vector.memset(run_max[:, :, :], -3.0e38)
            link(nc.vector.memset(vbd[:, :, :, :], 0.0))
            for j in range(2):
                nc.vector.memset(vbd[L * j:L * (j + 1), :, j, HD:HD + 1], 1.0)
            nc.vector.memset(neg_half[:, :], -0.5).then_inc(const_ready, 1)
            dve.wait_ge(x_in_sem, 16)
            layernorm(0)
            queries(0)
            dve.wait_ge(bv_ps, 1)
            nc.vector.tensor_copy(bv_all[:, :], PS[:, 7, D:2 * D]).then_inc(bv_ready, 1)
            maxima(0)
            shift_parts(0)
            values(0)
            finish(0, pv_done, NT)
            add_projected(0)
            layernorm(1)
            self_attention(0)
            dve.wait_ge(ao_ready, 2)
            link(nc.vector.tensor_tensor(out=x[:, :], in0=x[:, :], in1=ao[:, :], op=ALU.add))
            layernorm(2)
            mlp0()
            layernorm(3)
            queries(1)
            maxima(1)
            shift_parts(1)
            values(1)
            finish(1, pv_done, 2 * NT)
            dve.wait_ge(ao_ready, 3)
            nc.vector.tensor_tensor(out=ao[:, :], in0=ao[:, :], in1=bv_all[0:L, :], op=ALU.add).then_inc(ao_biased, 1)
            add_projected(1)
            layernorm(4)
            self_attention(1)
            add_projected(2)
            layernorm(5)
            mlp1()

        @block.tensor
        def _(pe):
            def transposed_norm(n, before=None):
                pe.wait_ge(xn_ready, n + 1)
                if n == 3:
                    nc.tensor.matmul(PS[:, 7, 0:L], xn[:, :], valid_ident[:, :], start=True, stop=True).then_inc(xnT_ps, 1)
                else:
                    nc.tensor.transpose(PS[:, 7, 0:L], xn[:, :], ident[0:L, 0:L]).then_inc(xnT_ps, 1)
                if before is not None:
                    before()
                pe.wait_ge(xnT_ready, n + 1)

            def bias_first(dst, bias):
                nc.tensor.matmul(dst, ones[0:1, 0:L], bias, start=True, stop=False, skip_group_check=True)

            def add_product(dst, lhsT, w):
                return nc.tensor.matmul(dst, lhsT, w, start=False, stop=True, skip_group_check=True)

            def query_bias():
                pe.wait_ge(open_row_ready, 1)
                nc.tensor.matmul(PS[0:NR, 6, :], con["bq1"][0:NP, :], open_row[:, :, :].rearrange("p u l -> p (u l)"),
                                 start=True, stop=False, skip_group_check=True)

            def queries(l):
                pe.wait_ge(wq_sem, 16 * (l + 1))
                for u in range(NP):
                    ins = nc.tensor.matmul(PS[0:NR, 6, u * L:(u + 1) * L], wq[:, u * NR:(u + 1) * NR], xnT[:, :],
                                           start=not l, stop=True, skip_group_check=True)
                ins.then_inc(qrep_ps, 1)

            def open_latents():
                pe.wait_ge(open_known, 1)
                nc.tensor.matmul(PS[0:NP, 7, 0:L], ones[0:L, 0:NP], valid_ident[:, :], start=True, stop=True).then_inc(open_ps, 1)

            def project_k(l, c, par, half, at=0, width=512):
                if at == 0:
                    pe.wait_ge(ctx_in[par], 16 * ctx_loads(par, 2 * l, half))
                    if not known(c, 0) or l:
                        pe.wait_ge(kf_ready, 2 * (NC * l + c))
                last = C if width == 512 else min(at + width, C)
                for a in range(at, last, width):
                    b = min(a + width, C)
                    ins = nc.tensor.matmul(PS[:, a // 512, a % 512:a % 512 + b - a], mat[f"wk{l}"],
                                           ctx_c[:, par, a:b], start=True, stop=True)
                    if b in (512, C):
                        ins.then_inc(k_ps, 1)

            def project_v(l, c, par, k):
                h = 0 if k < VHALF[0][1] else 1
                bank = v_bank(l, c) + h
                if bank >= 6:
                    if k == VHALF[h][0] and not known(c, 1):
                        pe.wait_ge(v_ready, 2 * c + 2 * NC * l - 1 + h)
                at = D * (k - VHALF[h][0])
                ins = nc.tensor.matmul(PS[:, bank, at:at + D], ctx_c[:, par, k * T:(k + 1) * T], mat[f"wv{l}"],
                                       start=True, stop=True)
                if k == VHALF[h][1] - 1:
                    ins.then_inc(v_ps, 1)

            def first_v(l, c):
                for k in range(CT):
                    project_v(l, c, c, k)

            def pass_a(l):
                def step(c, par, half):
                    if known(c, 0):
                        pe.wait_ge(qstack_ready, 2 * (l + 1))
                    pe.wait_ge(ks_in[par], 16 * len(TERMS) * stack_loads(par, 2 * l, half))
                    for u in range(NP):
                        n = NP * c + u
                        if not isinstance(n, int) or n >= 2:
                            pe.wait_ge(a_used, NC * NP * l + n - 1)
                        if known(c, 0) and u == 1 - l:
                            pe.wait_ge(v_ready, 2 * NC * l + 2 * (l + 1))
                        for h in range(2):
                            ins = nc.tensor.matmul(PS[:, 2 + 2 * (u % 2) + h, 0:HC],
                                                   qstack[0:NR, u, :, :].rearrange("p a b -> p (a b)"),
                                                   kstack[0:NR, par, u, h * HC:(h + 1) * HC], start=True, stop=True)
                        ins.then_inc(a_ps, 1)
                        if u >= 1 and (not isinstance(c, int) or c + 2 < NC):
                            project_k(l, c + 2, par, half + 1, (u - 1) * PIECE, PIECE)
                        if known(c, 0) and l == 0:
                            for k in (2 * (u % 4), 2 * (u % 4) + 1):
                                if k < CT:
                                    project_v(l, 1 + u // 4, 1 - u // 4, k)
                        elif u >= 1 and (not isinstance(c, int) or c + 2 < NC):
                            project_v(l, c + 2, par, u - 1)
                over_chunks(pe, step)

            def shift(l):
                pe.wait_ge(v_ready, 2 * NC * (l + 1))
                pe.wait_ge(mpart_ready, l + 1)
                nc.tensor.matmul(PS[0:3 * NP, 7, 0:2 * L], mpart[:, :, :].rearrange("p k u -> p (k u)"), identb[:, :],
                                 start=True, stop=True).then_inc(shift_ps, 1)

            def clear_sums():
                nc.tensor.matmul(PS[:, 4, 0:4 * L], zeros[:, 0:128], zeros[:, :], start=True, stop=True)

            def pv(weights, moving):
                for n, (j, wc, mc, oc) in enumerate(PV):
                    k = wc.stop - wc.start
                    ins = nc.tensor.matmul(PS[32 * j:32 * j + k, 4, oc], weights[:, wc], moving[:, mc],
                                           start=False, stop=True, skip_group_check=True)
                return ins

            def pass_b(l):
                def scores(c, par, half, k):
                    t = c * CT + k
                    banks = score_banks(ring(par, k))
                    age = ring_age(par, k)
                    if k == 0:
                        pe.wait_ge(ks_in[par], 16 * len(TERMS) * stack_loads(par, 2 * l + 1, half))
                    if not isinstance(t, int) or t >= age:
                        if l:
                            pe.wait_ge(open_ready, t + 1 - age)
                        else:
                            pe.wait_ge(p_ready, t + 1 - age)
                    if l == 0 and k == CT - 1:
                        pe.wait_ge(mask_ready, c + 1)
                    if known(c, 0) and k == 0:
                        pe.wait_ge(shift_in, 16 * (l + 1))
                    for h in range(2):
                        for u in range(4 * h, 4 * h + 4):
                            ins = nc.tensor.matmul(PS[:, banks.start + h, 128 * (u % 4):128 * (u % 4 + 1)],
                                                   kstack[0:NS, par, u, k * T:(k + 1) * T],
                                                   qstack[0:NS, u, :, :].rearrange("p a b -> p (a b)"),
                                                   start=True, stop=True)
                    ins.then_inc(s_ps, 1)

                clear_sums()
                ahead = 3 if l else 2
                for k in range(ahead):
                    scores(0, 0, 0, k)

                def step(c, par, half):
                    for k in range(CT):
                        t = c * CT + k
                        if k + ahead < CT:
                            scores(c, par, half, k + ahead)
                        elif not isinstance(t, int) or t + ahead < NT:
                            scores(c + 1, 1 - par, half + par, k + ahead - CT)
                        if k == 0:
                            pe.wait_ge(v_in[par], 16 * (l * ALL[par] + half + 1))
                        pe.wait_ge(p_ready, NT * l + t + 1)
                        pv(v_c[:, par, k * NV:(k + 1) * NV], probs[:, ring(par, k), :]).then_inc(pv_done, 1)
                over_chunks(pe, step)

            def finish(f):
                pe.wait_ge(osb_ready, f + 1)
                for a in range(4):
                    ins = nc.tensor.transpose(PS[0:L, 7, a * 128:(a + 1) * 128], o_sb[:, a * L:(a + 1) * L], ident)
                ins.then_inc(oT_ps, 1)
                pe.wait_ge(ao_ready, 2 * f + 1)

            def project_out(n, w, bias):
                nc.tensor.transpose(PS[:, 6, 0:L], ao[:, :], ident[0:L, 0:L]).then_inc(aoT_ps, 1)
                bias_first(PS[0:L, 7, 0:D], bias)
                pe.wait_ge(aoT_ready, n + 1)
                add_product(PS[0:L, 7, 0:D], aoT[:, :], w).then_inc(proj_ps, 1)

            def self_bias(s):
                if s == 0:
                    pe.wait_ge(kf_ready, 2 * (NC + 1))
                bias = row[f"bqkv{s}"]
                bias_first(PS[0:L, 0, 0:2 * D], bias[:, 0:2 * D])
                for j in range(2):
                    bias_first(PS[L * j:L * (j + 1), 1, 0:D], bias[:, 2 * D:3 * D])

            def self_attention(s):
                w = mat[f"wqkv{s}"]
                add_product(PS[0:L, 0, 0:2 * D], xnT[:, :], w[:, 0:2 * D]).then_inc(qk_ps, 1)
                for j in range(2):
                    ins = add_product(PS[L * j:L * (j + 1), 1, 0:D], xnT[:, :], w[:, 2 * D:3 * D])
                ins.then_inc(sv_ps, 1)
                pe.wait_ge(qk_ready, s + 1)
                for a in range(2):
                    ins = nc.tensor.transpose(PS[:, 2, a * L:(a + 1) * L], qk[:, a * D:(a + 1) * D], ident[0:L, 0:L])
                ins.then_inc(qkT_ps, 1)
                for a in range(2):
                    pe.wait_ge(kbd_ready, 2 * s + a + 1)
                    ins = nc.tensor.matmul(PS[L * a:L * (a + 1), 3, :], qkT[:, 0, :],
                                           kbd[:, NP * a:NP * (a + 1), :].rearrange("p h l -> p (h l)"), start=True, stop=True)
                ins.then_inc(ss_ps, 1)
                if s == 0:
                    pe.wait_ge(vbd_ready, 1)
                    for at in range(0, 512, PIECE):
                        project_k(1, 1, 1, 0, at, PIECE)
                for v in range(2):
                    pe.wait_ge(sp_ready, 2 * s + v + 1)
                    for b in range(2):
                        at = 128 * (2 * v + b)
                        ins = nc.tensor.transpose(PS[:, 5 + v, 128 * b:128 * (b + 1)], sa_probs[:, at:at + 128], ident)
                    ins.then_inc(spT_ps, 1)
                if s == 0:
                    open_latents()
                pe.wait_ge(vbd_ready, s + 1)
                for v in range(4):
                    if v % 2 == 0:
                        pe.wait_ge(spT_ready, 2 * s + v // 2 + 1)
                    for a in range(2):
                        u = 4 * a + v
                        ins = nc.tensor.matmul(PS[0:L, 4, 2 * (HD + 1) * u:2 * (HD + 1) * (u + 1)],
                                               sa_probsT[:, 128 * v + L * a:128 * v + L * (a + 1)],
                                               vbd[:, u, :, :].rearrange("p j d -> p (j d)"), start=True, stop=True)
                ins.then_inc(sa_pv, 1)
                if s == 0:
                    for at in range(512, C, PIECE):
                        project_k(1, 1, 1, 0, at, PIECE)
                pe.wait_ge(ao_ready, 2 * s + 2)

            def gate_bias():
                pe.wait_ge(kf_ready, 2 * (NC + 2))
                bias_first(PS[0:L, 0, 0:E0], row["gb0"])

            def mlp0():
                add_product(PS[0:L, 0, 0:E0], xnT[:, :], mat["gate0"]).then_inc(g_ps, 1)
                pe.wait_ge(w0_sem, 16)
                def up(p):
                    if p >= 2:
                        pe.wait_ge(raw0_ready, p - 1)
                    for j in range(2):
                        ins = nc.tensor.matmul(PS[L * j:L * (j + 1), 1 + p % 2, :], xnT[:, :], w1[:, 2 * p + j, :],
                                               start=True, stop=True)
                    ins.then_inc(h_ps, 1)

                def turn(p):
                    pe.wait_ge(raw0_ready, p + 1)
                    if p >= 2:
                        pe.wait_ge(h_ready, p - 1)
                    for k in range(K0):
                        ins = nc.tensor.transpose(PS[:, 3 + p % 2, k * 128:(k + 1) * 128],
                                                  raw0[:, p % 2, k * 128:(k + 1) * 128], ident)
                    ins.then_inc(hT_ps, 1)

                def down(p):
                    pe.wait_ge(h_ready, p + 1)
                    if p >= 2:
                        pe.wait_ge(y_used, p - 1)
                    for k in range(K0):
                        for j in range(2):
                            ins = nc.tensor.matmul(PS[L * j:L * (j + 1), 5 + 2 * (p % 2), D * (p // 2):D * (p // 2 + 1)],
                                                   h0[:, p % 2, k * 128 + j * L:k * 128 + (j + 1) * L],
                                                   w2[:, (2 * p + j) * K0 + k, :], start=(k == 0), stop=(k == K0 - 1),
                                                   skip_group_check=True)
                    ins.then_inc(y_ps, 1)

                up(0)
                pe.wait_ge(chosen_ready, 1)
                nc.tensor.transpose(PS[0:E0, 0, 128:128 + L], hot[:, 0, 0:E0], ident[0:L, 0:L]).then_inc(chosenT_ps, 1)
                up(1)
                turn(0)
                pe.wait_ge(chosenT_ready, 1)
                pair_factors(chosenT[:, :], E0, PS[:, 0, 256:256 + E0 // 2])
                for p in range(E0 // 2):
                    if p + 2 < E0 // 2:
                        up(p + 2)
                    if p + 1 < E0 // 2:
                        turn(p + 1)
                    down(p)
                nc.tensor.matmul(PS[0:L, 0, 0:D], chosenT[:, :], con["b2"][0:E0, :], start=True, stop=False)
                pe.wait_ge(y_used, E0 // 2)
                nc.tensor.matmul(PS[0:L, 0, 0:D], con["fold"], pair_sum[:, :], start=False, stop=True).then_inc(sum_ps, 1)

            def pair_factors(gT_, n, dst):
                for j in range(2):
                    ins = nc.tensor.matmul(dst[L * j:L * (j + 1)], gT_, ident[0:n, j:n:2], start=True, stop=True)
                ins.then_inc(pair_ps, 1)

            def mlp1():
                nc.tensor.matmul(PS[0:L, 6, 256 + E1:256 + 2 * E1], ones[0:1, 0:L], row["gb1"], start=True, stop=True)
                nc.tensor.matmul(PS[0:L, 6, 256:256 + E1], xnT[:, :], mat["gate1"], start=True, stop=True).then_inc(g_ps, 1)
                pe.wait_ge(w1_sem, 16)

                def up(p):
                    if p >= 4:
                        pe.wait_ge(m_ready, p - 3)
                    for j in range(2):
                        ins = nc.tensor.matmul(PS[L * j:L * (j + 1), UP_BANKS[p % 4], :], xnT[:, :], w13s[:, 2 * p + j, :],
                                               start=True, stop=True)
                    ins.then_inc(m_ps, 1)

                def turn(p):
                    pe.wait_ge(m_ready, p + 1)
                    if p >= 2:
                        pe.wait_ge(mT_ready, p - 1)
                    for k in range(K1):
                        ins = nc.tensor.transpose(PS[:, 3 + p % 2, k * 128:(k + 1) * 128],
                                                  h1[:, p % 2, k * 128:(k + 1) * 128], ident)
                    ins.then_inc(mT_ps, 1)

                def down(p):
                    pe.wait_ge(mT_ready, p + 1)
                    for k in range(K1):
                        for j in range(2):
                            ins = nc.tensor.matmul(PS[L * j:L * (j + 1), 5, 0:D],
                                                   h1T[:, p % 2, k * 128 + j * L:k * 128 + (j + 1) * L],
                                                   w2s[:, (2 * p + j) * K1 + k, :], start=(p == 0 and k == 0),
                                                   stop=(p == NE1 // 2 - 1 and k == K1 - 1), skip_group_check=True)
                    ins.then_inc(z_ps, 1)

                up(0)
                up(1)
                pe.wait_ge(wm_ready, 1)
                nc.tensor.transpose(PS[0:E1, 6, 0:L], wm[:, :], ident[0:L, 0:L]).then_inc(wmT_ps, 1)
                up(2)
                up(3)
                pe.wait_ge(gT_ready, 1)
                pair_factors(gT[:, :], E1, PS[:, 6, 384:384 + E1 // 2])
                pe.wait_ge(w2_sem, 16)
                for p in range(NE1 // 2):
                    turn(p)
                    if p + 4 < NE1 // 2:
                        up(p + 4)
                    if p >= 1:
                        down(p - 1)
                down(NE1 // 2 - 1)
                pe.wait_ge(sum_ready, 1)
                nc.tensor.matmul(PS[0:L, 0, 0:D], con["fold"], pair_sum[:, :], start=True, stop=True).then_inc(sum_ps, 1)

            pe.wait_ge(first_mats_sem, 16)
            project_k(0, 0, 0, 0)
            pe.wait_ge(const_ready, 1)
            transposed_norm(0)
            queries(0)
            first_v(0, 0)
            project_k(0, 1, 1, 0)
            pe.wait_ge(mats_sem, 32)
            nc.tensor.matmul(PS[:, 7, D:2 * D], ones[0:1, :], row["bv1"], start=True, stop=True).then_inc(bv_ps, 1)
            pe.wait_ge(bv_ready, 1)
            pass_a(0)
            shift(0)
            pe.wait_ge(const_ready, 2)
            pass_b(0)
            project_k(1, 0, 0, 0)
            finish(0)
            project_out(0, mat["wo0"], row["bo0"])
            transposed_norm(1, lambda: self_bias(0))
            self_attention(0)
            query_bias()
            transposed_norm(2, gate_bias)
            mlp0()
            first_v(1, 0)
            transposed_norm(3)
            queries(1)
            first_v(1, 1)
            pass_a(1)
            shift(1)
            pass_b(1)
            finish(1)
            pe.wait_ge(ao_biased, 1)
            project_out(1, mat["wo1"], row["bo1"])
            transposed_norm(4, lambda: self_bias(1))
            self_attention(1)
            project_out(2, mat["wout1"], row["bout1"])
            transposed_norm(5)
            mlp1()


def constants():
    con = np.zeros((128, CONS["bk1"][0]), np.float32)

    def put(name, a):
        at = CONS[name][0]
        con[:a.shape[0], at:at + a.shape[1]] = a
    put("ident", np.eye(128, dtype=np.float32))
    put("fold", np.tile(np.eye(L, dtype=np.float32), (2, 1)))
    put("head", (np.arange(D)[:, None] // HD == np.arange(NH)[None, :]).astype(np.float32))
    put("hsel", (np.arange(NR)[:, None] // HD % 2 == np.arange(2)[None, :]).astype(np.float32))
    theta = np.float32(10000.0) ** (np.float32(-2.0) * np.arange(HD // 2, dtype=np.float32) / np.float32(HD))
    ang = np.outer(np.arange(L, dtype=np.float32), theta.astype(np.float32)).astype(np.float32)
    put("cos2", np.repeat(np.cos(ang), 2, axis=1))
    put("nsin", -np.sin(ang))
    put("sin", np.sin(ang))
    put("iota", np.tile(np.arange(E1, dtype=np.float32), (L, 1)))
    return con


def kernel(**inputs):
    import concourse.bacc as bacc
    from concourse.bass_utils import run_bass_kernel_spmd

    a = {k: np.asarray(v) for k, v in inputs.items()}

    def by_pair(w):
        return w.reshape(w.shape[0], NP, 2, HD).transpose(0, 2, 3, 1).reshape(w.shape[0], D)

    def stacked(w):
        return np.tile(w.reshape(w.shape[0], NP, 1, 2 * HD), (1, 1, len(TERMS), 1)).reshape(w.shape[0], NP * NR)

    mats = np.concatenate([
        by_pair(a["L0_xattn_w_kv"][:D].T), a["L0_xattn_w_kv"][D:].T, a["L0_xattn_w_out"].T,
        a["L0_attn_wq_w"].T, a["L0_attn_wk_w"].T, a["L0_attn_wv_w"].T,
        by_pair(a["L1_xattn_Wk"]), a["L1_xattn_Wv"], a["L1_xattn_Wo"],
        a["L1_attn_Wqkv"], a["L1_attn_Wout"], a["L0_ffn_gate_w"].T, a["L1_ffn_gate_w"]], axis=1)
    rows = np.concatenate([
        a["L0_xattn_b_out"], a["L0_attn_wq_b"], a["L0_attn_wk_b"], a["L0_attn_wv_b"], a["L1_xattn_bv"],
        a["L1_xattn_bo"], a["L1_attn_bqkv"], a["L1_attn_bout"], a["L0_ffn_gate_b"], a["L1_ffn_gate_b"]])[None, :]
    cons = np.concatenate([constants(), by_pair(a["L1_xattn_bk"][None, :]).T,
                           np.concatenate([a["L0_ffn_b2"], np.zeros((128 - E0, D), np.float32)]),
                           np.concatenate([stacked(a["L1_xattn_bq"][None]).reshape(NP, NR),
                                           np.zeros((128 - NP, NR), np.float32)])], axis=1)
    arrays = {
        "x_in": a["x"][0],
        "ctx_t": a["ctx_1024"][0].T,
        "mask_in": a["mask_Bx1xSxS2_ik1"][0, 0],
        "mask_cols": a["mask_Bx1xSxS2_ik1"][0, 0].T.reshape(NC, CT, T, L)[::-1].transpose(2, 0, 1, 3).reshape(T, NT * L),
        "wq_in": np.stack([stacked(a["L0_xattn_w_q"].T), stacked(a["L1_xattn_Wq"])]),
        "b1_in": np.broadcast_to(a["L0_ffn_b1"].reshape(E0 // 2, 2, 1, H0), (E0 // 2, 2, L, H0))
                 .transpose(1, 2, 0, 3).reshape(128, E0 // 2 * H0),
        "mats_in": mats,
        "rows_in": rows,
        "cons_in": cons,
        "f0w12": np.concatenate([
            a["L0_ffn_w1"].transpose(2, 0, 1).reshape(D, E0 * H0),
            a["L0_ffn_w2"].reshape(E0, D, K0, 128).transpose(3, 0, 2, 1).reshape(128, E0 * K0 * D)], axis=1),
        "f1w13": np.concatenate([np.concatenate([a["L1_ffn_ew1"], a["L1_ffn_sw1"]]),
                                 np.concatenate([a["L1_ffn_ew3"], a["L1_ffn_sw3"]])], axis=2).transpose(1, 0, 2),
        "f1w2": np.concatenate([a["L1_ffn_ew2"], a["L1_ffn_sw2"]]).reshape(NE1, K1, 128, D)
                .transpose(2, 0, 1, 3).reshape(128, NE1 * K1, D),
    }
    arrays = {k: np.ascontiguousarray(v) for k, v in arrays.items()}
    nc = bacc.Bacc("TRN2", target_bir_lowering=False, num_devices=1)
    args = [nc.dram_tensor(k, v.shape, mybir.dt.from_np(v.dtype), kind="ExternalInput").ap() for k, v in arrays.items()]
    args.append(nc.dram_tensor("x_out", (L, D), F32, kind="ExternalOutput").ap())
    perceiver(nc, *args)
    r = run_bass_kernel_spmd(nc, [arrays], core_ids=[0])
    return r.results[0]["x_out"].reshape(1, L, D)
```
